# Optimizing a Trainium2 kernel written in Bass

```python
import numpy as np
import jax
import jax.numpy as jnp

def _softmax(x, axis=-1):
    return jax.nn.softmax(x, axis=axis)

def _gelu(x):
    return jax.nn.gelu(x, approximate=True)

def _silu(x):
    return jax.nn.silu(x)

def _sigmoid(x):
    return jax.nn.sigmoid(x)

def _layernorm(x, axis=-1, eps=1e-05):
    m = jnp.mean(x, axis=axis, keepdims=True)
    v = jnp.var(x, axis=axis, keepdims=True)
    return (x - m) / jnp.sqrt(v + eps)

def _scatter_add(tgt, idx, src, axis=0):
    return tgt.at[idx].add(src)

def _segment_sum(src, seg, n):
    return jax.ops.segment_sum(src, seg, n)
kernel_name = 'mk_perceiver_d1_seqx_r4_7ed362'

def setup_inputs(seed: int=0):
    np.random.seed(seed)
    _w = jnp.asarray

    def _rec_inputs():
        import jax
        import jax.numpy as jnp
        _rk = jax.random.key(seed)
        x = -0.0005207 + 1.001 * jax.random.normal(jax.random.fold_in(_rk, 1), (1, 256, 512), jnp.float32)
        _lenS = 256 - jax.random.randint(jax.random.fold_in(_rk, 7), (1,), 0, max(1, 256 // 4) + 1, jnp.int32)
        _lenS2 = 4096 - jax.random.randint(jax.random.fold_in(_rk, 8), (1,), 0, max(1, 4096 // 4) + 1, jnp.int32)
        _ctx_2048P = jax.random.normal(jax.random.fold_in(_rk, 12), (1, 16, 512), jnp.float32)
        _ctx_2048c = jax.random.dirichlet(jax.random.fold_in(_rk, 512), 0.3 * jnp.ones((16,), jnp.float32), (1, 4096))
        _ctx_2048t = jnp.einsum('bsk,bkd->bsd', _ctx_2048c, _ctx_2048P)
        _ctx_2048t = _ctx_2048t * jax.lax.rsqrt(jnp.mean(jnp.square(_ctx_2048t)) + 1e-12) * 0.953939
        ctx_2048 = -5.72187e-05 + 0.999849 * (_ctx_2048t + 0.3 * jax.random.normal(jax.random.fold_in(_rk, 612), (1, 4096, 512), jnp.float32))
        _validS = jnp.arange(256)[None, :] < _lenS[:, None]
        _validS2 = jnp.arange(4096)[None, :] < _lenS2[:, None]
        _causal = jnp.tril(jnp.ones((256, 256), dtype=bool))
        mask_BxSx4224_bf0 = jnp.logical_not(jnp.ones((1, 256, 1056), dtype=bool))
        return (x, ctx_2048, mask_BxSx4224_bf0)
    x, ctx_2048, mask_BxSx4224_bf0 = _rec_inputs()

    def _L0_xattn_setup():
        import jax, jax.numpy as jnp
        import numpy as np
        import math
        DIM = 512
        B, Q_LEN, KV_LEN = (8, 128, 1024)
        key = jax.random.key(seed)
        ks = jax.random.split(key, 8)
        x = jax.random.normal(ks[0], (B, Q_LEN, DIM), dtype=jnp.float32)
        mask = jnp.zeros((B, Q_LEN, KV_LEN + Q_LEN), dtype=bool)
        k_cache = jax.random.normal(ks[1], (B, KV_LEN, DIM), dtype=jnp.float32)
        v_cache = jax.random.normal(ks[2], (B, KV_LEN, DIM), dtype=jnp.float32)
        scale = 1.0 / math.sqrt(DIM)
        wq = jax.random.normal(ks[3], (DIM, DIM), dtype=jnp.float32) * scale
        wk = jax.random.normal(ks[4], (DIM, DIM), dtype=jnp.float32) * scale
        wv = jax.random.normal(ks[5], (DIM, DIM), dtype=jnp.float32) * scale
        wo = jax.random.normal(ks[6], (DIM, DIM), dtype=jnp.float32) * scale
        return {'x': x, 'mask': mask, 'k_cache': k_cache, 'v_cache': v_cache, 'wq': wq, 'wk': wk, 'wv': wv, 'wo': wo}
    _L0_xattn_all = _L0_xattn_setup()
    _L0_xattn_in = {k: v for k, v in _L0_xattn_all.items() if k in ('wq', 'wk', 'wv', 'wo')}
    del _L0_xattn_all

    def _L0_attn_setup():
        import jax, jax.numpy as jnp
        import numpy as np
        HID = 512
        H = 16
        Q_RANK = 192
        KV_RANK = 128
        NOPE = 128
        ROPE = 64
        VDIM = 128
        QK_DIM = NOPE + ROPE
        EPS = 1e-06
        THETA = 10000.0

        def rms_norm(x, g):
            var = jnp.mean(x * x, axis=-1, keepdims=True)
            return x * jax.lax.rsqrt(var + EPS) * g

        def rope_cos_sin(S, dtype):
            inv_freq = 1.0 / THETA ** (jnp.arange(0, ROPE, 2, dtype=jnp.float32) / ROPE)
            ang = jnp.arange(S, dtype=jnp.float32)[:, None] * inv_freq[None, :]
            emb = jnp.concatenate([ang, ang], axis=-1)
            return (jnp.cos(emb).astype(dtype), jnp.sin(emb).astype(dtype))

        def rotate_half(x):
            half = x.shape[-1] // 2
            return jnp.concatenate([-x[..., half:], x[..., :half]], axis=-1)

        def apply_rope(x, cos, sin):
            return x * cos[None, None] + rotate_half(x) * sin[None, None]
        key = jax.random.key(seed)
        ks = jax.random.split(key, 7)
        B, S = (2, 512)
        sc = lambda fan_in: 1.0 / np.sqrt(fan_in)
        return {'hidden_states': jax.random.normal(ks[0], (B, S, HID), jnp.float32), 'Wqa': jax.random.normal(ks[1], (HID, Q_RANK), jnp.float32) * sc(HID), 'g_qa': jnp.ones((Q_RANK,), jnp.float32), 'Wqb': jax.random.normal(ks[2], (Q_RANK, H * QK_DIM), jnp.float32) * sc(Q_RANK), 'Wkva': jax.random.normal(ks[3], (HID, KV_RANK + ROPE), jnp.float32) * sc(HID), 'g_kva': jnp.ones((KV_RANK,), jnp.float32), 'Wkvb': jax.random.normal(ks[4], (KV_RANK, H * (NOPE + VDIM)), jnp.float32) * sc(KV_RANK), 'Wo': jax.random.normal(ks[5], (H * VDIM, HID), jnp.float32) * sc(H * VDIM)}
    _L0_attn_all = _L0_attn_setup()
    _L0_attn_in = {k: v for k, v in _L0_attn_all.items() if k in ('Wqa', 'g_qa', 'Wqb', 'Wkva', 'g_kva', 'Wkvb', 'Wo')}
    del _L0_attn_all

    def _L0_ffn_setup():
        import jax, jax.numpy as jnp
        import numpy as np
        B, S, H = (2, 512, 512)
        E, G, TKG, K = (32, 8, 4, 8)
        I, SI = (256, 512)
        ROUTED_SCALE = 2.5

        def _moe_forward(hidden_states, router_w, router_bias, w_gate, w_up, w_down, sw_gate, sw_up, sw_down):
            x = hidden_states.reshape(-1, H)
            T = x.shape[0]
            logits = x.astype(jnp.float32) @ router_w.astype(jnp.float32)
            scores = jax.nn.sigmoid(logits)
            scores_grouped = (scores + router_bias).reshape(T, G, E // G)
            top2, _ = jax.lax.top_k(scores_grouped, 2)
            group_scores = top2.sum(-1)
            _, top_groups = jax.lax.top_k(group_scores, TKG)
            mask = jnp.ones((T, G), bool).at[jnp.arange(T)[:, None], top_groups].set(False)
            masked = jnp.where(mask[:, :, None], 0.0, scores_grouped).reshape(T, E)
            _, top_k_index = jax.lax.top_k(masked, K)
            tkw = jnp.take_along_axis(scores, top_k_index, axis=-1)
            tkw = tkw / tkw.sum(-1, keepdims=True)
            tkw = (tkw * ROUTED_SCALE).astype(hidden_states.dtype)
            flat_idx = top_k_index.reshape(-1)
            sort_idx = jnp.argsort(flat_idx)
            xs = jnp.repeat(x, K, axis=0)[sort_idx]
            group_sizes = jnp.bincount(flat_idx, length=E).astype(jnp.int32)
            gate = jax.lax.ragged_dot(xs, w_gate, group_sizes)
            up = jax.lax.ragged_dot(xs, w_up, group_sizes)
            down = jax.lax.ragged_dot(jax.nn.silu(gate) * up, w_down, group_sizes)
            unsort = jnp.argsort(sort_idx)
            routed = (down[unsort].reshape(T, K, H) * tkw[..., None]).sum(axis=1)
            shared = jax.nn.silu(x @ sw_gate) * (x @ sw_up) @ sw_down
            return (routed + shared).reshape(hidden_states.shape)
        key = jax.random.key(seed)
        ks = jax.random.split(key, 9)

        def w(k, shape, fan_in):
            return jax.random.normal(k, shape, jnp.float32) / np.float32(np.sqrt(fan_in))
        return dict(hidden_states=jax.random.normal(ks[0], (B, S, H), jnp.float32), router_w=w(ks[1], (H, E), H), router_bias=jnp.zeros((E,), jnp.float32), w_gate=w(ks[2], (E, H, I), H), w_up=w(ks[3], (E, H, I), H), w_down=w(ks[4], (E, I, H), I), sw_gate=w(ks[5], (H, SI), H), sw_up=w(ks[6], (H, SI), H), sw_down=w(ks[7], (SI, H), SI))
    _L0_ffn_all = _L0_ffn_setup()
    _L0_ffn_in = {k: v for k, v in _L0_ffn_all.items() if k in ('router_w', 'router_bias', 'w_gate', 'w_up', 'w_down', 'sw_gate', 'sw_up', 'sw_down')}
    del _L0_ffn_all
    return {'x': x, 'ctx_2048': ctx_2048, 'mask_BxSx4224_bf0': mask_BxSx4224_bf0, 'L0_xattn_wq': _L0_xattn_in['wq'], 'L0_xattn_wk': _L0_xattn_in['wk'], 'L0_xattn_wv': _L0_xattn_in['wv'], 'L0_xattn_wo': _L0_xattn_in['wo'], 'L0_attn_Wqa': _L0_attn_in['Wqa'], 'L0_attn_g_qa': _L0_attn_in['g_qa'], 'L0_attn_Wqb': _L0_attn_in['Wqb'], 'L0_attn_Wkva': _L0_attn_in['Wkva'], 'L0_attn_g_kva': _L0_attn_in['g_kva'], 'L0_attn_Wkvb': _L0_attn_in['Wkvb'], 'L0_attn_Wo': _L0_attn_in['Wo'], 'L0_ffn_router_w': _L0_ffn_in['router_w'], 'L0_ffn_router_bias': _L0_ffn_in['router_bias'], 'L0_ffn_w_gate': _L0_ffn_in['w_gate'], 'L0_ffn_w_up': _L0_ffn_in['w_up'], 'L0_ffn_w_down': _L0_ffn_in['w_down'], 'L0_ffn_sw_gate': _L0_ffn_in['sw_gate'], 'L0_ffn_sw_up': _L0_ffn_in['sw_up'], 'L0_ffn_sw_down': _L0_ffn_in['sw_down']}

def reference(x, ctx_2048, mask_BxSx4224_bf0, L0_xattn_wq, L0_xattn_wk, L0_xattn_wv, L0_xattn_wo, L0_attn_Wqa, L0_attn_g_qa, L0_attn_Wqb, L0_attn_Wkva, L0_attn_g_kva, L0_attn_Wkvb, L0_attn_Wo, L0_ffn_router_w, L0_ffn_router_bias, L0_ffn_w_gate, L0_ffn_w_up, L0_ffn_w_down, L0_ffn_sw_gate, L0_ffn_sw_up, L0_ffn_sw_down):
    import jax
    import jax.numpy as jnp

    def _L0_xattn_ref(x, mask, k_cache, v_cache, wq, wk, wv, wo):
        import jax, jax.numpy as jnp
        import numpy as np
        import math
        DIM = 512
        B, Q_LEN, KV_LEN = (8, 128, 1024)
        q = jnp.einsum('bsd,ed->bse', x, wq)
        k_new = jnp.einsum('bsd,ed->bse', x, wk)
        v_new = jnp.einsum('bsd,ed->bse', x, wv)
        k = jnp.concatenate([k_cache, k_new], axis=1)
        v = jnp.concatenate([v_cache, v_new], axis=1)
        scale = 1.0 / math.sqrt(q.shape[-1])
        scores = jnp.einsum('bqd,bkd->bqk', q, k) * scale
        attn = jax.nn.softmax(scores, axis=-1)
        out = jnp.einsum('bqk,bkd->bqd', attn, v)
        return jnp.einsum('bqd,ed->bqe', out, wo)

    def _L0_attn_ref(hidden_states, Wqa, g_qa, Wqb, Wkva, g_kva, Wkvb, Wo):
        import jax, jax.numpy as jnp
        import numpy as np
        HID = 512
        H = 16
        Q_RANK = 192
        KV_RANK = 128
        NOPE = 128
        ROPE = 64
        VDIM = 128
        QK_DIM = NOPE + ROPE
        EPS = 1e-06
        THETA = 10000.0

        def rms_norm(x, g):
            var = jnp.mean(x * x, axis=-1, keepdims=True)
            return x * jax.lax.rsqrt(var + EPS) * g

        def rope_cos_sin(S, dtype):
            inv_freq = 1.0 / THETA ** (jnp.arange(0, ROPE, 2, dtype=jnp.float32) / ROPE)
            ang = jnp.arange(S, dtype=jnp.float32)[:, None] * inv_freq[None, :]
            emb = jnp.concatenate([ang, ang], axis=-1)
            return (jnp.cos(emb).astype(dtype), jnp.sin(emb).astype(dtype))

        def rotate_half(x):
            half = x.shape[-1] // 2
            return jnp.concatenate([-x[..., half:], x[..., :half]], axis=-1)

        def apply_rope(x, cos, sin):
            return x * cos[None, None] + rotate_half(x) * sin[None, None]
        B, S, _ = hidden_states.shape
        dtype = hidden_states.dtype
        q_c = rms_norm(hidden_states @ Wqa, g_qa)
        q = (q_c @ Wqb).reshape(B, S, H, QK_DIM).transpose(0, 2, 1, 3)
        q_nope, q_rope = (q[..., :NOPE], q[..., NOPE:])
        kv = hidden_states @ Wkva
        kv_c, k_rope_raw = (kv[..., :KV_RANK], kv[..., KV_RANK:])
        kv_exp = rms_norm(kv_c, g_kva) @ Wkvb
        kv_exp = kv_exp.reshape(B, S, H, NOPE + VDIM).transpose(0, 2, 1, 3)
        k_nope, v = (kv_exp[..., :NOPE], kv_exp[..., NOPE:])
        cos, sin = rope_cos_sin(S, dtype)
        q_rope = apply_rope(q_rope, cos, sin)
        k_rope = apply_rope(k_rope_raw[:, None], cos, sin)
        k_rope = jnp.broadcast_to(k_rope, (B, H, S, ROPE))
        q_full = jnp.concatenate([q_nope, q_rope], axis=-1)
        k_full = jnp.concatenate([k_nope, k_rope], axis=-1)
        scale = QK_DIM ** (-0.5)
        scores = jnp.einsum('bhsd,bhtd->bhst', q_full, k_full) * scale
        causal = jnp.triu(jnp.ones((S, S), dtype=bool), k=1)
        scores = jnp.where(causal[None, None], -jnp.inf, scores)
        probs = jax.nn.softmax(scores.astype(jnp.float32), axis=-1).astype(dtype)
        out = jnp.einsum('bhst,bhtv->bhsv', probs, v)
        out = out.transpose(0, 2, 1, 3).reshape(B, S, H * VDIM)
        return out @ Wo

    def _L0_ffn_ref(hidden_states, router_w, router_bias, w_gate, w_up, w_down, sw_gate, sw_up, sw_down):
        import jax, jax.numpy as jnp
        import numpy as np
        B, S, H = (2, 512, 512)
        E, G, TKG, K = (32, 8, 4, 8)
        I, SI = (256, 512)
        ROUTED_SCALE = 2.5

        def _moe_forward(hidden_states, router_w, router_bias, w_gate, w_up, w_down, sw_gate, sw_up, sw_down):
            x = hidden_states.reshape(-1, H)
            T = x.shape[0]
            logits = x.astype(jnp.float32) @ router_w.astype(jnp.float32)
            scores = jax.nn.sigmoid(logits)
            scores_grouped = (scores + router_bias).reshape(T, G, E // G)
            top2, _ = jax.lax.top_k(scores_grouped, 2)
            group_scores = top2.sum(-1)
            _, top_groups = jax.lax.top_k(group_scores, TKG)
            mask = jnp.ones((T, G), bool).at[jnp.arange(T)[:, None], top_groups].set(False)
            masked = jnp.where(mask[:, :, None], 0.0, scores_grouped).reshape(T, E)
            _, top_k_index = jax.lax.top_k(masked, K)
            tkw = jnp.take_along_axis(scores, top_k_index, axis=-1)
            tkw = tkw / tkw.sum(-1, keepdims=True)
            tkw = (tkw * ROUTED_SCALE).astype(hidden_states.dtype)
            flat_idx = top_k_index.reshape(-1)
            sort_idx = jnp.argsort(flat_idx)
            xs = jnp.repeat(x, K, axis=0)[sort_idx]
            group_sizes = jnp.bincount(flat_idx, length=E).astype(jnp.int32)
            gate = jax.lax.ragged_dot(xs, w_gate, group_sizes)
            up = jax.lax.ragged_dot(xs, w_up, group_sizes)
            down = jax.lax.ragged_dot(jax.nn.silu(gate) * up, w_down, group_sizes)
            unsort = jnp.argsort(sort_idx)
            routed = (down[unsort].reshape(T, K, H) * tkw[..., None]).sum(axis=1)
            shared = jax.nn.silu(x @ sw_gate) * (x @ sw_up) @ sw_down
            return (routed + shared).reshape(hidden_states.shape)
        return _moe_forward(hidden_states, router_w, router_bias, w_gate, w_up, w_down, sw_gate, sw_up, sw_down)
    x = x + _L0_xattn_ref(_layernorm(x, axis=-1), mask_BxSx4224_bf0, ctx_2048, ctx_2048, L0_xattn_wq, L0_xattn_wk, L0_xattn_wv, L0_xattn_wo)
    x = x + _L0_attn_ref(_layernorm(x, axis=-1), L0_attn_Wqa, L0_attn_g_qa, L0_attn_Wqb, L0_attn_Wkva, L0_attn_g_kva, L0_attn_Wkvb, L0_attn_Wo)
    x = x + _L0_ffn_ref(_layernorm(x, axis=-1), L0_ffn_router_w, L0_ffn_router_bias, L0_ffn_w_gate, L0_ffn_w_up, L0_ffn_w_down, L0_ffn_sw_gate, L0_ffn_sw_up, L0_ffn_sw_down)
    return x

_drawn_inputs = setup_inputs


def setup_inputs(seed=0):
    import zlib

    import numpy as np

    out = dict(_drawn_inputs(seed))
    spreads = {'L0_attn_g_qa': (1.0, 0.2), 'L0_attn_g_kva': (1.0, 0.2), 'L0_ffn_router_bias': (0.0, 0.1)}
    factors = {}
    for name, (base, spread) in spreads.items():
        noise = np.random.default_rng([zlib.crc32(name.encode()), seed]).standard_normal(out[name].shape)
        drawn = base * np.exp(spread * noise) if base else spread * noise
        out[name] = jnp.asarray(drawn.astype(out[name].dtype))
    for name, factor in factors.items():
        out[name] = (out[name] * factor).astype(out[name].dtype)
    return out
```

```python
from contextlib import ExitStack

import numpy as np

import concourse.bass as bass
from concourse import mybir

F32 = mybir.dt.float32
F32R = mybir.dt.float32r
ALU = mybir.AluOpType
ACT = mybir.ActivationFunctionType
AX = mybir.AxisListType.X

P = 128
T = 256
D = 512
NC = D // P
CTX = 4096
NG = CTX // 512
KEYS = CTX + T
HEADS, NOPE, ROPE, VDIM = 16, 128, 64, 128
Q_RANK, KV_RANK = 192, 128
QR2 = Q_RANK // 2
PAIRS = HEADS // 2
E, GROUPS, TOP_GROUPS, TOP, I = 32, 8, 4, 8, 256
PER = E // GROUPS
SHARED = 2
NE = E + SHARED
ROUTED_SCALE = 2.5
LN_EPS, RMS_EPS = 1e-5, 1e-6
XSCALE = 1.0 / float(np.sqrt(D))
MSCALE = float(NOPE + ROPE) ** -0.5
MASKED = -1e30
TAKEN = -3e38

T_WQ, T_WK, T_CT, T_WV, T_CN, T_WO, T_QKV, T_M = 0, 1, 2, 10, 11, 19, 20, 21
T_E = T_M + PAIRS

OFF = (0, 1280, 2304)
SLOT = 3072
X_SIZES = (1024, 1024)
Q_SIZES = (768, 768)
M_SIZES = (1280, 1024)
E_SIZES = (1280, 1024, 768)

C_ID, C_MASK, C_COS, C_SIN, C_RW, C_BIAS, C_GQ, C_GKV, C_TIE = 0, 128, 256, 512, 768, 896, 960, 962, 963
C_END = C_TIE + 2 * GROUPS * GROUPS

F01 = dict(ln1=1, s_even=2, s_new=6, pt_even=7, ot=11, ln2=12, y=13, ln3=14, moe=15)
F23 = dict(q=1, s_odd=2, pt_new=6, pt_odd=7, qkv=11, scores=12, pt=13, moe=28)
F45 = dict(k=1, v=2, wo=3, c=4)
F4 = dict(q=5, router=13, moe=14)
F5 = dict(k0=5, k=4, o=7, o_last=20, moe=21)
F67 = dict(pv=1)
F6 = dict(v=2, moe=10)
F7 = dict(rope=2, rope_t=3, moe=18)

V_LN1, V_Q, V_K, V_V, V_PT, V_OT, V_LN2, V_QC, V_KV, V_KR, V_M0 = 1, 3, 5, 7, 9, 27, 29, 31, 33, 34, 36
V_MLA = V_M0 + 4
PER_PAIR = 7
V_LN3 = V_MLA + (PAIRS - 1) * PER_PAIR + 3
V_H = V_LN3 + 2


class Tile:

    def __init__(self, j, s):
        self.slot = s % 2
        self.loaded = (j + (s // 2 + 1)) * 16
        self.number = j * 2 + s

    def split(self, k):
        return self.number + 1 if k < 2 else self.number + (1 - T_E)

    def free(self, k):
        return self.number - 1 if k < 2 else self.number + (-1 - T_E)


def perceiver_layer(nc, x, small, wq, wk, wv, wo, ctx_t, ctx_n, w_qkv, w_mla, w_exp, out):
    with ExitStack() as ctx:
        def sb(name, shape, dt=F32):
            return ctx.enter_context(nc.sbuf_tensor(name, shape, dt))

        def sem(name):
            return ctx.enter_context(nc.semaphore(name))

        bank = [ctx.enter_context(nc.psum_tensor(f"bank{b}", [P, 512], F32)) for b in range(8)]

        raw = sb("raw", [P, 2, SLOT])
        w_hi = sb("w_hi", [P, 2, SLOT], F32R)
        w_lo = sb("w_lo", [P, 2, SLOT], F32R)
        smalls = sb("smalls", [P, C_END])
        res = sb("res", [P, 2, D])
        xn = sb("xn", [P, 2, D])
        xt_hi = sb("xt_hi", [P, NC, T], F32R)
        xt_lo = sb("xt_lo", [P, NC, T], F32R)
        probs = sb("probs", [P, 2, 2, 512])
        o_row = sb("o_row", [P, 2, D])
        ident_r = sb("ident_r", [P, P], F32R)
        mask_r = sb("mask_r", [P, P], F32R)
        rw_hi = sb("rw_hi", [P, NC, E], F32R)
        rw_lo = sb("rw_lo", [P, NC, E], F32R)
        stat = sb("stat", [P, 2, 6])
        mean_var = sb("mean_var", [P, 2, 2])
        var_eps = sb("var_eps", [P, 4])
        power = sb("power", [P, 4])
        rstd = sb("rstd", [P, 4])
        row_max = sb("row_max", [P, 2, NG + 1])
        neg_max = sb("neg_max", [P, 2])
        exp_bias = sb("exp_bias", [P, 2])
        sums = sb("sums", [P, 2, NG + 1])
        row_sum = sb("row_sum", [P, 2])
        row_inv = sb("row_inv", [P, 2])
        m_neg = sb("m_neg", [P, 4])
        m_bias = sb("m_bias", [P, 4])
        m_sum = sb("m_sum", [P, 4])
        m_inv = sb("m_inv", [P, 4])
        weights = sb("weights", [P, 2, NE])

        operands = sb("operands", [P, 11776], F32R)

        def op(at, *shape):
            v = operands[:, at:at + int(np.prod(shape))]
            names = "abc"[:len(shape)]
            if len(shape) == 1:
                return v
            return v.rearrange(f"p ({' '.join(names)}) -> p {' '.join(names)}",
                               **dict(zip(names[1:], shape[1:])))

        q_hi, q_lo = op(0, NC, T), op(1024, NC, T)
        k_hi, k_lo = op(2048, NC, T), op(3072, NC, T)
        v_hi, v_lo = op(4096, 2, D), op(5120, 2, D)
        pt_hi, pt_lo = op(6144, 2, 2, 512), op(8192, 2, 2, 512)
        ot_hi, ot_lo = op(0, NC, T), op(1024, NC, T)
        qc_hi, qc_lo = op(2048, 2, T), op(2560, 2, T)
        kvc_hi, kvc_lo = op(3072, T), op(3328, T)
        kr_hi, kr_lo = op(3584, 2, T), op(4096, 2, T)
        mq_hi, mq_lo = op(4608, 2, T), op(5120, 2, T)
        mk_hi, mk_lo = op(5632, 2, T), op(6144, 2, T)
        qr_hi, qr_lo = op(6656, T), op(6912, T)
        mv_hi, mv_lo = op(7168, 2, 2, T), op(8192, 2, 2, T)
        mpt_hi, mpt_lo = op(9216, 2, 384), op(9984, 2, 384)
        mo_hi, mo_lo = op(10752, 2, T), op(11264, 2, T)
        h_hi, h_lo = op(0, 2, 512), op(1024, 2, 512)

        scores = sb("scores", [P, 2, KEYS])

        def row(at, n):
            return scores[:, 0, at:at + n]

        qkv_row = row(0, 768).rearrange("p (h n) -> p h n", h=2)
        squares = row(768, 192)
        qc_row = row(1024, 384).rearrange("p (h n) -> p h n", h=2)
        kvc_row = row(1408, 256).rearrange("p (h n) -> p h n", h=2)
        kr_cos, kr_sin = row(1664, 128), row(1792, 128)
        kr_row = row(1920, 256).rearrange("p (h n) -> p h n", h=2)
        pair_probs = row(2176, 768).rearrange("p (h n) -> p h n", h=2)
        q_cos, q_sin, q_rope = row(2944, 256), row(3200, 256), row(3456, 256)
        gate_act = scores[:, 1, 0:1024].rearrange("p (r n) -> p r n", r=2)
        h_row = scores[:, 1, 1024:2048].rearrange("p (r n) -> p r n", r=2)

        def route(at, n):
            return scores[:, 1, 2048 + at:2048 + at + n]

        x_loaded = sem("x_loaded")
        small_loaded = sem("small_loaded")
        loaded_a = [sem(f"loaded_a{s}") for s in range(2)]
        loaded_b = [sem(f"loaded_b{s}") for s in range(2)]
        hi_split = [sem(f"hi_split{k}") for k in range(3)]
        lo_split = [sem(f"lo_split{k}") for k in range(3)]
        used = [sem(f"used{k}") for k in range(3)]
        bank_full = [sem(f"bank_full{b}") for b in range(8)]
        ev_hi = sem("ev_hi")
        ev_lo = sem("ev_lo")
        consts_rounded = sem("consts_rounded")
        vec = sem("vec")
        power_set = sem("power_set")
        var_ready = sem("var_ready")
        eps_added = sem("eps_added")
        rstd_ready = sem("rstd_ready")
        xn_ready = sem("xn_ready")
        s_copied = sem("s_copied")
        s_max = sem("s_max")
        bias_ready = sem("bias_ready")
        p_ready = sem("p_ready")
        o_ready = sem("o_ready")
        res_done = sem("res_done")
        qkv_copied = sem("qkv_copied")
        rows_ready = sem("rows_ready")
        kr_zeroed = sem("kr_zeroed")
        m_neg_ready = sem("m_neg_ready")
        m_bias_ready = sem("m_bias_ready")
        m_exp = sem("m_exp")
        m_inv_ready = sem("m_inv_ready")
        m_norm = sem("m_norm")
        rope_part = sem("rope_part")
        rope_ready = sem("rope_ready")
        sigmoid_ready = sem("sigmoid_ready")
        silu_ready = sem("silu_ready")
        h_ready = sem("h_ready")
        stored = sem("stored")

        def split_hi(act, t, k, sizes, first=False):
            act.wait_ge((loaded_b if k else loaded_a)[t.slot], t.loaded)
            if not first:
                act.wait_ge(used[k], t.free(k))
            at, n = OFF[k], sizes[k]
            act.copy(w_hi[:, t.slot, at:at + n], raw[:, t.slot, at:at + n]).then_inc(hi_split[k], 1)

        def split_lo(eng, t, k, sizes, handed_over=False):
            eng.wait_ge(hi_split[k], t.split(k))
            if handed_over:
                eng.wait_ge(lo_split[k], t.split(k) - 1)
            at, n = OFF[k], sizes[k]
            eng.tensor_tensor(w_lo[:, t.slot, at:at + n], raw[:, t.slot, at:at + n],
                              w_hi[:, t.slot, at:at + n].bitcast(F32), ALU.subtract) \
               .then_inc(lo_split[k], 1)

        def out_hi(act, b, full, hi, n, rows=slice(0, P), at=0, scale=1.0):
            act.wait_ge(bank_full[b], full)
            act.activation(hi, bank[b][rows, at:at + n], ACT.Copy, scale=scale).then_inc(ev_hi, 1)

        def out_lo(dve, b, number, hi, lo, n, rows=slice(0, P), at=0):
            dve.wait_ge(ev_hi, number)
            dve.tensor_tensor(lo, bank[b][rows, at:at + n], hi.bitcast(F32), ALU.subtract) \
               .then_inc(ev_lo, 1)

        def flat(v):
            return v.rearrange("p a b -> p (a b)")

        block = ctx.enter_context(nc.Block())

        @block.sync
        def _(sp):
            def load(t, src, sizes, first=False):
                for part, k, at, n in ((loaded_a, 0, 0, sizes[0]), (loaded_b, 1, sizes[0], sum(sizes[1:]))):
                    if not first:
                        sp.wait_ge(lo_split[k], t.free(k))
                    sp.dma_start(raw[:, t.slot, OFF[k]:OFF[k] + n], src[:, at:at + n]).then_inc(part[t.slot], 16)

            sp.dma_start(res[:, :, :], x).then_inc(x_loaded, 16)
            sp.dma_start(smalls[:, :], small).then_inc(small_loaded, 16)
            load(Tile(0, T_WQ), wq, X_SIZES, first=True)
            load(Tile(0, T_WK), wk, X_SIZES, first=True)
            with sp.Fori(0, NG // 2) as j:
                for s in range(2):
                    load(Tile(j, T_CT + s), ctx_t[bass.ds(j * 2 + s, 1)].squeeze(0), X_SIZES)
            load(Tile(0, T_WV), wv, X_SIZES)
            with sp.Fori(0, NG // 2) as j:
                for s in range(2):
                    load(Tile(j, T_CN + s), ctx_n[bass.ds(j * 2 + s, 1)].squeeze(0), X_SIZES)
            load(Tile(0, T_WO), wo, X_SIZES)
            load(Tile(0, T_QKV), w_qkv, Q_SIZES)
            with sp.Fori(0, PAIRS // 2) as j:
                for s in range(2):
                    load(Tile(j, T_M + s), w_mla[bass.ds(j * 2 + s, 1)].squeeze(0), M_SIZES)
            for s in range(2):
                load(Tile(0, T_E + s), w_exp[s], E_SIZES)
            with sp.Fori(0, NE // 2 - 1) as j:
                for s in range(2, 4):
                    load(Tile(j, T_E + s), w_exp[bass.ds(j * 2 + s, 1)].squeeze(0), E_SIZES)
            sp.wait_ge(res_done, 4 + 2 * NE)
            sp.dma_start(out, res[:, :, :]).then_inc(stored, 16)
            sp.wait_ge(stored, 16)

        @block.tensor
        def _(pe):
            ident = smalls[:, C_ID:C_ID + P]

            def product(o, a, b, start, stop, told=None):
                ins = pe.matmul(o, a[0], b[0], start=start, stop=False)
                if told is not None:
                    ins.then_inc(told, 1)
                pe.matmul(o, a[0], b[1], start=False, stop=False)
                return pe.matmul(o, a[1], b[0], start=False, stop=stop)

            def ready(t, k):
                pe.wait_ge(lo_split[k], t.split(k))

            def wcols(t, at, n, rows=P):
                return w_hi[0:rows, t.slot, at:at + n], w_lo[0:rows, t.slot, at:at + n]

            def x_chunk(t, c, at=0, n=512):
                return wcols(t, OFF[c // 2] + (c % 2) * 512 + at, n)

            def half(h):
                return slice(h * P, h * P + P)

            def transpose_rows(src, told=None):
                for b in range(2):
                    for c in range(2):
                        for h in range(2):
                            ins = pe.transpose(bank[b][:, c * T + h * P:c * T + h * P + P],
                                               src[:, h, (2 * b + c) * P:(2 * b + c + 1) * P], ident)
                            if told is not None and b == c == h == 0:
                                ins.then_inc(told, 1)
                    ins.then_inc(bank_full[b], 1)

            def project_t(t, first_bank, told=None):
                for m in range(NC):
                    b = first_bank + m // 2
                    for c in range(NC):
                        if m == 0 and c % 2 == 0:
                            ready(t, c // 2)
                        ins = product(bank[b][:, (m % 2) * T:(m % 2) * T + T], x_chunk(t, c, m * P, P),
                                      (xt_hi[:, c, :], xt_lo[:, c, :]), c == 0, c == NC - 1,
                                      told if m == c == 0 else None)
                        if m == NC - 1 and c == 1:
                            ins.then_inc(used[0], 1)
                    if m % 2:
                        ins.then_inc(bank_full[b], 1)

            def project_rows(t, a_hi, a_lo, first_bank, width=512, told=None):
                for h in range(2):
                    for c in range(NC):
                        if h == 0 and c % 2 == 0:
                            ready(t, c // 2)
                        w = wcols(t, OFF[c // 2] + (c % 2) * width, width)
                        ins = product(bank[first_bank + h][:, 0:width],
                                      (a_hi[:, c, half(h)], a_lo[:, c, half(h)]), w, c == 0, c == NC - 1,
                                      told if h == c == 0 else None)
                        if h == 1 and c == 1:
                            ins.then_inc(used[0], 1)
                    ins.then_inc(bank_full[first_bank + h], 1)

            pe.wait_ge(small_loaded, 16)
            pe.wait_ge(xn_ready, 2)
            transpose_rows(xn)
            pe.wait_ge(ev_lo, V_LN1 + 1)
            project_t(Tile(0, T_WQ), 2)
            project_t(Tile(0, T_WK), 4, told=used[1])
            pe.wait_ge(ev_lo, V_Q + 1)

            def score_group(j, s):
                t = Tile(j, T_CT + s)
                for h in range(2):
                    b = 2 * (s % 2) + h
                    if not isinstance(j, int):
                        pe.wait_ge(s_copied, j * 4 + (2 * s + h - 3))
                    for c in range(NC):
                        if h == 0 and c % 2 == 0:
                            ready(t, c // 2)
                        ins = product(bank[b][:, :], (q_hi[:, c, half(h)], q_lo[:, c, half(h)]),
                                      x_chunk(t, c), c == 0, c == NC - 1,
                                      used[1] if h == c == 0 else None)
                        if h == 1 and c == 1:
                            ins.then_inc(used[0], 1)
                    ins.then_inc(bank_full[b], 1)

            score_group(0, 0)
            score_group(0, 1)
            with pe.Fori(1, NG // 2) as j:
                score_group(j, 0)
                score_group(j, 1)
            for h in range(2):
                pe.wait_ge(s_copied, 2 * (NG - 2) + h + 1)
                for c in range(NC):
                    ins = product(bank[h][:, 0:T], (q_hi[:, c, half(h)], q_lo[:, c, half(h)]),
                                  (k_hi[:, c, :], k_lo[:, c, :]), c == 0, c == NC - 1,
                                  used[1] if h == c == 0 else None)
                ins.then_inc(bank_full[h], 1)
            project_rows(Tile(0, T_WV), xt_hi, xt_lo, 4)

            def transpose_probs(ring, exps, blocks=4, told=None):
                for h in range(2):
                    pe.wait_ge(p_ready, exps + (h + 1))
                    for k in range(blocks):
                        ins = pe.transpose(bank[2 * ring + h][:, k * P:k * P + P],
                                           probs[:, ring, h, k * P:k * P + P], ident)
                        if told is not None and h == k == 0:
                            ins.then_inc(told, 1)
                    ins.then_inc(bank_full[2 * ring + h], 1)

            def times_values(ring, t, number, last=False):
                for h in range(2):
                    pe.wait_ge(ev_lo, number + h)
                    for k in range(4):
                        if h == 0 and k % 2 == 0:
                            ready(t, k // 2)
                        ins = product(bank[6 + h][:, :], (pt_hi[:, ring, h, k * P:k * P + P],
                                                          pt_lo[:, ring, h, k * P:k * P + P]),
                                      x_chunk(t, k), False, last and k == 3)
                        if h == 1 and k == 1:
                            ins.then_inc(used[0], 1)
                    if last:
                        ins.then_inc(bank_full[6 + h], 1)
                if not last:
                    ins.then_inc(used[1], 1)

            transpose_probs(1, 0, blocks=2, told=used[1])
            transpose_probs(0, 2)
            for h in range(2):
                pe.wait_ge(ev_lo, V_PT + h)
                for k in range(2):
                    product(bank[6 + h][:, :], (pt_hi[:, 1, h, k * P:k * P + P], pt_lo[:, 1, h, k * P:k * P + P]),
                            (v_hi[:, k, :], v_lo[:, k, :]), k == 0, False)
            with pe.Fori(0, NG // 2 - 1) as j:
                transpose_probs(1, j * 4 + 4)
                times_values(0, Tile(j, T_CN), j * 4 + (V_PT + 2))
                transpose_probs(0, j * 4 + 6)
                times_values(1, Tile(j, T_CN + 1), j * 4 + (V_PT + 4))
            transpose_probs(1, 2 * NG)
            times_values(0, Tile(0, T_CN + 6), V_PT + 14)
            times_values(1, Tile(0, T_CN + 7), V_PT + 16, last=True)

            pe.wait_ge(o_ready, 2)
            transpose_rows(o_row, told=used[1])
            pe.wait_ge(ev_lo, V_OT + 1)
            project_rows(Tile(0, T_WO), ot_hi, ot_lo, 4)

            pe.wait_ge(xn_ready, 4)
            transpose_rows(xn, told=used[1])
            pe.wait_ge(ev_lo, V_LN2 + 1)
            project_rows(Tile(0, T_QKV), xt_hi, xt_lo, 2, width=384)
            pe.wait_ge(rows_ready, 1)
            for c in range(2):
                for h in range(2):
                    ins = pe.transpose(bank[4][0:QR2, c * T + h * P:c * T + h * P + P],
                                       qc_row[:, h, c * QR2:c * QR2 + QR2], ident)
                    if c == h == 0:
                        ins.then_inc(used[1], 1)
            ins.then_inc(bank_full[4], 1)
            for h in range(2):
                pe.transpose(bank[5][:, half(h)], kvc_row[:, h, :], ident)
            for h in range(2):
                ins = pe.transpose(bank[5][:, T + h * P:T + h * P + P], kr_row[:, h, :], ident)
            ins.then_inc(bank_full[5], 1)
            pe.wait_ge(ev_lo, V_KR + 1)
            pe.wait_ge(consts_rounded, 3)

            def project_pair(t, out_split=None):
                ready(t, 0)
                for h in range(2):
                    for c in range(2):
                        ins = product(bank[7][:, half(h)], (qc_hi[0:QR2, c, half(h)], qc_lo[0:QR2, c, half(h)]),
                                      wcols(t, c * 384 + 256, P, QR2), c == 0, c == 1)
                ins.then_inc(bank_full[7], 1)
                for hd in range(2):
                    for c in range(2):
                        ins = product(bank[4][:, hd * T:hd * T + T], wcols(t, c * 384 + hd * P, P, QR2),
                                      (qc_hi[0:QR2, c, :], qc_lo[0:QR2, c, :]), c == 0, c == 1)
                ins.then_inc(bank_full[4], 1)
                if out_split is not None:
                    pe.wait_ge(ev_lo, out_split)
                for hd in range(2):
                    ins = product(bank[5][:, hd * T:hd * T + T], wcols(t, 768 + hd * P, P),
                                  (kvc_hi, kvc_lo), True, True)
                ins.then_inc(bank_full[5], 1)
                for h in range(2):
                    ins = product(bank[6][:, h * T:h * T + T], (kvc_hi[:, half(h)], kvc_lo[:, half(h)]),
                                  wcols(t, 1024, T), True, True)
                ins.then_inc(bank_full[6], 1)

            def rope_transpose(rope, told=None):
                pe.wait_ge(rope_ready, rope)
                for h in range(2):
                    ins = pe.transpose(bank[7][:, T + h * P:T + h * P + P], q_rope[:, half(h)], ident)
                    if told is not None and h == 0:
                        ins.then_inc(told, 1)
                ins.then_inc(bank_full[7], 1)

            def score_pair():
                for hd in range(2):
                    for h, at, n in ((1, 0, T), (0, T, P)):
                        o = bank[2 + hd][:, at:at + n]
                        product(o, (mq_hi[:, hd, half(h)], mq_lo[:, hd, half(h)]),
                                (mk_hi[:, hd, 0:n], mk_lo[:, hd, 0:n]), True, False)
                        product(o, (qr_hi[:, half(h)], qr_lo[:, half(h)]),
                                (kr_hi[:, hd, 0:n], kr_lo[:, hd, 0:n]), False, False)
                        ins = pe.matmul(bank[2 + hd][:, at + n - P:at + n], ident_r[:, :], mask_r[:, :],
                                        start=False, stop=True)
                    ins.then_inc(bank_full[2 + hd], 1)

            def transpose_pair(normed, told=None):
                for hd in range(2):
                    pe.wait_ge(m_norm, normed + 2 * (hd + 1))
                    for dst, src in ((0, T), (P, 0), (T, P)):
                        ins = pe.transpose(bank[2 + hd][:, dst:dst + P], pair_probs[:, hd, src:src + P], ident)
                        if told is not None and hd == dst == 0:
                            ins.then_inc(told, 1)
                    ins.then_inc(bank_full[2 + hd], 1)

            def values_pair(ring):
                for hd in range(2):
                    a = slice(hd * VDIM, hd * VDIM + VDIM)
                    product(bank[5][:, hd * T:hd * T + T], (mv_hi[:, ring, 0, a], mv_lo[:, ring, 0, a]),
                            (mpt_hi[:, hd, 0:T], mpt_lo[:, hd, 0:T]), True, False)
                    ins = product(bank[5][:, hd * T + P:hd * T + T], (mv_hi[:, ring, 1, a], mv_lo[:, ring, 1, a]),
                                  (mpt_hi[:, hd, T:T + P], mpt_lo[:, hd, T:T + P]), False, True)
                ins.then_inc(bank_full[5], 1)

            def out_pair(t, first=False, last=False, halves=(0, 1)):
                ready(t, 1)
                for h in halves:
                    for hd in range(2):
                        ins = product(bank[h][:, :], (mo_hi[:, hd, half(h)], mo_lo[:, hd, half(h)]),
                                      wcols(t, OFF[1] + hd * 512, 512), first and hd == 0, last and hd == 1)
                    if last:
                        ins.then_inc(bank_full[h], 1)
                if not last and 1 in halves:
                    ins.then_inc(used[1], 1)

            def pair_step(j, s, first_out=False):
                n = j * (2 * PER_PAIR) + s * PER_PAIR
                start = isinstance(j, int) and s == 0
                last_out = Tile(j, T_M + s - 1)
                pe.wait_ge(ev_lo, V_MLA - 2 if start else n + (V_MLA - 3))
                score_pair()
                project_pair(Tile(j, T_M + s + 1), n + (V_MLA - 1))
                if not start:
                    out_pair(last_out, first=first_out, halves=(0,))
                transpose_pair(j * 8 + 4 * s, told=used[0])
                rope_transpose(j * 2 + (s + 2))
                if not start:
                    out_pair(last_out, first=first_out, halves=(1,))
                pe.wait_ge(ev_lo, n + (V_MLA + 3))
                values_pair(s % 2)

            project_pair(Tile(0, T_M))
            rope_transpose(1, told=used[0])
            pair_step(0, 0)
            pair_step(0, 1, first_out=True)
            with pe.Fori(0, 2) as j:
                pair_step(j, 2)
                pair_step(j, 3)
            pair_step(0, 6)
            n = V_MLA + (PAIRS - 1) * PER_PAIR
            pe.wait_ge(ev_lo, n - 3)
            score_pair()
            pe.wait_ge(ev_lo, n - 1)
            out_pair(Tile(0, T_M + PAIRS - 2))
            transpose_pair(4 * (PAIRS - 1))
            pe.wait_ge(ev_lo, n + 1)
            values_pair((PAIRS - 1) % 2)
            pe.wait_ge(ev_lo, n + 2)
            out_pair(Tile(0, T_M + PAIRS - 1), last=True)

            pe.wait_ge(xn_ready, 6)
            transpose_rows(xn)
            pe.wait_ge(ev_lo, V_LN3 + 1)

            def gate_up(j, s, told=None):
                t = Tile(j, T_E + s)
                b = 2 * (s % 2)
                for u in range(2):
                    for m in range(2):
                        for c in range(NC):
                            k = 0 if u == 0 or c == 0 else 2
                            if m == 0 and (c == 0 and u == 0 or c == 1 and u == 1):
                                ready(t, k)
                            at = (u * NC + c) * I if k == 0 else OFF[2] + (c - 1) * I
                            ins = product(bank[b + u][:, m * T:m * T + T], wcols(t, at + m * P, P),
                                          (xt_hi[:, c, :], xt_lo[:, c, :]), c == 0, c == NC - 1,
                                          told if u == m == c == 0 else None)
                            if u == m == 1 and c == 0:
                                ins.then_inc(used[0], 1)
                    ins.then_inc(bank_full[b + u], 1)

            def down(j, s, told=None):
                t = Tile(j, T_E + s)
                pe.wait_ge(ev_lo, j * 2 + (V_H + s))
                ready(t, 1)
                for h in range(2):
                    b = 4 + 2 * (s % 2) + h
                    pe.wait_ge(res_done, j * 4 + (2 * s + h + 1))
                    for m in range(2):
                        a = slice(m * T + h * P, m * T + h * P + P)
                        ins = product(bank[b][:, :], (h_hi[:, s % 2, a], h_lo[:, s % 2, a]),
                                      wcols(t, OFF[1] + m * 512, 512), m == 0, m == 1,
                                      told if h == m == 0 else None)
                    ins.then_inc(bank_full[b], 1)

            for h in range(2):
                for c in range(NC):
                    ins = product(bank[4][:, h * E:h * E + E], (xt_hi[:, c, half(h)], xt_lo[:, c, half(h)]),
                                  (rw_hi[:, c, :], rw_lo[:, c, :]), c == 0, c == NC - 1,
                                  used[1] if h == c == 0 else None)
            ins.then_inc(bank_full[4], 1)
            gate_up(0, 0)
            gate_up(0, 1, told=used[2])
            pe.wait_ge(sigmoid_ready, 1)
            down(0, 0, told=used[2])
            gate_up(0, 2, told=used[1])
            down(0, 1, told=used[2])
            with pe.Fori(1, NE // 2 - 1) as j:
                gate_up(j, 1, told=used[1])
                down(j, 0, told=used[2])
                gate_up(j, 2, told=used[1])
                down(j, 1, told=used[2])
            gate_up(0, NE - 1, told=used[1])
            down(0, NE - 2, told=used[2])
            down(0, NE - 1)

        @block.scalar
        def _(act):
            act.wait_ge(small_loaded, 16)
            act.copy(ident_r[:, :], smalls[:, C_ID:C_ID + P]).then_inc(consts_rounded, 1)
            act.copy(mask_r[:, :], smalls[:, C_MASK:C_MASK + P]).then_inc(consts_rounded, 1)
            act.copy(flat(rw_hi[:, :, :]), smalls[:, C_RW:C_RW + NC * E]).then_inc(consts_rounded, 1)
            for k in range(2):
                split_hi(act, Tile(0, T_WQ), k, X_SIZES, first=True)
            for b in range(2):
                out_hi(act, b, F01["ln1"], flat(xt_hi[:, 2 * b:2 * b + 2, :]), 512)
            for k in range(2):
                split_hi(act, Tile(0, T_WK), k, X_SIZES, first=True)
            for b in range(2):
                out_hi(act, 2 + b, F23["q"], flat(q_hi[:, 2 * b:2 * b + 2, :]), 512)
            for k in range(2):
                split_hi(act, Tile(0, T_CT), k, X_SIZES)
            for b in range(2):
                out_hi(act, 4 + b, F45["k"], flat(k_hi[:, 2 * b:2 * b + 2, :]), 512)

            with act.Fori(0, NG // 2) as j:
                for s in range(2):
                    for k in range(2):
                        split_hi(act, Tile(j, T_CT + s + 1), k, X_SIZES)
                    for h in range(2):
                        b = 2 * s + h
                        act.wait_ge(bank_full[b], j + (F01["s_even"] if s == 0 else F23["s_odd"]))
                        act.copy(scores[:, h, bass.ds(j * 1024 + s * 512, 512)], bank[b][:, :]) \
                           .then_inc(s_copied, 1)
            for h in range(2):
                act.wait_ge(bank_full[h], F01["s_new"])
                act.copy(scores[:, h, CTX:KEYS], bank[h][:, 0:T]).then_inc(s_copied, 1)
            for k in range(2):
                split_hi(act, Tile(0, T_CN), k, X_SIZES)

            def exps(ring, at, n, sum_at):
                for h in range(2):
                    act.activation(probs[:, ring, h, 0:n], scores[:, h, at], ACT.Exp, bias=exp_bias[:, h:h + 1],
                                   scale=XSCALE, accum_out=sums[:, h, sum_at]).then_inc(p_ready, 1)

            def probs_hi(ring, full, n=512):
                for h in range(2):
                    out_hi(act, 2 * ring + h, full, pt_hi[:, ring, h, 0:n], n)

            act.wait_ge(bias_ready, 1)
            exps(1, slice(CTX, KEYS), T, slice(NG, NG + 1))
            exps(0, slice(0, 512), 512, slice(0, 1))
            for b in range(2):
                out_hi(act, 4 + b, F45["v"], v_hi[:, b, :], 512)
            probs_hi(1, F23["pt_new"], T)
            exps(1, slice(512, 1024), 512, slice(1, 2))
            probs_hi(0, F01["pt_even"])
            with act.Fori(0, NG // 2 - 1) as j:
                for s in range(2):
                    exps(s, bass.ds(j * 1024 + (s + 2) * 512, 512), 512, bass.ds(j * 2 + (s + 2), 1))
                    probs_hi(1 - s, j + (F23["pt_odd"] if s == 0 else F01["pt_even"] + 1))
                    for k in range(2):
                        split_hi(act, Tile(j, T_CN + s + 1), k, X_SIZES)
            probs_hi(1, F23["pt_odd"] + 3)
            for s in (NG - 1, NG):
                for k in range(2):
                    split_hi(act, Tile(0, T_CN + s), k, X_SIZES)

            for b in range(2):
                out_hi(act, b, F01["ot"], flat(ot_hi[:, 2 * b:2 * b + 2, :]), 512)
            for k in range(2):
                split_hi(act, Tile(0, T_QKV), k, Q_SIZES)
            for b in range(2):
                out_hi(act, b, F01["ln2"], flat(xt_hi[:, 2 * b:2 * b + 2, :]), 512)
            for k in range(2):
                split_hi(act, Tile(0, T_M), k, M_SIZES)
            for h in range(2):
                act.wait_ge(bank_full[2 + h], F23["qkv"])
                act.copy(qkv_row[:, h, :], bank[2 + h][:, 0:384]).then_inc(qkv_copied, 1)
            for c in range(2):
                out_hi(act, 4, F45["c"], qc_hi[0:QR2, c, :], T, rows=slice(0, QR2), at=c * T,
                       scale=smalls[0:QR2, C_GQ + c:C_GQ + c + 1])
            out_hi(act, 5, F45["c"], kvc_hi, T, scale=smalls[:, C_GKV:C_GKV + 1])
            act.wait_ge(kr_zeroed, 2)
            for hd in range(2):
                r = slice(hd * ROPE, hd * ROPE + ROPE)
                out_hi(act, 5, F45["c"], kr_hi[r, hd, :], T, rows=r, at=T)
            split_hi(act, Tile(0, T_M + 1), 0, M_SIZES)

            def pair_qk_hi(j, s):
                out_hi(act, 4, j * 2 + (F4["q"] + s), flat(mq_hi[:, :, :]), 512)
                out_hi(act, 5, F5["k0"] if isinstance(j, int) and s == 0 else j * 4 + (F5["k"] + 2 * s),
                       flat(mk_hi[:, :, :]), 512)

            def pair_v_hi(j, s):
                out_hi(act, 6, j * 2 + (F6["v"] + s), flat(mv_hi[:, s % 2, :, :]), 512)

            def pair_exps(j, s):
                act.wait_ge(m_bias_ready, j * 2 + (s + 1))
                for hd in range(2):
                    for late, at, n in ((0, 0, T), (1, T, P)):
                        k = 2 * hd + late
                        act.activation(pair_probs[:, hd, at:at + n], bank[2 + hd][:, at:at + n], ACT.Exp,
                                       bias=m_bias[:, k:k + 1], scale=MSCALE, accum_out=m_sum[:, k:k + 1]) \
                           .then_inc(m_exp, 1)

            def pair_probs_hi(j, s):
                for hd in range(2):
                    out_hi(act, 2 + hd, j * 4 + (F23["pt"] + 2 * s), mpt_hi[:, hd, :], 384)

            def rope_hi(j, s):
                out_hi(act, 7, j * 4 + (F7["rope_t"] + 2 * s), qr_hi, T, at=T)

            def pair_step(j, s):
                split_hi(act, Tile(j, T_M + s + 2), 0, M_SIZES)
                pair_exps(j, s)
                pair_qk_hi(j, s + 1)
                pair_probs_hi(j, s)
                rope_hi(j, s + 1)
                pair_v_hi(j, s + 1)
                out_hi(act, 5, j * 4 + (F5["o"] + 2 * s), flat(mo_hi[:, :, :]), 512)
                split_hi(act, Tile(j, T_M + s + 1), 1, M_SIZES)

            pair_qk_hi(0, 0)
            rope_hi(0, 0)
            pair_v_hi(0, 0)
            pair_step(0, 0)
            with act.Fori(0, (PAIRS - 2) // 2) as j:
                pair_step(j, 1)
                pair_step(j, 2)
            pair_exps(0, PAIRS - 1)
            pair_probs_hi(0, PAIRS - 1)
            split_hi(act, Tile(0, T_E), 2, E_SIZES, first=True)
            split_hi(act, Tile(0, T_E), 1, E_SIZES)
            split_hi(act, Tile(0, T_E + 1), 0, E_SIZES)
            out_hi(act, 5, F5["o_last"], flat(mo_hi[:, :, :]), 512)
            split_hi(act, Tile(0, T_E + 1), 2, E_SIZES, first=True)
            for b in range(2):
                out_hi(act, b, F01["ln3"], flat(xt_hi[:, 2 * b:2 * b + 2, :]), 512)
            act.wait_ge(bank_full[4], F4["router"])
            act.activation(route(0, 2 * E), bank[4][:, 0:2 * E], ACT.Sigmoid).then_inc(sigmoid_ready, 1)

            def expert_step(j, s, ahead=2):
                act.wait_ge(bank_full[2 * (s % 2)], j + ((F01 if s % 2 == 0 else F23)["moe"] + s // 2))
                act.activation(gate_act[:, s % 2, :], bank[2 * (s % 2)][:, :], ACT.Silu).then_inc(silu_ready, 1)
                if ahead >= 1:
                    split_hi(act, Tile(j, T_E + s + 1), 1, E_SIZES)
                act.wait_ge(h_ready, j * 2 + (s + 1))
                act.copy(h_hi[:, s % 2, :], h_row[:, s % 2, :]).then_inc(ev_hi, 1)
                if ahead >= 2:
                    split_hi(act, Tile(j, T_E + s + 2), 0, E_SIZES)
                    split_hi(act, Tile(j, T_E + s + 2), 2, E_SIZES)

            with act.Fori(0, NE // 2 - 1) as j:
                expert_step(j, 0)
                expert_step(j, 1)
            expert_step(0, NE - 2, ahead=1)
            expert_step(0, NE - 1, ahead=0)

        @block.vector
        def _(dve):
            step = [0]

            def then(ins):
                step[0] += 1
                ins.then_inc(vec, 1)
                dve.wait_ge(vec, step[0])

            def layer_norm(n):
                for h in range(2):
                    then(dve.bn_stats(stat[:, h, :], res[:, h, :]))
                for h in range(2):
                    then(dve.bn_aggr(mean_var[:, h, :], stat[:, h, :]))
                dve.tensor_scalar(var_eps[:, 0:2], mean_var[:, :, 1], LN_EPS, None, ALU.add) \
                   .then_inc(var_ready, 1)
                dve.wait_ge(rstd_ready, (1, 2, 4)[n])
                for h in range(2):
                    dve.tensor_scalar(xn[:, h, :], res[:, h, :], mean_var[:, h, 0:1], rstd[:, h:h + 1],
                                      ALU.subtract, ALU.mult).then_inc(xn_ready, 1)

            def add_to_residual(b, full, number):
                for h in range(2):
                    dve.wait_ge(bank_full[b + h], full)
                    dve.tensor_tensor(res[:, h, :], bank[b + h][:, :], res[:, h, :], ALU.add) \
                       .then_inc(res_done, 1)
                dve.wait_ge(res_done, number)

            def split_pair_lo(number, b, hi, lo):
                for k in range(2):
                    out_lo(dve, b + k, number + k, flat(hi[:, 2 * k:2 * k + 2, :]),
                           flat(lo[:, 2 * k:2 * k + 2, :]), 512)

            dve.wait_ge(x_loaded, 16)
            layer_norm(0)
            dve.wait_ge(consts_rounded, 3)
            then(dve.tensor_tensor(flat(rw_lo[:, :, :]), smalls[:, C_RW:C_RW + NC * E],
                                   flat(rw_hi[:, :, :]).bitcast(F32), ALU.subtract))
            split_lo(dve, Tile(0, T_WQ), 0, X_SIZES)
            split_pair_lo(V_LN1, 0, xt_hi, xt_lo)
            split_lo(dve, Tile(0, T_WK), 0, X_SIZES)
            split_pair_lo(V_Q, 2, q_hi, q_lo)
            split_lo(dve, Tile(0, T_CT), 0, X_SIZES)
            split_pair_lo(V_K, 4, k_hi, k_lo)
            with dve.Fori(0, NG // 2) as j:
                for s in range(2):
                    split_lo(dve, Tile(j, T_CT + s + 1), 0, X_SIZES)
                    for h in range(2):
                        dve.wait_ge(s_copied, j * 4 + (2 * s + h + 1))
                        dve.tensor_reduce(row_max[:, h, bass.ds(j * 2 + s, 1)],
                                          scores[:, h, bass.ds(j * 1024 + s * 512, 512)], AX, ALU.max) \
                           .then_inc(s_max, 1)
            for h in range(2):
                dve.wait_ge(s_copied, 2 * NG + h + 1)
                dve.tensor_reduce(row_max[:, h, NG:NG + 1], scores[:, h, CTX:KEYS], AX, ALU.max) \
                   .then_inc(s_max, 1)
            dve.wait_ge(s_max, 2 * NG + 2)
            then(dve.tensor_reduce(neg_max[:, :], row_max[:, :, :], AX, ALU.max, negate=True))
            dve.tensor_scalar(exp_bias[:, :], neg_max[:, :], XSCALE, None, ALU.mult).then_inc(bias_ready, 1)
            split_lo(dve, Tile(0, T_CN), 0, X_SIZES)
            for b in range(2):
                out_lo(dve, 4 + b, V_V + b, v_hi[:, b, :], v_lo[:, b, :], 512)

            def probs_lo(ring, number, n=512):
                for h in range(2):
                    out_lo(dve, 2 * ring + h, number + h, pt_hi[:, ring, h, 0:n], pt_lo[:, ring, h, 0:n], n)

            probs_lo(1, V_PT, T)
            probs_lo(0, V_PT + 2)
            with dve.Fori(0, NG // 2 - 1) as j:
                for s in range(2):
                    probs_lo(1 - s, j * 4 + (V_PT + 4 + 2 * s))
                    split_lo(dve, Tile(j, T_CN + s + 1), 0, X_SIZES)
            probs_lo(1, V_PT + 16)
            for s in (NG - 1, NG):
                split_lo(dve, Tile(0, T_CN + s), 0, X_SIZES)
            dve.wait_ge(p_ready, 2 * (NG + 1))
            then(dve.tensor_reduce(row_sum[:, :], sums[:, :, :], AX, ALU.add))
            then(dve.reciprocal(row_inv[:, :], row_sum[:, :]))
            for h in range(2):
                dve.wait_ge(bank_full[6 + h], F67["pv"])
                dve.tensor_scalar(o_row[:, h, :], bank[6 + h][:, :], row_inv[:, h:h + 1], None, ALU.mult) \
                   .then_inc(o_ready, 1)
            split_pair_lo(V_OT, 0, ot_hi, ot_lo)
            split_lo(dve, Tile(0, T_QKV), 0, Q_SIZES)
            add_to_residual(4, F45["wo"], 2)

            layer_norm(1)
            split_pair_lo(V_LN2, 0, xt_hi, xt_lo)
            dve.memset(kr_hi.bitcast(F32)[:, :, :], 0.0).then_inc(kr_zeroed, 1)
            dve.memset(kr_lo.bitcast(F32)[:, :, :], 0.0).then_inc(kr_zeroed, 1)
            dve.wait_ge(qkv_copied, 2)
            for h in range(2):
                for at, n, k in ((0, Q_RANK, h), (Q_RANK, KV_RANK, 2 + h)):
                    v = qkv_row[:, h, at:at + n]
                    then(dve.tensor_tensor_reduce(squares[:, 0:n], v, v, 1.0 / n, 0.0, ALU.mult, ALU.add,
                                                  rstd[:, k:k + 1]))
            dve.tensor_scalar(var_eps[:, :], rstd[:, :], RMS_EPS, None, ALU.add).then_inc(var_ready, 1)
            cos64 = smalls[:, C_COS:C_COS + 256].rearrange("p (h d n) -> p h d n", h=2, d=2)[:, :, 0, :]
            sin64 = smalls[:, C_SIN:C_SIN + 256].rearrange("p (h d n) -> p h d n", h=2, d=2)[:, :, 0, :]
            kr_raw = qkv_row[:, :, Q_RANK + KV_RANK:384]
            kc = kr_cos.rearrange("p (h n) -> p h n", h=2)
            ks = kr_sin.rearrange("p (h n) -> p h n", h=2)
            R2 = ROPE // 2
            then(dve.tensor_tensor(kc, kr_raw, cos64, ALU.mult))
            then(dve.tensor_tensor(ks[:, :, 0:R2], kr_raw[:, :, R2:ROPE], sin64[:, :, 0:R2], ALU.mult))
            then(dve.tensor_tensor(ks[:, :, R2:ROPE], kr_raw[:, :, 0:R2], sin64[:, :, R2:ROPE], ALU.mult))
            for d in range(2):
                then(dve.tensor_tensor(kr_row[:, :, d * ROPE:d * ROPE + ROPE], kc, ks, ALU.add))
            dve.wait_ge(rstd_ready, 3)
            for h in range(2):
                then(dve.tensor_scalar(qc_row[:, h, :], qkv_row[:, h, 0:Q_RANK], rstd[:, h:h + 1], None, ALU.mult))
                ins = dve.tensor_scalar(kvc_row[:, h, :], qkv_row[:, h, Q_RANK:Q_RANK + KV_RANK],
                                        rstd[:, 2 + h:3 + h], None, ALU.mult)
                if h == 0:
                    then(ins)
            ins.then_inc(rows_ready, 1)

            def gained_lo(b, at, rows, gain, number, hi, lo):
                dve.wait_ge(ev_hi, number)
                dve.scalar_tensor_tensor(out=lo, in0=bank[b][rows, at:at + T], scalar=gain,
                                         in1=hi.bitcast(F32), op0=ALU.mult, op1=ALU.subtract) \
                   .then_inc(ev_lo, 1)

            q96 = slice(0, QR2)
            for c in range(2):
                gained_lo(4, c * T, q96, smalls[q96, C_GQ + c:C_GQ + c + 1], V_QC + 1, qc_hi[q96, c, :],
                          qc_lo[q96, c, :])
            gained_lo(5, 0, slice(0, P), smalls[:, C_GKV:C_GKV + 1], V_KR + 1, kvc_hi, kvc_lo)
            for hd in range(2):
                r = slice(hd * ROPE, hd * ROPE + ROPE)
                out_lo(dve, 5, V_KR + 1, kr_hi[r, hd, :], kr_lo[r, hd, :], T, rows=r, at=T)

            def pair_bias(j, s):
                for hd in range(2):
                    dve.wait_ge(bank_full[2 + hd], j * 4 + (F23["scores"] + 2 * s))
                    for k, at, n in ((2 * hd, 0, T), (2 * hd + 1, T, P)):
                        dve.tensor_reduce(m_neg[:, k:k + 1], bank[2 + hd][:, at:at + n], AX, ALU.max,
                                          negate=True).then_inc(m_neg_ready, 1)
                dve.wait_ge(m_neg_ready, j * 8 + (4 * s + 4))
                dve.tensor_scalar(m_bias[:, :], m_neg[:, :], MSCALE, None, ALU.mult).then_inc(m_bias_ready, 1)

            def rope_rows(j, s):
                dve.wait_ge(bank_full[7], j * 4 + (F7["rope"] + 2 * s))
                q = bank[7][:, 0:256]
                dve.tensor_tensor(q_cos, q, smalls[:, C_COS:C_COS + 256], ALU.mult).then_inc(rope_part, 1)
                q4, s4, t4 = (v.rearrange("p (g n) -> p g n", n=ROPE)
                              for v in (q, smalls[:, C_SIN:C_SIN + 256], q_sin))
                dve.tensor_tensor(t4[:, :, 0:R2], q4[:, :, R2:ROPE], s4[:, :, 0:R2], ALU.mult) \
                   .then_inc(rope_part, 1)
                dve.tensor_tensor(t4[:, :, R2:ROPE], q4[:, :, 0:R2], s4[:, :, R2:ROPE], ALU.mult) \
                   .then_inc(rope_part, 1)
                dve.wait_ge(rope_part, j * 6 + (3 * s + 3))
                dve.tensor_tensor(q_rope, q_cos, q_sin, ALU.add).then_inc(rope_ready, 1)

            def pair_normalize(j, s):
                dve.wait_ge(m_exp, j * 8 + (4 * s + 4))
                dve.reciprocal(m_inv[:, :], m_sum[:, :]).then_inc(m_inv_ready, 1)
                dve.wait_ge(m_inv_ready, j * 2 + (s + 1))
                for hd in range(2):
                    for k, at, n in ((2 * hd, 0, T), (2 * hd + 1, T, P)):
                        v = pair_probs[:, hd, at:at + n]
                        dve.tensor_scalar(v, v, m_inv[:, k:k + 1], None, ALU.mult).then_inc(m_norm, 1)

            def pair_qk_lo(n):
                out_lo(dve, 4, n, flat(mq_hi[:, :, :]), flat(mq_lo[:, :, :]), 512)
                out_lo(dve, 5, n + 1, flat(mk_hi[:, :, :]), flat(mk_lo[:, :, :]), 512)

            def pair_rope_v_lo(n, s):
                out_lo(dve, 7, n, qr_hi, qr_lo, T, at=T)
                out_lo(dve, 6, n + 1, flat(mv_hi[:, s % 2, :, :]), flat(mv_lo[:, s % 2, :, :]), 512)

            def pair_probs_lo(n):
                for hd in range(2):
                    out_lo(dve, 2 + hd, n + hd, mpt_hi[:, hd, :], mpt_lo[:, hd, :], 384)

            def pair_step(j, s):
                n = j * (2 * PER_PAIR) + (V_MLA + s * PER_PAIR)
                pair_bias(j, s)
                rope_rows(j, s + 1)
                pair_normalize(j, s)
                pair_qk_lo(n)
                pair_probs_lo(n + 2)
                pair_rope_v_lo(n + 4, s + 1)
                out_lo(dve, 5, n + 6, flat(mo_hi[:, :, :]), flat(mo_lo[:, :, :]), 512)

            rope_rows(0, 0)
            pair_qk_lo(V_M0)
            pair_rope_v_lo(V_M0 + 2, 0)
            pair_step(0, 0)
            with dve.Fori(0, (PAIRS - 2) // 2) as j:
                pair_step(j, 1)
                pair_step(j, 2)
            pair_bias(0, PAIRS - 1)
            pair_normalize(0, PAIRS - 1)
            n = V_MLA + (PAIRS - 1) * PER_PAIR
            pair_probs_lo(n)
            out_lo(dve, 5, n + 2, flat(mo_hi[:, :, :]), flat(mo_lo[:, :, :]), 512)
            split_lo(dve, Tile(0, T_E), 2, E_SIZES)
            split_lo(dve, Tile(0, T_E), 1, E_SIZES, handed_over=True)
            split_lo(dve, Tile(0, T_E + 1), 2, E_SIZES)
            add_to_residual(0, F01["y"], 4)

            layer_norm(2)
            split_pair_lo(V_LN3, 0, xt_hi, xt_lo)

            score = route(0, 64)
            choice, big, small_, g_top, g_low, g_two = (route(64 + 64 * k, 64) for k in range(6))
            beats, ties = route(448, 128), route(576, 128)
            rank, chosen_g = route(704, 16), route(720, 16)
            masked, replaced = route(736, 64), route(800, 64)
            top8, picked = route(864, 16), route(880, 64)
            total, scaled = route(944, 2), route(946, 2)

            def pairs_of(v):
                g = v.rearrange("p (g n) -> p g n", n=PER)
                return g[:, :, 0:2], g[:, :, 2:4]

            def by2(v):
                return v[:, 0:32].rearrange("p (g n) -> p g n", n=2)

            dve.wait_ge(sigmoid_ready, 1)
            then(dve.tensor_tensor(choice, score, smalls[:, C_BIAS:C_BIAS + 64], ALU.add))
            a, b = pairs_of(choice)
            then(dve.tensor_tensor(by2(big), a, b, ALU.max))
            then(dve.tensor_tensor(by2(small_), a, b, ALU.min))
            big2, small2 = by2(big), by2(small_)
            then(dve.tensor_tensor(g_top[:, 0:16], big2[:, :, 0], big2[:, :, 1], ALU.max))
            then(dve.tensor_tensor(g_low[:, 0:16], big2[:, :, 0], big2[:, :, 1], ALU.min))
            then(dve.tensor_tensor(g_two[:, 0:16], small2[:, :, 0], small2[:, :, 1], ALU.max))
            then(dve.tensor_tensor(g_two[:, 16:32], g_low[:, 0:16], g_two[:, 0:16], ALU.max))
            then(dve.tensor_tensor(g_two[:, 32:48], g_top[:, 0:16], g_two[:, 16:32], ALU.add))
            by_half = g_two[:, 32:48].rearrange("p (h g) -> p h g", h=2)
            cube = [P, 2, GROUPS, GROUPS]
            other = by_half.unsqueeze(2).broadcast_to(cube)
            own = by_half.unsqueeze(3).broadcast_to(cube)

            def cubed(v):
                return v.rearrange("p (h i k) -> p h i k", h=2, i=GROUPS)

            then(dve.tensor_tensor(cubed(beats), other, own, ALU.is_gt))
            then(dve.tensor_tensor(cubed(ties), other, own, ALU.is_equal))
            then(dve.tensor_tensor(ties, ties, smalls[:, C_TIE:C_TIE + 128], ALU.mult))
            then(dve.tensor_tensor(beats, beats, ties, ALU.add))
            then(dve.tensor_reduce(rank, beats.rearrange("p (g k) -> p g k", k=GROUPS), AX, ALU.add))
            then(dve.tensor_scalar(chosen_g, rank, float(TOP_GROUPS), None, ALU.is_lt))
            then(dve.tensor_tensor(masked.rearrange("p (g n) -> p g n", n=PER),
                                   choice.rearrange("p (g n) -> p g n", n=PER),
                                   chosen_g.unsqueeze(2).broadcast_to([P, 2 * GROUPS, PER]), ALU.mult))
            then(dve.tensor_scalar(masked, masked, 0.0, None, ALU.add))
            for h in range(2):
                m = masked[:, h * E:h * E + E]
                then(dve.max(top8[:, h * TOP:h * TOP + TOP], m))
                then(dve.match_replace(replaced[:, h * E:h * E + E], top8[:, h * TOP:h * TOP + TOP], m, TAKEN))
            then(dve.tensor_tensor(picked, replaced, masked, ALU.not_equal))
            then(dve.tensor_tensor(picked, picked, score, ALU.mult))
            then(dve.tensor_reduce(total, picked.rearrange("p (h n) -> p h n", h=2), AX, ALU.add))
            then(dve.reciprocal(scaled, total))
            then(dve.memset(weights[:, :, 0:SHARED], 1.0))
            for h in range(2):
                then(dve.tensor_scalar(weights[:, h, SHARED:NE], picked[:, h * E:h * E + E], scaled[:, h:h + 1],
                                       ROUTED_SCALE, ALU.mult, ALU.mult))

            def expert_step(j, s, ahead=2):
                dve.wait_ge(silu_ready, j * 2 + (s + 1))
                up = 2 * (s % 2) + 1
                dve.wait_ge(bank_full[up], j + ((F01 if s % 2 == 0 else F23)["moe"] + s // 2))
                dve.tensor_tensor(h_row[:, s % 2, :], bank[up][:, :], gate_act[:, s % 2, :], ALU.mult) \
                   .then_inc(h_ready, 1)
                dve.wait_ge(ev_hi, j * 2 + (V_H + s))
                dve.tensor_tensor(h_lo[:, s % 2, :], h_row[:, s % 2, :], h_hi[:, s % 2, :].bitcast(F32),
                                  ALU.subtract).then_inc(ev_lo, 1)
                if ahead >= 1:
                    split_lo(dve, Tile(j, T_E + s + 1), 1, E_SIZES)
                if ahead >= 2:
                    split_lo(dve, Tile(j, T_E + s + 2), 2, E_SIZES)
                for h in range(2):
                    b = 4 + 2 * (s % 2) + h
                    first = {4: F4, 5: F5, 6: F6, 7: F7}[b]["moe"]
                    dve.wait_ge(bank_full[b], j + (first + s // 2))
                    dve.wait_ge(res_done, j * 4 + (3 + 2 * s + h))
                    w = weights[:, h, bass.ds(j * 2 + s, 1)]
                    dve.scalar_tensor_tensor(out=res[:, h, :], in0=bank[b][:, :], scalar=w, in1=res[:, h, :],
                                             op0=ALU.mult, op1=ALU.add).then_inc(res_done, 1)

            with dve.Fori(0, NE // 2 - 1) as j:
                expert_step(j, 0)
                expert_step(j, 1)
            expert_step(0, NE - 2, ahead=1)
            expert_step(0, NE - 1, ahead=0)

        @block.gpsimd
        def _(pool):
            def root(n, cols):
                pool.wait_ge(var_ready, n)
                pool.tensor_tensor(rstd[:, 0:cols], var_eps[:, 0:cols], power[:, 0:cols], ALU.pow) \
                    .then_inc(rstd_ready, 1)

            pool.memset(power[:, :], -0.5).then_inc(power_set, 1)
            pool.wait_ge(power_set, 1)
            root(1, 2)
            for t in (T_WQ, T_WK, T_CT):
                split_lo(pool, Tile(0, t), 1, X_SIZES)
            with pool.Fori(0, NG // 2) as j:
                for s in range(2):
                    split_lo(pool, Tile(j, T_CT + s + 1), 1, X_SIZES)
            split_lo(pool, Tile(0, T_CN), 1, X_SIZES)
            with pool.Fori(0, NG // 2) as j:
                for s in range(2):
                    split_lo(pool, Tile(j, T_CN + s + 1), 1, X_SIZES)
            split_lo(pool, Tile(0, T_QKV), 1, Q_SIZES)
            root(2, 2)
            split_lo(pool, Tile(0, T_M), 0, M_SIZES, handed_over=True)
            split_lo(pool, Tile(0, T_M), 1, M_SIZES)
            root(3, 4)
            split_lo(pool, Tile(0, T_M + 1), 0, M_SIZES)
            split_lo(pool, Tile(0, T_M + 2), 0, M_SIZES)
            split_lo(pool, Tile(0, T_M + 1), 1, M_SIZES)
            with pool.Fori(0, (PAIRS - 2) // 2) as j:
                for s in range(1, 3):
                    split_lo(pool, Tile(j, T_M + s + 2), 0, M_SIZES)
                    split_lo(pool, Tile(j, T_M + s + 1), 1, M_SIZES)
            split_lo(pool, Tile(0, T_E + 1), 0, E_SIZES)
            root(4, 2)
            with pool.Fori(0, NE // 2 - 1) as j:
                for s in range(2):
                    split_lo(pool, Tile(j, T_E + s + 2), 0, E_SIZES)


def _rope_tables():
    half = np.arange(0, ROPE, 2, dtype=np.float32) / np.float32(ROPE)
    inv = (np.float32(1.0) / np.power(np.float32(10000.0), half)).astype(np.float32)
    ang = np.arange(T, dtype=np.float32)[:, None] * inv[None, :]
    ang = np.concatenate([ang, ang], axis=-1).astype(np.float32)
    sign = np.where(np.arange(ROPE) < ROPE // 2, np.float32(-1), np.float32(1))
    return np.cos(ang), np.sin(ang) * sign


def _chunked(w):
    return np.ascontiguousarray(w.reshape(NC, P, -1).transpose(1, 0, 2).reshape(P, -1))


def kernel(**inputs):
    import concourse.bacc as _bacc
    from concourse.bass_utils import run_bass_kernel_spmd as _run

    a = {k: np.asarray(v) for k, v in inputs.items()}
    rows = a["x"][0].reshape(2, P, D).transpose(1, 0, 2)

    small = np.zeros((P, C_END), np.float32)
    small[:, C_ID:C_ID + P] = np.eye(P, dtype=np.float32)
    small[:, C_MASK:C_MASK + P] = np.triu(np.full((P, P), MASKED, np.float32), 1)
    cos, sin = _rope_tables()
    for at, table in ((C_COS, cos), (C_SIN, sin)):
        t = np.repeat(table.reshape(2, P, 1, ROPE), 2, axis=2).transpose(1, 0, 2, 3)
        small[:, at:at + 256] = t.reshape(P, 256)
    small[:, C_RW:C_RW + NC * E] = _chunked(a["L0_ffn_router_w"])
    small[:, C_BIAS:C_BIAS + 64] = np.tile(a["L0_ffn_router_bias"], 2)[None, :]
    small[0:QR2, C_GQ:C_GQ + 2] = a["L0_attn_g_qa"].reshape(2, QR2).T
    small[:, C_GKV] = a["L0_attn_g_kva"]
    tie = np.tril(np.ones((GROUPS, GROUPS), np.float32), -1)
    small[:, C_TIE:C_END] = np.tile(tie.reshape(-1), 2)[None, :]

    context = a["ctx_2048"][0]
    ctx_t = np.stack([_chunked(context[g * 512:(g + 1) * 512].T) for g in range(NG)])
    ctx_n = np.stack([_chunked(context[g * 512:(g + 1) * 512]) for g in range(NG)])
    w_qkv = _chunked(np.concatenate([a["L0_attn_Wqa"], a["L0_attn_Wkva"]], axis=1))

    wqb = a["L0_attn_Wqb"].reshape(2, QR2, PAIRS, 2, NOPE + ROPE)
    wkvb = a["L0_attn_Wkvb"].reshape(KV_RANK, PAIRS, 2, NOPE + VDIM)
    wout = a["L0_attn_Wo"].reshape(PAIRS, 2, VDIM, D)
    w_mla = np.zeros((PAIRS, P, sum(M_SIZES)), np.float32)
    for i in range(PAIRS):
        for c in range(2):
            w = wqb[c, :, i]
            w_mla[i, 0:QR2, c * 384:c * 384 + 256] = w[:, :, 0:NOPE].reshape(QR2, 256)
            w_mla[i, 0:QR2, c * 384 + 256:c * 384 + 384] = w[:, :, NOPE:].reshape(QR2, 128)
        w_mla[i, :, 768:1024] = wkvb[:, i, :, 0:NOPE].reshape(P, 256)
        w_mla[i, :, 1024:1280] = wkvb[:, i, :, NOPE:].reshape(P, 256)
        w_mla[i, :, 1280:2304] = wout[i].transpose(1, 0, 2).reshape(P, 1024)

    def halves(w, axis):
        return np.stack(np.split(w, 2, axis=axis))

    gate = np.concatenate([halves(a["L0_ffn_sw_gate"], 1), a["L0_ffn_w_gate"]])
    up = np.concatenate([halves(a["L0_ffn_sw_up"], 1), a["L0_ffn_w_up"]])
    down = np.concatenate([halves(a["L0_ffn_sw_down"], 0), a["L0_ffn_w_down"]])
    gate, up = (w.reshape(NE, NC, P, I).transpose(0, 2, 1, 3).reshape(NE, P, NC * I) for w in (gate, up))
    down = down.reshape(NE, 2, P, D).transpose(0, 2, 1, 3).reshape(NE, P, 2 * D)
    w_exp = np.concatenate([gate, up[:, :, 0:I], down, up[:, :, I:]], axis=2)

    arrays = {
        "x": rows, "small": small,
        "wq": _chunked(a["L0_xattn_wq"].T), "wk": _chunked(a["L0_xattn_wk"].T),
        "wv": _chunked(a["L0_xattn_wv"].T), "wo": _chunked(a["L0_xattn_wo"].T),
        "ctx_t": ctx_t, "ctx_n": ctx_n, "w_qkv": w_qkv, "w_mla": w_mla, "w_exp": w_exp,
    }
    arrays = {f"{k}_dram": np.ascontiguousarray(v) for k, v in arrays.items()}
    nc = _bacc.Bacc("TRN2", target_bir_lowering=False, num_devices=1)
    args = [nc.dram_tensor(k, v.shape, F32, kind="ExternalInput").ap() for k, v in arrays.items()]
    args.append(nc.dram_tensor("out_dram", (P, 2, D), F32, kind="ExternalOutput").ap())
    perceiver_layer(nc, *args)
    r = _run(nc, [arrays], core_ids=[0])
    return r.results[0]["out_dram"].transpose(1, 0, 2).reshape(1, T, D)
```

```python
from contextlib import ExitStack

import numpy as np

import concourse.bass as bass
from concourse import mybir

F32 = mybir.dt.float32
F32R = mybir.dt.float32r
ALU = mybir.AluOpType
ACT = mybir.ActivationFunctionType
AX = mybir.AxisListType.X

P = 128
T = 256
D = 512
NC = D // P
CTX = 4096
NG = CTX // 512
KEYS = CTX + T
HEADS, NOPE, ROPE, VDIM = 16, 128, 64, 128
Q_RANK, KV_RANK = 192, 128
QR2 = Q_RANK // 2
PAIRS = HEADS // 2
E, GROUPS, TOP_GROUPS, TOP, I = 32, 8, 4, 8, 256
PER = E // GROUPS
SHARED = 2
NE = E + SHARED
ROUTED_SCALE = 2.5
LN_EPS, RMS_EPS = 1e-5, 1e-6
XSCALE = 1.0 / float(np.sqrt(D))
MSCALE = float(NOPE + ROPE) ** -0.5
MASKED = -1e30
TAKEN = -3e38

T_WQ, T_WK, T_CT, T_WV, T_CN, T_WO, T_QKV, T_ROPE, T_M = 0, 1, 2, 10, 11, 19, 20, 21, 22
T_E = T_M + PAIRS

OFF = (0, 1280, 2304)
SLOT = 3072
X_SIZES = (1024, 1024)
Q_SIZES = (768, 768)
M_SIZES = (1024, 1024)
E_SIZES = (1280, 1024, 768)

C_ID, C_MASK, C_COS, C_SIN, C_RW, C_BIAS, C_GQ, C_GKV, C_TIE = 0, 128, 256, 384, 512, 640, 704, 896, 1024
C_END = C_TIE + 2 * GROUPS * GROUPS

F01 = dict(ln1=1, s_even=2, s_new=6, pt_even=7, ot=11, ln2=12, rope=13, y=14, ln3=15, moe=16)
F23 = dict(q=1, s_odd=2, pt_new=6, pt_odd=7, qkv=11, rope=12, scores=13, pt=14, moe=29)
F45 = dict(k=1, v=2, wo=3, c=4)
F4 = dict(q=5, o_last=13, router=14, moe=15)
F5 = dict(k0=5, k=4, o=7, o_last=20, moe=21)
F67 = dict(pv=1, c=2)
F6 = dict(v=3, score=11, moe=12)
F7 = dict(rope_t=3, moe=11)

V_LN1, V_Q, V_K, V_V, V_PT, V_OT, V_LN2, V_C, V_M0 = 1, 3, 5, 7, 9, 27, 29, 31, 35
V_MLA = V_M0 + 4
PER_PAIR = 7
V_LN3 = V_MLA + (PAIRS - 1) * PER_PAIR + 4
V_H = V_LN3 + 2


class Tile:

    def __init__(self, j, s):
        self.slot = s % 2
        self.loaded = (j + (s // 2 + 1)) * 16
        self.number = j * 2 + s

    def split(self, k):
        return self.number + 1 if k < 2 else self.number + (1 - T_E)

    def free(self, k):
        return self.number - 1 if k < 2 else self.number + (-1 - T_E)


def perceiver_layer(nc, x, small, wq, wk, wv, wo, ctx_t, ctx_n, w_qkv, w_rope, w_mla, w_exp, out):
    with ExitStack() as ctx:
        def sb(name, shape, dt=F32):
            return ctx.enter_context(nc.sbuf_tensor(name, shape, dt))

        def sem(name):
            return ctx.enter_context(nc.semaphore(name))

        bank = [ctx.enter_context(nc.psum_tensor(f"bank{b}", [P, 512], F32)) for b in range(8)]

        raw = sb("raw", [P, 2, SLOT])
        w_hi = sb("w_hi", [P, 2, SLOT], F32R)
        w_lo = sb("w_lo", [P, 2, SLOT], F32R)
        smalls = sb("smalls", [P, C_END])
        res = sb("res", [P, 2, D])
        xn = sb("xn", [P, 2, D])
        xt_hi = sb("xt_hi", [P, NC, T], F32R)
        xt_lo = sb("xt_lo", [P, NC, T], F32R)
        probs = sb("probs", [P, 2, 2, 512])
        o_row = sb("o_row", [P, 2, D])
        ident_r = sb("ident_r", [P, P], F32R)
        mask_r = sb("mask_r", [P, P], F32R)
        rw_hi = sb("rw_hi", [P, NC, E], F32R)
        rw_lo = sb("rw_lo", [P, NC, E], F32R)
        stat = sb("stat", [P, 2, 6])
        mean_var = sb("mean_var", [P, 2, 2])
        var_eps = sb("var_eps", [P, 6])
        power = sb("power", [P, 6])
        rstd = sb("rstd", [P, 6])
        row_max = sb("row_max", [P, 2, NG + 1])
        neg_max = sb("neg_max", [P, 2])
        exp_bias = sb("exp_bias", [P, 2])
        sums = sb("sums", [P, 2, NG + 1])
        row_sum = sb("row_sum", [P, 2])
        row_inv = sb("row_inv", [P, 2])
        m_neg = sb("m_neg", [P, 4])
        m_bias = sb("m_bias", [P, 4])
        m_sum = sb("m_sum", [P, 4])
        m_inv = sb("m_inv", [P, 4])
        weights = sb("weights", [P, 2, NE])

        operands = sb("operands", [P, 11776], F32R)

        def op(at, *shape):
            v = operands[:, at:at + int(np.prod(shape))]
            names = "abc"[:len(shape)]
            if len(shape) == 1:
                return v
            return v.rearrange(f"p ({' '.join(names)}) -> p {' '.join(names)}",
                               **dict(zip(names[1:], shape[1:])))

        q_hi, q_lo = op(0, NC, T), op(1024, NC, T)
        k_hi, k_lo = op(2048, NC, T), op(3072, NC, T)
        v_hi, v_lo = op(4096, 2, D), op(5120, 2, D)
        pt_hi, pt_lo = op(6144, 2, 2, 512), op(8192, 2, 2, 512)
        ot_hi, ot_lo = op(0, NC, T), op(1024, NC, T)
        qc_hi, qc_lo = op(2048, 2, T), op(2560, 2, T)
        ckr_hi, ckr_lo = op(3072, 3, T), op(3840, 3, T)
        kvc_hi, kvc_lo = ckr_hi[:, 0, :], ckr_lo[:, 0, :]
        kr_hi, kr_lo = ckr_hi[:, 1:3, :], ckr_lo[:, 1:3, :]
        mq_hi, mq_lo = op(4608, 2, T), op(5120, 2, T)
        mk_hi, mk_lo = op(5632, 2, T), op(6144, 2, T)
        qr_hi, qr_lo = op(6656, T), op(6912, T)
        mv_hi, mv_lo = op(7168, 2, 2, T), op(8192, 2, 2, T)
        mpt_hi, mpt_lo = op(9216, 2, 384), op(9984, 2, 384)
        mo_hi, mo_lo = op(10752, 2, T), op(11264, 2, T)
        h_hi, h_lo = op(0, 2, 512), op(1024, 2, 512)

        scores = sb("scores", [P, 2, KEYS])

        def row(at, n):
            return scores[:, 0, at:at + n]

        squares = row(0, 192)
        qkv_row = row(3712, 640).rearrange("p (h n) -> p h n", h=2)
        qc_row = row(1024, 384).rearrange("p (h n) -> p h n", h=2)
        kvc_row = row(1408, 256).rearrange("p (h n) -> p h n", h=2)
        kr_cos, kr_sin = row(256, ROPE), row(320, ROPE)
        kr_row = row(384, 512).rearrange("p (h n) -> p h n", h=2)
        pair_probs = row(2176, 768).rearrange("p (h n) -> p h n", h=2)
        q_cos = scores[:, 1, 0:2048].rearrange("p (h n) -> p h n", h=2)
        q_sin = scores[:, 1, 2048:4096].rearrange("p (h n) -> p h n", h=2)
        q_rope = row(3456, 256).rearrange("p (h n) -> p h n", h=2)
        gate_act = scores[:, 1, 0:1024].rearrange("p (r n) -> p r n", r=2)
        h_row = scores[:, 1, 1024:2048].rearrange("p (r n) -> p r n", r=2)

        score_t = scores[0:E, 1, 3200:3200 + T]

        def route(at, n):
            return scores[:, 1, 2048 + at:2048 + at + n]

        x_loaded = [sem(f"x_loaded{h}") for h in range(2)]
        ident_loaded = sem("ident_loaded")
        small_loaded = sem("small_loaded")
        loaded_a = [sem(f"loaded_a{s}") for s in range(2)]
        loaded_b = [sem(f"loaded_b{s}") for s in range(2)]
        hi_split = [sem(f"hi_split{k}") for k in range(3)]
        lo_split = [sem(f"lo_split{k}") for k in range(3)]
        used = [sem(f"used{k}") for k in range(3)]
        bank_full = [sem(f"bank_full{b}") for b in range(8)]
        ev_hi = sem("ev_hi")
        ev_lo = sem("ev_lo")
        consts_rounded = sem("consts_rounded")
        rw_split = sem("rw_split")
        vec = sem("vec")
        power_set = sem("power_set")
        var_ready = sem("var_ready")
        eps_added = sem("eps_added")
        rstd_ready = sem("rstd_ready")
        xn_ready = sem("xn_ready")
        s_copied = sem("s_copied")
        s_max = sem("s_max")
        bias_ready = sem("bias_ready")
        p_ready = sem("p_ready")
        o_ready = sem("o_ready")
        res_done = sem("res_done")
        kr_zeroed = sem("kr_zeroed")
        kr_part = sem("kr_part")
        kr_done = sem("kr_done")
        rows_ready = sem("rows_ready")
        m_neg_ready = sem("m_neg_ready")
        m_bias_ready = sem("m_bias_ready")
        m_exp = sem("m_exp")
        m_inv_ready = sem("m_inv_ready")
        m_norm = sem("m_norm")
        rope_part = sem("rope_part")
        rope_ready = sem("rope_ready")
        sigmoid_ready = sem("sigmoid_ready")
        score_taken = sem("score_taken")
        silu_ready = sem("silu_ready")
        h_ready = sem("h_ready")
        stored = sem("stored")

        def split_hi(act, t, k, sizes, first=False):
            act.wait_ge((loaded_b if k else loaded_a)[t.slot], t.loaded)
            if not first:
                act.wait_ge(used[k], t.free(k))
            at, n = OFF[k], sizes[k]
            act.copy(w_hi[:, t.slot, at:at + n], raw[:, t.slot, at:at + n]).then_inc(hi_split[k], 1)

        def split_lo(eng, t, k, sizes, handed_over=False):
            eng.wait_ge(hi_split[k], t.split(k))
            if handed_over:
                eng.wait_ge(lo_split[k], t.split(k) - 1)
            at, n = OFF[k], sizes[k]
            eng.tensor_tensor(w_lo[:, t.slot, at:at + n], raw[:, t.slot, at:at + n],
                              w_hi[:, t.slot, at:at + n].bitcast(F32), ALU.subtract) \
               .then_inc(lo_split[k], 1)

        def out_hi(act, b, full, hi, n, rows=slice(0, P), at=0, scale=1.0):
            act.wait_ge(bank_full[b], full)
            act.activation(hi, bank[b][rows, at:at + n], ACT.Copy, scale=scale).then_inc(ev_hi, 1)

        def out_lo(dve, b, number, hi, lo, n, rows=slice(0, P), at=0):
            dve.wait_ge(ev_hi, number)
            dve.tensor_tensor(lo, bank[b][rows, at:at + n], hi.bitcast(F32), ALU.subtract) \
               .then_inc(ev_lo, 1)

        def flat(v):
            return v.rearrange("p a b -> p (a b)")

        def half(h):
            return slice(h * P, h * P + P)

        def half_hi(act, b, full, hi, h, n=NC, rows=slice(0, P)):
            act.wait_ge(bank_full[b], full)
            act.activation(hi[rows, :, half(h)], bank[b][rows, 0:n * P].rearrange("p (c n) -> p c n", c=n),
                           ACT.Copy).then_inc(ev_hi, 1)

        def half_lo(dve, b, number, hi, lo, h, n=NC, rows=slice(0, P)):
            dve.wait_ge(ev_hi, number)
            dve.tensor_tensor(lo[rows, :, half(h)], bank[b][rows, 0:n * P].rearrange("p (c n) -> p c n", c=n),
                              hi[rows, :, half(h)].bitcast(F32), ALU.subtract).then_inc(ev_lo, 1)

        block = ctx.enter_context(nc.Block())

        @block.sync
        def _(sp):
            def load(t, src, sizes, first=False):
                for part, k, at, n in ((loaded_a, 0, 0, sizes[0]), (loaded_b, 1, sizes[0], sum(sizes[1:]))):
                    if not first:
                        sp.wait_ge(lo_split[k], t.free(k))
                    sp.dma_start(raw[:, t.slot, OFF[k]:OFF[k] + n], src[:, at:at + n]).then_inc(part[t.slot], 16)

            for h in range(2):
                sp.dma_start(res[:, h, :], x[:, h, :]).then_inc(x_loaded[h], 16)
            sp.dma_start(smalls[:, C_ID:C_MASK], small[:, C_ID:C_MASK]).then_inc(ident_loaded, 16)
            load(Tile(0, T_WQ), wq, X_SIZES, first=True)
            sp.dma_start(smalls[:, C_MASK:C_END], small[:, C_MASK:C_END]).then_inc(small_loaded, 16)
            load(Tile(0, T_WK), wk, X_SIZES, first=True)
            with sp.Fori(0, NG // 2) as j:
                for s in range(2):
                    load(Tile(j, T_CT + s), ctx_t[bass.ds(j * 2 + s, 1)].squeeze(0), X_SIZES)
            load(Tile(0, T_WV), wv, X_SIZES)
            with sp.Fori(0, NG // 2) as j:
                for s in range(2):
                    load(Tile(j, T_CN + s), ctx_n[bass.ds(j * 2 + s, 1)].squeeze(0), X_SIZES)
            load(Tile(0, T_WO), wo, X_SIZES)
            load(Tile(0, T_QKV), w_qkv, Q_SIZES)
            load(Tile(0, T_ROPE), w_rope, X_SIZES)
            with sp.Fori(0, PAIRS // 2) as j:
                for s in range(2):
                    load(Tile(j, T_M + s), w_mla[bass.ds(j * 2 + s, 1)].squeeze(0), M_SIZES)
            for s in range(2):
                load(Tile(0, T_E + s), w_exp[s], E_SIZES)
            with sp.Fori(0, NE // 2 - 1) as j:
                for s in range(2, 4):
                    load(Tile(j, T_E + s), w_exp[bass.ds(j * 2 + s, 1)].squeeze(0), E_SIZES)
            for h in range(2):
                sp.wait_ge(res_done, 4 + 2 * NE - 1 + h)
                sp.dma_start(out[:, h, :], res[:, h, :]).then_inc(stored, 16)
            sp.wait_ge(stored, 32)

        @block.tensor
        def _(pe):
            ident = smalls[:, C_ID:C_ID + P]

            def product(o, a, b, start, stop, told=None):
                ins = pe.matmul(o, a[0], b[0], start=start, stop=False)
                if told is not None:
                    ins.then_inc(told, 1)
                pe.matmul(o, a[0], b[1], start=False, stop=False)
                return pe.matmul(o, a[1], b[0], start=False, stop=stop)

            def ready(t, k):
                pe.wait_ge(lo_split[k], t.split(k))

            def wcols(t, at, n, rows=P):
                return w_hi[0:rows, t.slot, at:at + n], w_lo[0:rows, t.slot, at:at + n]

            def x_chunk(t, c, at=0, n=512):
                return wcols(t, OFF[c // 2] + (c % 2) * 512 + at, n)

            def transpose_half(src, h, ready_sem, count, told=None):
                pe.wait_ge(ready_sem, count)
                for c in range(NC):
                    ins = pe.transpose(bank[h][:, c * P:c * P + P], src[:, h, c * P:c * P + P], ident)
                    if told is not None and c == 0:
                        ins.then_inc(told, 1)
                ins.then_inc(bank_full[h], 1)

            def project_t(t, first_bank, told=None):
                for m in range(NC):
                    b = first_bank + m // 2
                    for c in range(NC):
                        if m == 0 and c % 2 == 0:
                            ready(t, c // 2)
                        ins = product(bank[b][:, (m % 2) * T:(m % 2) * T + T], x_chunk(t, c, m * P, P),
                                      (xt_hi[:, c, :], xt_lo[:, c, :]), c == 0, c == NC - 1,
                                      told if m == c == 0 else None)
                        if m == NC - 1 and c == 1:
                            ins.then_inc(used[0], 1)
                    if m % 2:
                        ins.then_inc(bank_full[b], 1)

            def project_rows(t, a_hi, a_lo, first_bank, width=512, told=None, split=None, midway=(None, None)):
                for h in range(2):
                    if split is not None:
                        pe.wait_ge(ev_lo, split + h)
                    for c in range(NC):
                        if h == 0 and c % 2 == 0:
                            ready(t, c // 2)
                        w = wcols(t, OFF[c // 2] + (c % 2) * width, width)
                        ins = product(bank[first_bank + h][:, 0:width],
                                      (a_hi[:, c, half(h)], a_lo[:, c, half(h)]), w, c == 0, c == NC - 1,
                                      told if h == c == 0 else None)
                        if h == 1 and c == 1:
                            ins.then_inc(used[0], 1)
                        if c == 1 and midway[h] is not None:
                            midway[h]()
                    ins.then_inc(bank_full[first_bank + h], 1)

            pe.wait_ge(ident_loaded, 16)
            for h in range(2):
                transpose_half(xn, h, xn_ready, h + 1)
            pe.wait_ge(ev_lo, V_LN1 + 1)
            project_t(Tile(0, T_WQ), 2)
            project_t(Tile(0, T_WK), 4, told=used[1])
            pe.wait_ge(ev_lo, V_Q + 1)

            def score_group(j, s):
                t = Tile(j, T_CT + s)
                for h in range(2):
                    b = 2 * (s % 2) + h
                    if not isinstance(j, int):
                        pe.wait_ge(s_copied, j * 4 + (2 * s + h - 3))
                    for c in range(NC):
                        if h == 0 and c % 2 == 0:
                            ready(t, c // 2)
                        ins = product(bank[b][:, :], (q_hi[:, c, half(h)], q_lo[:, c, half(h)]),
                                      x_chunk(t, c), c == 0, c == NC - 1,
                                      used[1] if h == c == 0 else None)
                        if h == 1 and c == 1:
                            ins.then_inc(used[0], 1)
                    ins.then_inc(bank_full[b], 1)

            score_group(0, 0)
            score_group(0, 1)
            with pe.Fori(1, NG // 2) as j:
                score_group(j, 0)
                score_group(j, 1)
            for h in range(2):
                pe.wait_ge(s_copied, 2 * (NG - 2) + h + 1)
                for c in range(NC):
                    ins = product(bank[h][:, 0:T], (q_hi[:, c, half(h)], q_lo[:, c, half(h)]),
                                  (k_hi[:, c, :], k_lo[:, c, :]), c == 0, c == NC - 1,
                                  used[1] if h == c == 0 else None)
                ins.then_inc(bank_full[h], 1)
            project_rows(Tile(0, T_WV), xt_hi, xt_lo, 4)

            def transpose_probs(ring, exps, blocks=4, told=None):
                for h in range(2):
                    pe.wait_ge(p_ready, exps + (h + 1))
                    for k in range(blocks):
                        ins = pe.transpose(bank[2 * ring + h][:, k * P:k * P + P],
                                           probs[:, ring, h, k * P:k * P + P], ident)
                        if told is not None and h == k == 0:
                            ins.then_inc(told, 1)
                    ins.then_inc(bank_full[2 * ring + h], 1)

            def times_values(ring, t, number, last=False, midway=None):
                for h in range(2):
                    pe.wait_ge(ev_lo, number + h)
                    for k in range(4):
                        if h == 0 and k % 2 == 0:
                            ready(t, k // 2)
                        ins = product(bank[6 + h][:, :], (pt_hi[:, ring, h, k * P:k * P + P],
                                                          pt_lo[:, ring, h, k * P:k * P + P]),
                                      x_chunk(t, k), False, last and k == 3)
                        if h == 1 and k == 1:
                            ins.then_inc(used[0], 1)
                            if midway is not None:
                                midway()
                    if last:
                        ins.then_inc(bank_full[6 + h], 1)
                if not last:
                    ins.then_inc(used[1], 1)

            transpose_probs(1, 0, blocks=2, told=used[1])
            transpose_probs(0, 2)
            for h in range(2):
                pe.wait_ge(ev_lo, V_PT + h)
                for k in range(2):
                    product(bank[6 + h][:, :], (pt_hi[:, 1, h, k * P:k * P + P], pt_lo[:, 1, h, k * P:k * P + P]),
                            (v_hi[:, k, :], v_lo[:, k, :]), k == 0, False)
            with pe.Fori(0, NG // 2 - 1) as j:
                transpose_probs(1, j * 4 + 4)
                times_values(0, Tile(j, T_CN), j * 4 + (V_PT + 2))
                transpose_probs(0, j * 4 + 6)
                times_values(1, Tile(j, T_CN + 1), j * 4 + (V_PT + 4))
            transpose_probs(1, 2 * NG)
            times_values(0, Tile(0, T_CN + 6), V_PT + 14)
            times_values(1, Tile(0, T_CN + 7), V_PT + 16, last=True,
                         midway=lambda: transpose_half(o_row, 0, o_ready, 1))

            project_rows(Tile(0, T_WO), ot_hi, ot_lo, 4, told=used[1], split=V_OT,
                         midway=(lambda: transpose_half(o_row, 1, o_ready, 2), None))

            def transpose_compressed(h):
                pe.wait_ge(rows_ready, h + 1)
                for c in range(2):
                    ins = pe.transpose(bank[4 + 2 * h][0:QR2, c * P:c * P + P],
                                       qc_row[:, h, c * QR2:c * QR2 + QR2], ident)
                ins.then_inc(bank_full[4 + 2 * h], 1)
                pe.transpose(bank[5 + 2 * h][:, 0:P], kvc_row[:, h, :], ident)
                for d in range(2):
                    ins = pe.transpose(bank[5 + 2 * h][:, (d + 1) * P:(d + 2) * P],
                                       kr_row[:, h, d * P:d * P + P], ident)
                ins.then_inc(bank_full[5 + 2 * h], 1)

            def qkv_half(h, midway=None):
                t = Tile(0, T_QKV)
                pe.wait_ge(ev_lo, V_LN2 + h)
                for c in range(NC):
                    if h == 0 and c % 2 == 0:
                        ready(t, c // 2)
                    ins = product(bank[2 + h][:, 0:384], (xt_hi[:, c, half(h)], xt_lo[:, c, half(h)]),
                                  wcols(t, OFF[c // 2] + (c % 2) * 384, 384), c == 0, c == NC - 1)
                    if h == 1 and c == 1:
                        ins.then_inc(used[0], 1)
                        midway()
                ins.then_inc(bank_full[2 + h], 1)

            transpose_half(xn, 0, xn_ready, 3, told=used[1])
            qkv_half(0)
            transpose_half(xn, 1, xn_ready, 4)
            qkv_half(1, midway=lambda: transpose_compressed(0))

            def rope_queries(h, told=(None, None)):
                t = Tile(0, T_ROPE)
                for g in range(2):
                    if h == 0:
                        ready(t, g)
                    for c in range(2):
                        w = x_chunk(t, 2 * g + c)
                        ins = product(bank[2 * h + g][:, :], (qc_hi[0:QR2, c, half(h)], qc_lo[0:QR2, c, half(h)]),
                                      (w[0][0:QR2], w[1][0:QR2]), c == 0, c == 1, told[g] if c == 0 else None)
                    ins.then_inc(bank_full[2 * h + g], 1)

            pe.wait_ge(ev_lo, V_C)
            rope_queries(0, told=(used[1], None))
            transpose_compressed(1)
            pe.wait_ge(ev_lo, V_C + 3)
            rope_queries(1, told=(None, used[0]))
            pe.wait_ge(consts_rounded, 3)

            def project_pair(t, out_split=None, told=None):
                ready(t, 0)
                for hd in range(2):
                    for c in range(2):
                        ins = product(bank[4][:, hd * T:hd * T + T], wcols(t, c * 256 + hd * P, P, QR2),
                                      (qc_hi[0:QR2, c, :], qc_lo[0:QR2, c, :]), c == 0, c == 1,
                                      told if hd == c == 0 else None)
                ins.then_inc(bank_full[4], 1)
                if out_split is not None:
                    pe.wait_ge(ev_lo, out_split)
                for hd in range(2):
                    ins = product(bank[5][:, hd * T:hd * T + T], wcols(t, 512 + hd * P, P),
                                  (kvc_hi, kvc_lo), True, True)
                ins.then_inc(bank_full[5], 1)
                for h in range(2):
                    ins = product(bank[6][:, h * T:h * T + T], (kvc_hi[:, half(h)], kvc_lo[:, half(h)]),
                                  wcols(t, 768, T), True, True)
                ins.then_inc(bank_full[6], 1)

            def rope_transpose(rope, told=None):
                pe.wait_ge(rope_ready, rope)
                for h in range(2):
                    ins = pe.transpose(bank[7][:, half(h)], q_rope[:, h, :], ident)
                    if told is not None and h == 0:
                        ins.then_inc(told, 1)
                ins.then_inc(bank_full[7], 1)

            def score_pair():
                for hd in range(2):
                    for h, at, n in ((1, 0, T), (0, T, P)):
                        o = bank[2 + hd][:, at:at + n]
                        product(o, (mq_hi[:, hd, half(h)], mq_lo[:, hd, half(h)]),
                                (mk_hi[:, hd, 0:n], mk_lo[:, hd, 0:n]), True, False)
                        product(o, (qr_hi[:, half(h)], qr_lo[:, half(h)]),
                                (kr_hi[:, hd, 0:n], kr_lo[:, hd, 0:n]), False, False)
                        ins = pe.matmul(bank[2 + hd][:, at + n - P:at + n], ident_r[:, :], mask_r[:, :],
                                        start=False, stop=True)
                    ins.then_inc(bank_full[2 + hd], 1)

            def transpose_pair(normed, told=None):
                for hd in range(2):
                    pe.wait_ge(m_norm, normed + 2 * (hd + 1))
                    for dst, src in ((0, T), (P, 0), (T, P)):
                        ins = pe.transpose(bank[2 + hd][:, dst:dst + P], pair_probs[:, hd, src:src + P], ident)
                        if told is not None and hd == dst == 0:
                            ins.then_inc(told, 1)
                    ins.then_inc(bank_full[2 + hd], 1)

            def values_pair(ring):
                for hd in range(2):
                    a = slice(hd * VDIM, hd * VDIM + VDIM)
                    product(bank[5][:, hd * T:hd * T + T], (mv_hi[:, ring, 0, a], mv_lo[:, ring, 0, a]),
                            (mpt_hi[:, hd, 0:T], mpt_lo[:, hd, 0:T]), True, False)
                    ins = product(bank[5][:, hd * T + P:hd * T + T], (mv_hi[:, ring, 1, a], mv_lo[:, ring, 1, a]),
                                  (mpt_hi[:, hd, T:T + P], mpt_lo[:, hd, T:T + P]), False, True)
                ins.then_inc(bank_full[5], 1)

            def out_pair(t, first=False, last=False, halves=(0, 1)):
                ready(t, 1)
                for h in halves:
                    for hd in range(2):
                        ins = product(bank[h][:, :], (mo_hi[:, hd, half(h)], mo_lo[:, hd, half(h)]),
                                      wcols(t, OFF[1] + hd * 512, 512), first and hd == 0, last and hd == 1)
                    if last:
                        ins.then_inc(bank_full[h], 1)
                if not last and 1 in halves:
                    ins.then_inc(used[1], 1)

            def pair_step(j, s, first_out=False):
                n = j * (2 * PER_PAIR) + s * PER_PAIR
                start = isinstance(j, int) and s == 0
                last_out = Tile(j, T_M + s - 1)
                pe.wait_ge(ev_lo, V_MLA - 2 if start else n + (V_MLA - 3))
                score_pair()
                project_pair(Tile(j, T_M + s + 1), n + (V_MLA - 1))
                if not start:
                    out_pair(last_out, first=first_out, halves=(0,))
                transpose_pair(j * 8 + 4 * s, told=used[0])
                rope_transpose(j * 2 + (s + 2))
                if not start:
                    out_pair(last_out, first=first_out, halves=(1,))
                pe.wait_ge(ev_lo, n + (V_MLA + 3))
                values_pair(s % 2)

            project_pair(Tile(0, T_M), told=used[1])
            rope_transpose(1, told=used[0])
            pe.wait_ge(rope_part, 12)
            pair_step(0, 0)
            pair_step(0, 1, first_out=True)
            with pe.Fori(0, 2) as j:
                pair_step(j, 2)
                pair_step(j, 3)
            pair_step(0, 6)
            n = V_MLA + (PAIRS - 1) * PER_PAIR
            pe.wait_ge(ev_lo, n - 3)
            score_pair()
            pe.wait_ge(ev_lo, n - 1)
            out_pair(Tile(0, T_M + PAIRS - 2))
            transpose_pair(4 * (PAIRS - 1))
            pe.wait_ge(ev_lo, n + 1)
            ring = (PAIRS - 1) % 2
            for h in range(2):
                for hd in range(2):
                    a = slice(hd * VDIM, hd * VDIM + VDIM)
                    for key in range(h + 1):
                        p = slice((key + h) * P, (key + h + 1) * P)
                        ins = product(bank[4 + h][:, hd * P:hd * P + P],
                                      (mv_hi[:, ring, key, a], mv_lo[:, ring, key, a]),
                                      (mpt_hi[:, hd, p], mpt_lo[:, hd, p]), key == 0, key == h)
                ins.then_inc(bank_full[4 + h], 1)
            for h in range(2):
                pe.wait_ge(ev_lo, n + 2 + h)
                out_pair(Tile(0, T_M + PAIRS - 1), last=True, halves=(h,))

            for h in range(2):
                transpose_half(xn, h, xn_ready, 5 + h)
            pe.wait_ge(ev_lo, V_LN3 + 1)

            def gate_up(j, s, told=None, midway=None):
                t = Tile(j, T_E + s)
                b = 2 * (s % 2)
                for u in range(2):
                    for m in range(2):
                        for c in range(NC):
                            k = 0 if u == 0 or c == 0 else 2
                            if m == 0 and (c == 0 and u == 0 or c == 1 and u == 1):
                                ready(t, k)
                            at = (u * NC + c) * I if k == 0 else OFF[2] + (c - 1) * I
                            ins = product(bank[b + u][:, m * T:m * T + T], wcols(t, at + m * P, P),
                                          (xt_hi[:, c, :], xt_lo[:, c, :]), c == 0, c == NC - 1,
                                          told if u == m == c == 0 else None)
                            if u == m == 1 and c == 0:
                                ins.then_inc(used[0], 1)
                        if midway is not None and u == m == 0:
                            midway()
                    ins.then_inc(bank_full[b + u], 1)

            def down(j, s, told=None):
                t = Tile(j, T_E + s)
                pe.wait_ge(ev_lo, j * 2 + (V_H + s))
                ready(t, 1)
                for h in range(2):
                    b = 4 + 2 * (s % 2) + h
                    pe.wait_ge(res_done, j * 4 + (2 * s + h + 1))
                    for m in range(2):
                        a = slice(m * T + h * P, m * T + h * P + P)
                        ins = product(bank[b][:, :], (h_hi[:, s % 2, a], h_lo[:, s % 2, a]),
                                      wcols(t, OFF[1] + m * 512, 512), m == 0, m == 1,
                                      told if h == m == 0 else None)
                    ins.then_inc(bank_full[b], 1)

            pe.wait_ge(rw_split, 1)
            for c in range(NC):
                ins = product(bank[4][0:E, 0:T], (rw_hi[:, c, :], rw_lo[:, c, :]),
                              (xt_hi[:, c, :], xt_lo[:, c, :]), c == 0, c == NC - 1,
                              used[1] if c == 0 else None)
            ins.then_inc(bank_full[4], 1)

            def transpose_scores():
                pe.wait_ge(sigmoid_ready, 1)
                for h in range(2):
                    ins = pe.transpose(bank[6][:, h * E:h * E + E], score_t[:, half(h)], ident[0:E, 0:E])
                ins.then_inc(bank_full[6], 1)

            gate_up(0, 0, midway=transpose_scores)
            gate_up(0, 1, told=used[2])
            down(0, 0, told=used[2])
            gate_up(0, 2, told=used[1])
            pe.wait_ge(score_taken, 1)
            down(0, 1, told=used[2])
            with pe.Fori(1, NE // 2 - 1) as j:
                gate_up(j, 1, told=used[1])
                down(j, 0, told=used[2])
                gate_up(j, 2, told=used[1])
                down(j, 1, told=used[2])
            gate_up(0, NE - 1, told=used[1])
            down(0, NE - 2, told=used[2])
            down(0, NE - 1)

        @block.scalar
        def _(act):
            split_hi(act, Tile(0, T_WQ), 0, X_SIZES, first=True)
            for h in range(2):
                half_hi(act, h, F01["ln1"], xt_hi, h)
            split_hi(act, Tile(0, T_WQ), 1, X_SIZES, first=True)
            for k in range(2):
                split_hi(act, Tile(0, T_WK), k, X_SIZES, first=True)
            for b in range(2):
                out_hi(act, 2 + b, F23["q"], flat(q_hi[:, 2 * b:2 * b + 2, :]), 512)
            for k in range(2):
                split_hi(act, Tile(0, T_CT), k, X_SIZES)
            for b in range(2):
                out_hi(act, 4 + b, F45["k"], flat(k_hi[:, 2 * b:2 * b + 2, :]), 512)
            act.wait_ge(ident_loaded, 16)
            act.copy(ident_r[:, :], smalls[:, C_ID:C_ID + P]).then_inc(consts_rounded, 1)
            act.wait_ge(small_loaded, 16)
            act.copy(mask_r[:, :], smalls[:, C_MASK:C_MASK + P]).then_inc(consts_rounded, 1)
            act.copy(flat(rw_hi[:, :, :]), smalls[:, C_RW:C_RW + NC * E]).then_inc(consts_rounded, 1)

            with act.Fori(0, NG // 2) as j:
                for s in range(2):
                    for k in range(2):
                        split_hi(act, Tile(j, T_CT + s + 1), k, X_SIZES)
                    for h in range(2):
                        b = 2 * s + h
                        act.wait_ge(bank_full[b], j + (F01["s_even"] if s == 0 else F23["s_odd"]))
                        act.copy(scores[:, h, bass.ds(j * 1024 + s * 512, 512)], bank[b][:, :]) \
                           .then_inc(s_copied, 1)
            for h in range(2):
                act.wait_ge(bank_full[h], F01["s_new"])
                act.copy(scores[:, h, CTX:KEYS], bank[h][:, 0:T]).then_inc(s_copied, 1)
            for k in range(2):
                split_hi(act, Tile(0, T_CN), k, X_SIZES)

            def exps(ring, at, n, sum_at):
                for h in range(2):
                    act.activation(probs[:, ring, h, 0:n], scores[:, h, at], ACT.Exp, bias=exp_bias[:, h:h + 1],
                                   scale=XSCALE, accum_out=sums[:, h, sum_at]).then_inc(p_ready, 1)

            def probs_hi(ring, full, n=512):
                for h in range(2):
                    out_hi(act, 2 * ring + h, full, pt_hi[:, ring, h, 0:n], n)

            act.wait_ge(bias_ready, 1)
            exps(1, slice(CTX, KEYS), T, slice(NG, NG + 1))
            exps(0, slice(0, 512), 512, slice(0, 1))
            for b in range(2):
                out_hi(act, 4 + b, F45["v"], v_hi[:, b, :], 512)
            probs_hi(1, F23["pt_new"], T)
            exps(1, slice(512, 1024), 512, slice(1, 2))
            probs_hi(0, F01["pt_even"])
            with act.Fori(0, NG // 2 - 1) as j:
                for s in range(2):
                    exps(s, bass.ds(j * 1024 + (s + 2) * 512, 512), 512, bass.ds(j * 2 + (s + 2), 1))
                    probs_hi(1 - s, j + (F23["pt_odd"] if s == 0 else F01["pt_even"] + 1))
                    for k in range(2):
                        split_hi(act, Tile(j, T_CN + s + 1), k, X_SIZES)
            probs_hi(1, F23["pt_odd"] + 3)
            for s in (NG - 1, NG):
                for k in range(2):
                    split_hi(act, Tile(0, T_CN + s), k, X_SIZES)

            half_hi(act, 0, F01["ot"], ot_hi, 0)
            for k in range(2):
                split_hi(act, Tile(0, T_QKV), k, Q_SIZES)
            half_hi(act, 1, F01["ot"], ot_hi, 1)
            split_hi(act, Tile(0, T_ROPE), 0, X_SIZES)
            half_hi(act, 0, F01["ln2"], xt_hi, 0)
            split_hi(act, Tile(0, T_ROPE), 1, X_SIZES)
            half_hi(act, 1, F01["ln2"], xt_hi, 1)
            for h in range(2):
                full = (F45 if h == 0 else F67)["c"]
                half_hi(act, 4 + 2 * h, full, qc_hi, h, n=2, rows=slice(0, QR2))
                half_hi(act, 5 + 2 * h, full, ckr_hi, h, n=3)
                if h == 0:
                    split_hi(act, Tile(0, T_M), 0, M_SIZES)
            split_hi(act, Tile(0, T_M), 1, M_SIZES)
            split_hi(act, Tile(0, T_M + 1), 0, M_SIZES)

            def pair_qk_hi(j, s):
                out_hi(act, 4, j * 2 + (F4["q"] + s), flat(mq_hi[:, :, :]), 512)
                out_hi(act, 5, F5["k0"] if isinstance(j, int) and s == 0 else j * 4 + (F5["k"] + 2 * s),
                       flat(mk_hi[:, :, :]), 512)

            def pair_v_hi(j, s):
                out_hi(act, 6, j * 2 + (F6["v"] + s), flat(mv_hi[:, s % 2, :, :]), 512)

            def pair_exps(j, s):
                act.wait_ge(m_bias_ready, j * 2 + (s + 1))
                for hd in range(2):
                    for late, at, n in ((0, 0, T), (1, T, P)):
                        k = 2 * hd + late
                        act.activation(pair_probs[:, hd, at:at + n], bank[2 + hd][:, at:at + n], ACT.Exp,
                                       bias=m_bias[:, k:k + 1], scale=MSCALE, accum_out=m_sum[:, k:k + 1]) \
                           .then_inc(m_exp, 1)

            def pair_probs_hi(j, s):
                for hd in range(2):
                    out_hi(act, 2 + hd, j * 4 + (F23["pt"] + 2 * s), mpt_hi[:, hd, :], 384)

            def rope_hi(j, s):
                out_hi(act, 7, j * 2 + (F7["rope_t"] + s), qr_hi, T)

            def pair_step(j, s, sizes=M_SIZES):
                split_hi(act, Tile(j, T_M + s + 2), 0, sizes)
                pair_exps(j, s)
                pair_qk_hi(j, s + 1)
                pair_probs_hi(j, s)
                rope_hi(j, s + 1)
                pair_v_hi(j, s + 1)
                out_hi(act, 5, j * 4 + (F5["o"] + 2 * s), flat(mo_hi[:, :, :]), 512)
                split_hi(act, Tile(j, T_M + s + 1), 1, M_SIZES)

            pair_qk_hi(0, 0)
            rope_hi(0, 0)
            pair_v_hi(0, 0)
            pair_step(0, 0)
            with act.Fori(0, (PAIRS - 4) // 2) as j:
                pair_step(j, 1)
                pair_step(j, 2)
            pair_step(0, PAIRS - 3)
            pair_step(0, PAIRS - 2, E_SIZES)
            pair_exps(0, PAIRS - 1)
            pair_probs_hi(0, PAIRS - 1)
            split_hi(act, Tile(0, T_E), 2, E_SIZES, first=True)
            half_hi(act, 4, F4["o_last"], mo_hi, 0, n=2)
            half_hi(act, 5, F5["o_last"], mo_hi, 1, n=2)
            split_hi(act, Tile(0, T_E), 1, E_SIZES)
            split_hi(act, Tile(0, T_E + 1), 0, E_SIZES)
            split_hi(act, Tile(0, T_E + 1), 2, E_SIZES, first=True)
            for h in range(2):
                half_hi(act, h, F01["ln3"], xt_hi, h)
            act.wait_ge(bank_full[4], F4["router"])
            act.activation(score_t, bank[4][0:E, 0:T], ACT.Sigmoid).then_inc(sigmoid_ready, 1)

            def expert_step(j, s, ahead=2):
                act.wait_ge(bank_full[2 * (s % 2)], j + ((F01 if s % 2 == 0 else F23)["moe"] + s // 2))
                act.activation(gate_act[:, s % 2, :], bank[2 * (s % 2)][:, :], ACT.Silu).then_inc(silu_ready, 1)
                if ahead >= 1:
                    split_hi(act, Tile(j, T_E + s + 1), 1, E_SIZES)
                act.wait_ge(h_ready, j * 2 + (s + 1))
                act.copy(h_hi[:, s % 2, :], h_row[:, s % 2, :]).then_inc(ev_hi, 1)
                if ahead >= 2:
                    split_hi(act, Tile(j, T_E + s + 2), 0, E_SIZES)
                    split_hi(act, Tile(j, T_E + s + 2), 2, E_SIZES)

            with act.Fori(0, NE // 2 - 1) as j:
                expert_step(j, 0)
                expert_step(j, 1)
            expert_step(0, NE - 2, ahead=1)
            expert_step(0, NE - 1, ahead=0)

        @block.vector
        def _(dve):
            step = [0]

            def then(ins):
                step[0] += 1
                ins.then_inc(vec, 1)
                dve.wait_ge(vec, step[0])

            def norm_stats(h):
                then(dve.bn_stats(stat[:, h, :], res[:, h, :]))
                then(dve.bn_aggr(mean_var[:, h, :], stat[:, h, :]))
                dve.tensor_scalar(var_eps[:, h:h + 1], mean_var[:, h, 1:2], LN_EPS, None, ALU.add) \
                   .then_inc(var_ready, 1)

            def normalize(h, roots):
                dve.wait_ge(rstd_ready, roots)
                dve.tensor_scalar(xn[:, h, :], res[:, h, :], mean_var[:, h, 0:1], rstd[:, h:h + 1],
                                  ALU.subtract, ALU.mult).then_inc(xn_ready, 1)

            def add_to_residual(b, full, h, number):
                dve.wait_ge(bank_full[b + h], full)
                dve.tensor_tensor(res[:, h, :], bank[b + h][:, :], res[:, h, :], ALU.add) \
                   .then_inc(res_done, 1)
                dve.wait_ge(res_done, number)

            def split_pair_lo(number, b, hi, lo):
                for k in range(2):
                    out_lo(dve, b + k, number + k, flat(hi[:, 2 * k:2 * k + 2, :]),
                           flat(lo[:, 2 * k:2 * k + 2, :]), 512)

            for h in range(2):
                dve.wait_ge(x_loaded[h], 16)
                norm_stats(h)
            for h in range(2):
                normalize(h, h + 1)
            split_lo(dve, Tile(0, T_WQ), 0, X_SIZES)
            for h in range(2):
                half_lo(dve, h, V_LN1 + h, xt_hi, xt_lo, h)
            split_lo(dve, Tile(0, T_WQ), 1, X_SIZES)
            split_lo(dve, Tile(0, T_WK), 0, X_SIZES)
            split_pair_lo(V_Q, 2, q_hi, q_lo)
            split_lo(dve, Tile(0, T_CT), 0, X_SIZES)
            split_pair_lo(V_K, 4, k_hi, k_lo)
            dve.wait_ge(consts_rounded, 3)
            dve.tensor_tensor(flat(rw_lo[:, :, :]), smalls[:, C_RW:C_RW + NC * E],
                              flat(rw_hi[:, :, :]).bitcast(F32), ALU.subtract).then_inc(rw_split, 1)
            with dve.Fori(0, NG // 2) as j:
                for s in range(2):
                    split_lo(dve, Tile(j, T_CT + s + 1), 0, X_SIZES)
                    for h in range(2):
                        dve.wait_ge(s_copied, j * 4 + (2 * s + h + 1))
                        dve.tensor_reduce(row_max[:, h, bass.ds(j * 2 + s, 1)],
                                          scores[:, h, bass.ds(j * 1024 + s * 512, 512)], AX, ALU.max) \
                           .then_inc(s_max, 1)
            for h in range(2):
                dve.wait_ge(s_copied, 2 * NG + h + 1)
                dve.tensor_reduce(row_max[:, h, NG:NG + 1], scores[:, h, CTX:KEYS], AX, ALU.max) \
                   .then_inc(s_max, 1)
            dve.wait_ge(s_max, 2 * NG + 2)
            then(dve.tensor_reduce(neg_max[:, :], row_max[:, :, :], AX, ALU.max, negate=True))
            dve.tensor_scalar(exp_bias[:, :], neg_max[:, :], XSCALE, None, ALU.mult).then_inc(bias_ready, 1)
            split_lo(dve, Tile(0, T_CN), 0, X_SIZES)
            for b in range(2):
                out_lo(dve, 4 + b, V_V + b, v_hi[:, b, :], v_lo[:, b, :], 512)

            def probs_lo(ring, number, n=512):
                for h in range(2):
                    out_lo(dve, 2 * ring + h, number + h, pt_hi[:, ring, h, 0:n], pt_lo[:, ring, h, 0:n], n)

            probs_lo(1, V_PT, T)
            probs_lo(0, V_PT + 2)
            with dve.Fori(0, NG // 2 - 1) as j:
                for s in range(2):
                    probs_lo(1 - s, j * 4 + (V_PT + 4 + 2 * s))
                    split_lo(dve, Tile(j, T_CN + s + 1), 0, X_SIZES)
            probs_lo(1, V_PT + 16)
            for s in (NG - 1, NG):
                split_lo(dve, Tile(0, T_CN + s), 0, X_SIZES)
            dve.wait_ge(p_ready, 2 * (NG + 1))
            then(dve.tensor_reduce(row_sum[:, :], sums[:, :, :], AX, ALU.add))
            then(dve.reciprocal(row_inv[:, :], row_sum[:, :]))
            dve.memset(kr_row[:, :, :], 0.0).then_inc(kr_zeroed, 1)

            def normalize_output(h):
                dve.wait_ge(bank_full[6 + h], F67["pv"])
                dve.tensor_scalar(o_row[:, h, :], bank[6 + h][:, :], row_inv[:, h:h + 1], None, ALU.mult) \
                   .then_inc(o_ready, 1)

            def mean_squares(h):
                dve.wait_ge(bank_full[2 + h], F23["qkv"])
                then(dve.tensor_copy(qkv_row[:, h, :], bank[2 + h][:, 0:Q_RANK + KV_RANK]))
                for at, n, k in ((0, Q_RANK, 0), (Q_RANK, KV_RANK, 1)):
                    v = qkv_row[:, h, at:at + n]
                    ins = dve.tensor_tensor_reduce(squares[:, 0:n], v, v, 1.0 / n, RMS_EPS, ALU.mult, ALU.add,
                                                   var_eps[:, 2 + 2 * h + k:3 + 2 * h + k])
                    if k == 0:
                        then(ins)
                ins.then_inc(var_ready, 1)

            def rope_keys(h):
                raw_k = bank[2 + h][:, Q_RANK + KV_RANK:384]
                cos = smalls[:, C_COS + h * ROPE:C_COS + (h + 1) * ROPE]
                sin = smalls[:, C_SIN + h * ROPE:C_SIN + (h + 1) * ROPE]
                dve.tensor_tensor(kr_cos, raw_k, cos, ALU.mult).then_inc(kr_part, 1)
                dve.tensor_tensor(kr_sin[:, 0:R2], raw_k[:, R2:ROPE], sin[:, 0:R2], ALU.mult).then_inc(kr_part, 1)
                dve.tensor_tensor(kr_sin[:, R2:ROPE], raw_k[:, 0:R2], sin[:, R2:ROPE], ALU.mult) \
                   .then_inc(kr_part, 1)
                dve.wait_ge(kr_part, 3 * h + 3)
                for at in (0, 3 * ROPE):
                    dve.tensor_tensor(kr_row[:, h, at:at + ROPE], kr_cos, kr_sin, ALU.add).then_inc(kr_done, 1)

            def compressed_rows(h, roots):
                dve.wait_ge(rstd_ready, roots)
                for out_row, at, n, gain, k in ((qc_row, 0, Q_RANK, C_GQ, 0), (kvc_row, Q_RANK, KV_RANK, C_GKV, 1)):
                    ins = dve.scalar_tensor_tensor(
                        out=out_row[:, h, :], in0=qkv_row[:, h, at:at + n],
                        scalar=rstd[:, 2 + 2 * h + k:3 + 2 * h + k], in1=smalls[:, gain:gain + n],
                        op0=ALU.mult, op1=ALU.mult)
                    if k == 0:
                        then(ins)
                dve.wait_ge(kr_done, 2 * h + 2)
                ins.then_inc(rows_ready, 1)

            def compressed_q_lo(h):
                half_lo(dve, 4 + 2 * h, V_C + 2 * h, qc_hi, qc_lo, h, n=2, rows=slice(0, QR2))

            def compressed_kv_lo(h):
                half_lo(dve, 5 + 2 * h, V_C + 2 * h + 1, ckr_hi, ckr_lo, h, n=3)

            def rope_products(h, g):
                b = 2 * h + g
                dve.wait_ge(bank_full[b], (F01 if b < 2 else F23)["rope"])
                q, to_cos, to_sin = (v.rearrange("p (g n) -> p g n", n=ROPE)
                                     for v in (bank[b][:, :], q_cos[:, h, g * 512:g * 512 + 512],
                                               q_sin[:, h, g * 512:g * 512 + 512]))
                cos, sin = (smalls[:, at + h * ROPE:at + (h + 1) * ROPE].unsqueeze(1).broadcast_to([P, 8, ROPE])
                            for at in (C_COS, C_SIN))
                dve.tensor_tensor(to_cos, q, cos, ALU.mult).then_inc(rope_part, 1)
                dve.tensor_tensor(to_sin[:, :, 0:R2], q[:, :, R2:ROPE], sin[:, :, 0:R2], ALU.mult) \
                   .then_inc(rope_part, 1)
                dve.tensor_tensor(to_sin[:, :, R2:ROPE], q[:, :, 0:R2], sin[:, :, R2:ROPE], ALU.mult) \
                   .then_inc(rope_part, 1)

            R2 = ROPE // 2
            normalize_output(0)
            half_lo(dve, 0, V_OT, ot_hi, ot_lo, 0)
            normalize_output(1)
            split_lo(dve, Tile(0, T_QKV), 0, Q_SIZES)
            half_lo(dve, 1, V_OT + 1, ot_hi, ot_lo, 1)
            add_to_residual(4, F45["wo"], 0, 1)
            norm_stats(0)
            normalize(0, 3)
            add_to_residual(4, F45["wo"], 1, 2)
            half_lo(dve, 0, V_LN2, xt_hi, xt_lo, 0)
            norm_stats(1)
            normalize(1, 4)
            mean_squares(0)
            half_lo(dve, 1, V_LN2 + 1, xt_hi, xt_lo, 1)
            dve.wait_ge(kr_zeroed, 1)
            rope_keys(0)
            compressed_rows(0, 5)
            compressed_q_lo(0)
            mean_squares(1)
            rope_keys(1)
            compressed_kv_lo(0)
            compressed_rows(1, 6)
            rope_products(0, 0)
            compressed_q_lo(1)
            compressed_kv_lo(1)
            rope_products(0, 1)
            rope_products(1, 0)
            rope_products(1, 1)

            def pair_bias(j, s):
                for hd in range(2):
                    dve.wait_ge(bank_full[2 + hd], j * 4 + (F23["scores"] + 2 * s))
                    for k, at, n in ((2 * hd, 0, T), (2 * hd + 1, T, P)):
                        dve.tensor_reduce(m_neg[:, k:k + 1], bank[2 + hd][:, at:at + n], AX, ALU.max,
                                          negate=True).then_inc(m_neg_ready, 1)
                dve.wait_ge(m_neg_ready, j * 8 + (4 * s + 4))
                dve.tensor_scalar(m_bias[:, :], m_neg[:, :], MSCALE, None, ALU.mult).then_inc(m_bias_ready, 1)

            def pair_normalize(j, s):
                dve.wait_ge(m_exp, j * 8 + (4 * s + 4))
                dve.reciprocal(m_inv[:, :], m_sum[:, :]).then_inc(m_inv_ready, 1)
                dve.wait_ge(m_inv_ready, j * 2 + (s + 1))
                for hd in range(2):
                    for k, at, n in ((2 * hd, 0, T), (2 * hd + 1, T, P)):
                        v = pair_probs[:, hd, at:at + n]
                        dve.tensor_scalar(v, v, m_inv[:, k:k + 1], None, ALU.mult).then_inc(m_norm, 1)

            def pair_qk_lo(n):
                out_lo(dve, 4, n, flat(mq_hi[:, :, :]), flat(mq_lo[:, :, :]), 512)
                out_lo(dve, 5, n + 1, flat(mk_hi[:, :, :]), flat(mk_lo[:, :, :]), 512)

            def pair_rope_v_lo(n, s):
                out_lo(dve, 7, n, qr_hi, qr_lo, T)
                out_lo(dve, 6, n + 1, flat(mv_hi[:, s % 2, :, :]), flat(mv_lo[:, s % 2, :, :]), 512)

            def pair_probs_lo(n):
                for hd in range(2):
                    out_lo(dve, 2 + hd, n + hd, mpt_hi[:, hd, :], mpt_lo[:, hd, :], 384)

            def pair_step(j, s):
                n = j * (2 * PER_PAIR) + (V_MLA + s * PER_PAIR)
                pair_bias(j, s)
                pair_normalize(j, s)
                pair_qk_lo(n)
                pair_probs_lo(n + 2)
                pair_rope_v_lo(n + 4, s + 1)
                out_lo(dve, 5, n + 6, flat(mo_hi[:, :, :]), flat(mo_lo[:, :, :]), 512)

            pair_qk_lo(V_M0)
            pair_rope_v_lo(V_M0 + 2, 0)
            pair_step(0, 0)
            with dve.Fori(0, (PAIRS - 2) // 2) as j:
                pair_step(j, 1)
                pair_step(j, 2)
            pair_bias(0, PAIRS - 1)
            pair_normalize(0, PAIRS - 1)
            n = V_MLA + (PAIRS - 1) * PER_PAIR
            pair_probs_lo(n)
            for h in range(2):
                half_lo(dve, 4 + h, n + 2 + h, mo_hi, mo_lo, h, n=2)
            split_lo(dve, Tile(0, T_E), 2, E_SIZES)
            for h in range(2):
                add_to_residual(0, F01["y"], h, 3 + h)
                norm_stats(h)
            for h in range(2):
                normalize(h, 7 + h)
            for h in range(2):
                half_lo(dve, h, V_LN3 + h, xt_hi, xt_lo, h)
            split_lo(dve, Tile(0, T_E), 1, E_SIZES, handed_over=True)
            split_lo(dve, Tile(0, T_E + 1), 2, E_SIZES)

            score = route(0, 64)
            choice, big, small_, g_top, g_low, g_two = (route(64 + 64 * k, 64) for k in range(6))
            beats, ties = route(448, 128), route(576, 128)
            rank, chosen_g = route(704, 16), route(720, 16)
            masked, replaced = route(736, 64), route(800, 64)
            top8, picked = route(864, 16), route(880, 64)
            total, scaled = route(944, 2), route(946, 2)

            def pairs_of(v):
                g = v.rearrange("p (g n) -> p g n", n=PER)
                return g[:, :, 0:2], g[:, :, 2:4]

            def by2(v):
                return v[:, 0:32].rearrange("p (g n) -> p g n", n=2)

            dve.wait_ge(bank_full[6], F6["score"])
            dve.tensor_copy(score, bank[6][:, 0:2 * E]).then_inc(score_taken, 1)
            dve.wait_ge(score_taken, 1)
            then(dve.tensor_tensor(choice, score, smalls[:, C_BIAS:C_BIAS + 64], ALU.add))
            a, b = pairs_of(choice)
            then(dve.tensor_tensor(by2(big), a, b, ALU.max))
            then(dve.tensor_tensor(by2(small_), a, b, ALU.min))
            big2, small2 = by2(big), by2(small_)
            then(dve.tensor_tensor(g_top[:, 0:16], big2[:, :, 0], big2[:, :, 1], ALU.max))
            then(dve.tensor_tensor(g_low[:, 0:16], big2[:, :, 0], big2[:, :, 1], ALU.min))
            then(dve.tensor_tensor(g_two[:, 0:16], small2[:, :, 0], small2[:, :, 1], ALU.max))
            then(dve.tensor_tensor(g_two[:, 16:32], g_low[:, 0:16], g_two[:, 0:16], ALU.max))
            then(dve.tensor_tensor(g_two[:, 32:48], g_top[:, 0:16], g_two[:, 16:32], ALU.add))
            by_half = g_two[:, 32:48].rearrange("p (h g) -> p h g", h=2)
            cube = [P, 2, GROUPS, GROUPS]
            other = by_half.unsqueeze(2).broadcast_to(cube)
            own = by_half.unsqueeze(3).broadcast_to(cube)

            def cubed(v):
                return v.rearrange("p (h i k) -> p h i k", h=2, i=GROUPS)

            then(dve.tensor_tensor(cubed(beats), other, own, ALU.is_gt))
            then(dve.tensor_tensor(cubed(ties), other, own, ALU.is_equal))
            then(dve.tensor_tensor(ties, ties, smalls[:, C_TIE:C_TIE + 128], ALU.mult))
            then(dve.tensor_tensor(beats, beats, ties, ALU.add))
            then(dve.tensor_reduce(rank, beats.rearrange("p (g k) -> p g k", k=GROUPS), AX, ALU.add))
            then(dve.tensor_scalar(chosen_g, rank, float(TOP_GROUPS), None, ALU.is_lt))
            then(dve.tensor_tensor(masked.rearrange("p (g n) -> p g n", n=PER),
                                   choice.rearrange("p (g n) -> p g n", n=PER),
                                   chosen_g.unsqueeze(2).broadcast_to([P, 2 * GROUPS, PER]), ALU.mult))
            then(dve.tensor_scalar(masked, masked, 0.0, None, ALU.add))
            for h in range(2):
                m = masked[:, h * E:h * E + E]
                then(dve.max(top8[:, h * TOP:h * TOP + TOP], m))
                then(dve.match_replace(replaced[:, h * E:h * E + E], top8[:, h * TOP:h * TOP + TOP], m, TAKEN))
            then(dve.tensor_tensor(picked, replaced, masked, ALU.not_equal))
            then(dve.tensor_tensor(picked, picked, score, ALU.mult))
            then(dve.tensor_reduce(total, picked.rearrange("p (h n) -> p h n", h=2), AX, ALU.add))
            then(dve.reciprocal(scaled, total))
            then(dve.memset(weights[:, :, 0:SHARED], 1.0))
            for h in range(2):
                then(dve.tensor_scalar(weights[:, h, SHARED:NE], picked[:, h * E:h * E + E], scaled[:, h:h + 1],
                                       ROUTED_SCALE, ALU.mult, ALU.mult))

            def expert_hidden(j, s):
                dve.wait_ge(silu_ready, j * 2 + (s + 1))
                up = 2 * (s % 2) + 1
                dve.wait_ge(bank_full[up], j + ((F01 if s % 2 == 0 else F23)["moe"] + s // 2))
                dve.tensor_tensor(h_row[:, s % 2, :], bank[up][:, :], gate_act[:, s % 2, :], ALU.mult) \
                   .then_inc(h_ready, 1)
                dve.wait_ge(ev_hi, j * 2 + (V_H + s))
                dve.tensor_tensor(h_lo[:, s % 2, :], h_row[:, s % 2, :], h_hi[:, s % 2, :].bitcast(F32),
                                  ALU.subtract).then_inc(ev_lo, 1)

            def expert_add(j, s):
                for h in range(2):
                    b = 4 + 2 * (s % 2) + h
                    first = {4: F4, 5: F5, 6: F6, 7: F7}[b]["moe"]
                    dve.wait_ge(bank_full[b], j + (first + s // 2))
                    dve.wait_ge(res_done, j * 4 + (3 + 2 * s + h))
                    w = weights[:, h, bass.ds(j * 2 + s, 1)]
                    dve.scalar_tensor_tensor(out=res[:, h, :], in0=bank[b][:, :], scalar=w, in1=res[:, h, :],
                                             op0=ALU.mult, op1=ALU.add).then_inc(res_done, 1)

            with dve.Fori(0, NE // 2 - 1) as j:
                for s in range(2):
                    expert_hidden(j, s)
                    split_lo(dve, Tile(j, T_E + s + 1), 1, E_SIZES)
                    split_lo(dve, Tile(j, T_E + s + 2), 2, E_SIZES)
                    expert_add(j, s)
            expert_hidden(0, NE - 2)
            split_lo(dve, Tile(0, T_E + NE - 1), 1, E_SIZES)
            expert_hidden(0, NE - 1)
            expert_add(0, NE - 2)
            expert_add(0, NE - 1)

        @block.gpsimd
        def _(pool):
            def root(n, at, cols):
                pool.wait_ge(var_ready, n)
                pool.tensor_tensor(rstd[:, at:at + cols], var_eps[:, at:at + cols], power[:, at:at + cols],
                                   ALU.pow).then_inc(rstd_ready, 1)

            pool.memset(power[:, :], -0.5).then_inc(power_set, 1)
            pool.wait_ge(power_set, 1)
            for h in range(2):
                root(h + 1, h, 1)
            split_lo(pool, Tile(0, T_WK), 1, X_SIZES, handed_over=True)
            split_lo(pool, Tile(0, T_CT), 1, X_SIZES)
            with pool.Fori(0, NG // 2) as j:
                for s in range(2):
                    split_lo(pool, Tile(j, T_CT + s + 1), 1, X_SIZES)
            split_lo(pool, Tile(0, T_CN), 1, X_SIZES)
            with pool.Fori(0, NG // 2) as j:
                for s in range(2):
                    split_lo(pool, Tile(j, T_CN + s + 1), 1, X_SIZES)
            split_lo(pool, Tile(0, T_QKV), 1, Q_SIZES)
            def rope_sum(j, s):
                if not (isinstance(j, int) and s == 0):
                    pool.wait_ge(bank_full[7], j * 2 + (F7["rope_t"] - 1 + s))
                at = bass.ds(j * 2 * P + s * P, P)
                pool.tensor_tensor(q_rope, q_cos[:, :, at], q_sin[:, :, at], ALU.add).then_inc(rope_ready, 1)

            root(3, 0, 1)
            split_lo(pool, Tile(0, T_ROPE), 0, X_SIZES, handed_over=True)
            root(4, 1, 1)
            root(5, 2, 2)
            split_lo(pool, Tile(0, T_ROPE), 1, X_SIZES)
            root(6, 4, 2)
            split_lo(pool, Tile(0, T_M), 0, M_SIZES)
            pool.wait_ge(rope_part, 9)
            rope_sum(0, 0)
            split_lo(pool, Tile(0, T_M + 1), 0, M_SIZES)
            pool.wait_ge(rope_part, 12)
            rope_sum(0, 1)
            split_lo(pool, Tile(0, T_M), 1, M_SIZES)

            def pair_step(j, s, sizes=M_SIZES):
                split_lo(pool, Tile(j, T_M + s + 2), 0, sizes)
                split_lo(pool, Tile(j, T_M + s + 1), 1, M_SIZES)

            pair_step(0, 0)
            rope_sum(0, 2)
            with pool.Fori(0, (PAIRS - 4) // 2) as j:
                for s in range(1, 3):
                    pair_step(j, s)
                    rope_sum(j, s + 2)
            pair_step(0, PAIRS - 3)
            rope_sum(0, PAIRS - 1)
            pair_step(0, PAIRS - 2, E_SIZES)
            for h in range(2):
                root(7 + h, h, 1)
            split_lo(pool, Tile(0, T_E + 1), 0, E_SIZES)
            with pool.Fori(0, NE // 2 - 1) as j:
                for s in range(2):
                    split_lo(pool, Tile(j, T_E + s + 2), 0, E_SIZES)


def _rope_tables():
    half = np.arange(0, ROPE, 2, dtype=np.float32) / np.float32(ROPE)
    inv = (np.float32(1.0) / np.power(np.float32(10000.0), half)).astype(np.float32)
    ang = np.arange(T, dtype=np.float32)[:, None] * inv[None, :]
    ang = np.concatenate([ang, ang], axis=-1).astype(np.float32)
    sign = np.where(np.arange(ROPE) < ROPE // 2, np.float32(-1), np.float32(1))
    return np.cos(ang), np.sin(ang) * sign


def _chunked(w):
    return np.ascontiguousarray(w.reshape(NC, P, -1).transpose(1, 0, 2).reshape(P, -1))


def kernel(**inputs):
    import concourse.bacc as _bacc
    from concourse.bass_utils import run_bass_kernel_spmd as _run

    a = {k: np.asarray(v) for k, v in inputs.items()}
    rows = a["x"][0].reshape(2, P, D).transpose(1, 0, 2)

    small = np.zeros((P, C_END), np.float32)
    small[:, C_ID:C_ID + P] = np.eye(P, dtype=np.float32)
    small[:, C_MASK:C_MASK + P] = np.triu(np.full((P, P), MASKED, np.float32), 1)
    cos, sin = _rope_tables()
    for at, table in ((C_COS, cos), (C_SIN, sin)):
        small[:, at:at + 2 * ROPE] = table.reshape(2, P, ROPE).transpose(1, 0, 2).reshape(P, 2 * ROPE)
    small[:, C_RW:C_RW + NC * E] = _chunked(a["L0_ffn_router_w"])
    small[:, C_BIAS:C_BIAS + 64] = np.tile(a["L0_ffn_router_bias"], 2)[None, :]
    small[:, C_GQ:C_GQ + Q_RANK] = a["L0_attn_g_qa"][None, :]
    small[:, C_GKV:C_GKV + KV_RANK] = a["L0_attn_g_kva"][None, :]
    tie = np.tril(np.ones((GROUPS, GROUPS), np.float32), -1)
    small[:, C_TIE:C_END] = np.tile(tie.reshape(-1), 2)[None, :]

    context = a["ctx_2048"][0]
    ctx_t = np.stack([_chunked(context[g * 512:(g + 1) * 512].T) for g in range(NG)])
    ctx_n = np.stack([_chunked(context[g * 512:(g + 1) * 512]) for g in range(NG)])
    w_qkv = _chunked(np.concatenate([a["L0_attn_Wqa"], a["L0_attn_Wkva"]], axis=1))

    wqb = a["L0_attn_Wqb"].reshape(2, QR2, PAIRS, 2, NOPE + ROPE)
    wkvb = a["L0_attn_Wkvb"].reshape(KV_RANK, PAIRS, 2, NOPE + VDIM)
    wout = a["L0_attn_Wo"].reshape(PAIRS, 2, VDIM, D)
    w_mla = np.zeros((PAIRS, P, sum(M_SIZES)), np.float32)
    for i in range(PAIRS):
        for c in range(2):
            w = wqb[c, :, i]
            w_mla[i, 0:QR2, c * 256:c * 256 + 256] = w[:, :, 0:NOPE].reshape(QR2, 256)
        w_mla[i, :, 512:768] = wkvb[:, i, :, 0:NOPE].reshape(P, 256)
        w_mla[i, :, 768:1024] = wkvb[:, i, :, NOPE:].reshape(P, 256)
        w_mla[i, :, 1024:2048] = wout[i].transpose(1, 0, 2).reshape(P, 1024)
    w_rope = np.zeros((P, 2, 2, 512), np.float32)
    w_rope[0:QR2] = wqb[:, :, :, :, NOPE:].reshape(2, QR2, 2, 512).transpose(1, 2, 0, 3)

    def halves(w, axis):
        return np.stack(np.split(w, 2, axis=axis))

    gate = np.concatenate([halves(a["L0_ffn_sw_gate"], 1), a["L0_ffn_w_gate"]])
    up = np.concatenate([halves(a["L0_ffn_sw_up"], 1), a["L0_ffn_w_up"]])
    down = np.concatenate([halves(a["L0_ffn_sw_down"], 0), a["L0_ffn_w_down"]])
    gate, up = (w.reshape(NE, NC, P, I).transpose(0, 2, 1, 3).reshape(NE, P, NC * I) for w in (gate, up))
    down = down.reshape(NE, 2, P, D).transpose(0, 2, 1, 3).reshape(NE, P, 2 * D)
    w_exp = np.concatenate([gate, up[:, :, 0:I], down, up[:, :, I:]], axis=2)

    arrays = {
        "x": rows, "small": small,
        "wq": _chunked(a["L0_xattn_wq"].T), "wk": _chunked(a["L0_xattn_wk"].T),
        "wv": _chunked(a["L0_xattn_wv"].T), "wo": _chunked(a["L0_xattn_wo"].T),
        "ctx_t": ctx_t, "ctx_n": ctx_n, "w_qkv": w_qkv, "w_rope": w_rope.reshape(P, 2048), "w_mla": w_mla, "w_exp": w_exp,
    }
    arrays = {f"{k}_dram": np.ascontiguousarray(v) for k, v in arrays.items()}
    nc = _bacc.Bacc("TRN2", target_bir_lowering=False, num_devices=1)
    args = [nc.dram_tensor(k, v.shape, F32, kind="ExternalInput").ap() for k, v in arrays.items()]
    args.append(nc.dram_tensor("out_dram", (P, 2, D), F32, kind="ExternalOutput").ap())
    perceiver_layer(nc, *args)
    r = _run(nc, [arrays], core_ids=[0])
    return r.results[0]["out_dram"].transpose(1, 0, 2).reshape(1, T, D)
```

```python
from contextlib import ExitStack

import numpy as np

import concourse.bass as bass
from concourse import mybir

F32 = mybir.dt.float32
F32R = mybir.dt.float32r
ALU = mybir.AluOpType
ACT = mybir.ActivationFunctionType
AX = mybir.AxisListType.X

P = 128
T = 256
D = 512
NC = D // P
CTX = 4096
NG = CTX // 512
KEYS = CTX + T
HEADS, NOPE, ROPE, VDIM = 16, 128, 64, 128
Q_RANK, KV_RANK = 192, 128
QR2 = Q_RANK // 2
PAIRS = HEADS // 2
E, GROUPS, TOP_GROUPS, TOP, I = 32, 8, 4, 8, 256
PER = E // GROUPS
SHARED = 2
NE = E + SHARED
ROUTED_SCALE = 2.5
LN_EPS, RMS_EPS = 1e-5, 1e-6
XSCALE = 1.0 / float(np.sqrt(D))
MSCALE = float(NOPE + ROPE) ** -0.5
MASKED = -1e30
TAKEN = -3e38

T_WQ, T_WK, T_CT, T_WV, T_CN, T_WO, T_QKV, T_ROPE, T_M = 0, 1, 2, 10, 11, 19, 20, 21, 22
T_E = T_M + PAIRS

OFF = (0, 1280, 2304)
SLOT = 3072
X_SIZES = (1024, 1024)
Q_SIZES = (768, 768)
M_SIZES = (1024, 1024)
E_SIZES = (1280, 1024, 768)

C_ID, C_MASK, C_COS, C_SIN, C_RW, C_BIAS, C_GQ, C_GKV, C_TIE = 0, 128, 256, 384, 512, 640, 704, 896, 1024
C_END = C_TIE + 2 * GROUPS * GROUPS

F01 = dict(ln1=1, s_even=2, s_new=6, pt_even=7, ot=11, ln2=12, rope=13, y=14, ln3=15, h_t=16, moe=16)
F23 = dict(q=1, s_odd=2, pt_new=6, pt_odd=7, ot=11, qkv=12, rope=13, scores=14, pt=15, ln3=30, moe=30)
F45 = dict(ln1=1, k=2, v=3, wo=4, ln2=5, c=6)
F4 = dict(q=7, o_last=15, rows=16, moe=17)
F5 = dict(k0=7, k=6, o=9, o_last=22, rows=23, moe=24)
F67 = dict(pv=1, c=2, rows=11)
F6 = dict(v=3, router=12, moe=13)
F7 = dict(rope_t=3, score=12, moe=13)

V_LN1, V_Q, V_K, V_V, V_PT, V_OT, V_LN2, V_C, V_M0 = 1, 5, 7, 9, 11, 29, 33, 37, 41
V_MLA = V_M0 + 4
PER_PAIR = 7
V_LN3 = V_MLA + (PAIRS - 1) * PER_PAIR + 4
V_H = V_LN3 + 4


class Tile:

    def __init__(self, j, s):
        self.slot = s % 2
        self.loaded = (j + (s // 2 + 1)) * 16
        self.number = j * 2 + s

    def split(self, k):
        return self.number + 1 if k < 2 else self.number + (1 - T_E)

    def free(self, k):
        return self.number - 1 if k < 2 else self.number + (-1 - T_E)


def perceiver_layer(nc, x, small, wq, wk, wv, wo, ctx_t, ctx_n, w_qkv, w_rope, w_mla, w_exp, out):
    with ExitStack() as ctx:
        def sb(name, shape, dt=F32):
            return ctx.enter_context(nc.sbuf_tensor(name, shape, dt))

        def sem(name):
            return ctx.enter_context(nc.semaphore(name))

        bank = [ctx.enter_context(nc.psum_tensor(f"bank{b}", [P, 512], F32)) for b in range(8)]

        raw = sb("raw", [P, 2, SLOT])
        w_hi = sb("w_hi", [P, 2, SLOT], F32R)
        w_lo = sb("w_lo", [P, 2, SLOT], F32R)
        smalls = sb("smalls", [P, C_END])
        res = sb("res", [P, 2, D])
        xn = sb("xn", [P, 2, D])
        xt_hi = sb("xt_hi", [P, NC, T], F32R)
        xt_lo = sb("xt_lo", [P, NC, T], F32R)
        probs = sb("probs", [P, 2, 2, 512])
        o_row = sb("o_row", [P, 2, D])
        ident_r = sb("ident_r", [P, P], F32R)
        mask_r = sb("mask_r", [P, 3, P], F32R)
        rw_hi = sb("rw_hi", [P, NC, E], F32R)
        rw_lo = sb("rw_lo", [P, NC, E], F32R)
        stat = sb("stat", [P, 2, 6])
        mean_var = sb("mean_var", [P, 2, 2])
        var_eps = sb("var_eps", [P, 6])
        power = sb("power", [P, 6])
        rstd = sb("rstd", [P, 6])
        row_max = sb("row_max", [P, 2, NG + 1])
        neg_max = sb("neg_max", [P, 2])
        exp_bias = sb("exp_bias", [P, 2])
        sums = sb("sums", [P, 2, NG + 1])
        row_sum = sb("row_sum", [P, 2])
        row_inv = sb("row_inv", [P, 2])
        m_neg = sb("m_neg", [P, 4])
        m_bias = sb("m_bias", [P, 4])
        m_sum = sb("m_sum", [P, 4])
        m_inv = sb("m_inv", [P, 4])
        weights = sb("weights", [P, 2, NE])

        operands = sb("operands", [P, 11776], F32R)

        def op(at, *shape):
            v = operands[:, at:at + int(np.prod(shape))]
            names = "abc"[:len(shape)]
            if len(shape) == 1:
                return v
            return v.rearrange(f"p ({' '.join(names)}) -> p {' '.join(names)}",
                               **dict(zip(names[1:], shape[1:])))

        q_hi, q_lo = op(0, NC, T), op(1024, NC, T)
        k_hi, k_lo = op(2048, NC, T), op(3072, NC, T)
        v_hi, v_lo = op(4096, 2, D), op(5120, 2, D)
        pt_hi, pt_lo = op(6144, 2, 2, 512), op(8192, 2, 2, 512)
        ot_hi, ot_lo = op(0, NC, T), op(1024, NC, T)
        qc_hi, qc_lo = op(2048, 2, T), op(2560, 2, T)
        ckr_hi, ckr_lo = op(3072, 3, T), op(3840, 3, T)
        kvc_hi, kvc_lo = ckr_hi[:, 0, :], ckr_lo[:, 0, :]
        kr_hi, kr_lo = ckr_hi[:, 1:3, :], ckr_lo[:, 1:3, :]
        mq_hi, mq_lo = op(4608, 2, T), op(5120, 2, T)
        mk_hi, mk_lo = op(5632, 2, T), op(6144, 2, T)
        qr_hi, qr_lo = op(6656, T), op(6912, T)
        mv_hi, mv_lo = op(7168, 2, 2, T), op(8192, 2, 2, T)
        mpt_hi, mpt_lo = op(9216, 2, 384), op(9984, 2, 384)
        mo_hi, mo_lo = op(10752, 2, T), op(11264, 2, T)
        h_hi, h_lo = op(0, 2, 512), op(1024, 2, 512)

        scores = sb("scores", [P, 2, KEYS])

        def row(at, n):
            return scores[:, 0, at:at + n]

        squares = row(0, 192)
        qkv_row = row(3712, 640).rearrange("p (h n) -> p h n", h=2)
        qc_row = row(1024, 384).rearrange("p (h n) -> p h n", h=2)
        kvc_row = row(1408, 256).rearrange("p (h n) -> p h n", h=2)
        kr_cos, kr_sin = row(256, ROPE), row(320, ROPE)
        kr_row = row(384, 512).rearrange("p (h n) -> p h n", h=2)
        pair_probs = row(2176, 768).rearrange("p (h n) -> p h n", h=2)
        last_probs = row(2176, 256), row(2432, 512)
        last_pt_hi, last_pt_lo = (op(9216, 256), op(9472, 512)), (op(9984, 256), op(10240, 512))
        q_cos = scores[:, 1, 0:2048].rearrange("p (h n) -> p h n", h=2)
        q_sin = scores[:, 1, 2048:4096].rearrange("p (h n) -> p h n", h=2)
        q_rope = row(3456, 256).rearrange("p (h n) -> p h n", h=2)
        gate_act = scores[:, 1, 0:1024].rearrange("p (r n) -> p r n", r=2)
        h_row = scores[:, 1, 1024:2048].rearrange("p (r n) -> p r n", r=2)

        score_t = scores[0:E, 1, 3200:3200 + T]

        def route(at, n):
            return scores[:, 1, 2048 + at:2048 + at + n]

        x_loaded = [sem(f"x_loaded{h}") for h in range(2)]
        ident_loaded = sem("ident_loaded")
        small_loaded = sem("small_loaded")
        loaded_a = [sem(f"loaded_a{s}") for s in range(2)]
        loaded_b = [sem(f"loaded_b{s}") for s in range(2)]
        hi_split = [sem(f"hi_split{k}") for k in range(3)]
        lo_split = [sem(f"lo_split{k}") for k in range(3)]
        used = [sem(f"used{k}") for k in range(3)]
        bank_full = [sem(f"bank_full{b}") for b in range(8)]
        ev_hi = sem("ev_hi")
        ev_lo = sem("ev_lo")
        consts_rounded = sem("consts_rounded")
        mask_zeroed = sem("mask_zeroed")
        rw_split = sem("rw_split")
        vec = sem("vec")
        power_set = sem("power_set")
        var_ready = sem("var_ready")
        rstd_ready = sem("rstd_ready")
        xn_ready = sem("xn_ready")
        s_copied = sem("s_copied")
        s_max = sem("s_max")
        bias_ready = sem("bias_ready")
        p_ready = sem("p_ready")
        o_ready = sem("o_ready")
        res_done = sem("res_done")
        kr_zeroed = sem("kr_zeroed")
        kr_part = sem("kr_part")
        kr_done = sem("kr_done")
        rows_ready = sem("rows_ready")
        m_neg_ready = sem("m_neg_ready")
        m_bias_ready = sem("m_bias_ready")
        m_exp = sem("m_exp")
        m_inv_ready = sem("m_inv_ready")
        m_norm = sem("m_norm")
        rope_part = sem("rope_part")
        rope_ready = sem("rope_ready")
        sigmoid_ready = sem("sigmoid_ready")
        score_taken = sem("score_taken")
        row_silu = sem("row_silu")
        row_hidden = sem("row_hidden")
        silu_ready = sem("silu_ready")
        h_ready = sem("h_ready")
        stored = sem("stored")

        def split_hi(act, t, k, sizes, first=False):
            act.wait_ge((loaded_b if k else loaded_a)[t.slot], t.loaded)
            if not first:
                act.wait_ge(used[k], t.free(k))
            at, n = OFF[k], sizes[k]
            act.copy(w_hi[:, t.slot, at:at + n], raw[:, t.slot, at:at + n]).then_inc(hi_split[k], 1)

        def split_lo(eng, t, k, sizes, handed_over=False):
            eng.wait_ge(hi_split[k], t.split(k))
            if handed_over:
                eng.wait_ge(lo_split[k], t.split(k) - 1)
            at, n = OFF[k], sizes[k]
            eng.tensor_tensor(w_lo[:, t.slot, at:at + n], raw[:, t.slot, at:at + n],
                              w_hi[:, t.slot, at:at + n].bitcast(F32), ALU.subtract) \
               .then_inc(lo_split[k], 1)

        def out_hi(act, b, full, hi, n, rows=slice(0, P), at=0, scale=1.0):
            act.wait_ge(bank_full[b], full)
            act.activation(hi, bank[b][rows, at:at + n], ACT.Copy, scale=scale).then_inc(ev_hi, 1)

        def out_lo(dve, b, number, hi, lo, n, rows=slice(0, P), at=0):
            dve.wait_ge(ev_hi, number)
            dve.tensor_tensor(lo, bank[b][rows, at:at + n], hi.bitcast(F32), ALU.subtract) \
               .then_inc(ev_lo, 1)

        def flat(v):
            return v.rearrange("p a b -> p (a b)")

        def half(h):
            return slice(h * P, h * P + P)

        def chunks(v, b, h, rows, at, n):
            return v[rows, at:at + n, half(h)], bank[b][rows, 0:n * P].rearrange("p (c n) -> p c n", c=n)

        def half_hi(act, b, full, hi, h, n, rows=slice(0, P), at=0):
            act.wait_ge(bank_full[b], full)
            to, result = chunks(hi, b, h, rows, at, n)
            act.activation(to, result, ACT.Copy).then_inc(ev_hi, 1)

        def half_lo(dve, b, number, hi, lo, h, n, rows=slice(0, P), at=0):
            dve.wait_ge(ev_hi, number)
            to, result = chunks(lo, b, h, rows, at, n)
            dve.tensor_tensor(to, result, hi[rows, at:at + n, half(h)].bitcast(F32), ALU.subtract) \
               .then_inc(ev_lo, 1)

        def tokens_hi(act, b, full, hi, h):
            for k in range(2):
                half_hi(act, b + k, full, hi, h, 2, at=2 * k)

        def tokens_lo(dve, b, number, hi, lo, h):
            for k in range(2):
                half_lo(dve, b + k, number + k, hi, lo, h, 2, at=2 * k)

        block = ctx.enter_context(nc.Block())

        @block.sync
        def _(sp):
            def load(t, src, sizes, first=False):
                for part, k, at, n in ((loaded_a, 0, 0, sizes[0]), (loaded_b, 1, sizes[0], sum(sizes[1:]))):
                    if not first:
                        sp.wait_ge(lo_split[k], t.free(k))
                    sp.dma_start(raw[:, t.slot, OFF[k]:OFF[k] + n], src[:, at:at + n]).then_inc(part[t.slot], 16)

            for h in range(2):
                sp.dma_start(res[:, h, :], x[:, h, :]).then_inc(x_loaded[h], 16)
            sp.dma_start(smalls[:, C_ID:C_MASK], small[:, C_ID:C_MASK]).then_inc(ident_loaded, 16)
            load(Tile(0, T_WQ), wq, X_SIZES, first=True)
            sp.dma_start(smalls[:, C_MASK:C_END], small[:, C_MASK:C_END]).then_inc(small_loaded, 16)
            load(Tile(0, T_WK), wk, X_SIZES, first=True)
            with sp.Fori(0, NG // 2) as j:
                for s in range(2):
                    load(Tile(j, T_CT + s), ctx_t[bass.ds(j * 2 + s, 1)].squeeze(0), X_SIZES)
            load(Tile(0, T_WV), wv, X_SIZES)
            with sp.Fori(0, NG // 2) as j:
                for s in range(2):
                    load(Tile(j, T_CN + s), ctx_n[bass.ds(j * 2 + s, 1)].squeeze(0), X_SIZES)
            load(Tile(0, T_WO), wo, X_SIZES)
            load(Tile(0, T_QKV), w_qkv, Q_SIZES)
            load(Tile(0, T_ROPE), w_rope, X_SIZES)
            with sp.Fori(0, PAIRS // 2) as j:
                for s in range(2):
                    load(Tile(j, T_M + s), w_mla[bass.ds(j * 2 + s, 1)].squeeze(0), M_SIZES)
            for s in range(2):
                load(Tile(0, T_E + s), w_exp[s], E_SIZES)
            with sp.Fori(0, NE // 2 - 1) as j:
                for s in range(2, 4):
                    load(Tile(j, T_E + s), w_exp[bass.ds(j * 2 + s, 1)].squeeze(0), E_SIZES)
            for h in range(2):
                sp.wait_ge(res_done, 4 + 2 * NE - 1 + h)
                sp.dma_start(out[:, h, :], res[:, h, :]).then_inc(stored, 16)
            sp.wait_ge(stored, 32)

        @block.tensor
        def _(pe):
            ident = smalls[:, C_ID:C_ID + P]

            def product(o, a, b, start, stop, told=None):
                ins = pe.matmul(o, a[0], b[0], start=start, stop=False)
                if told is not None:
                    ins.then_inc(told, 1)
                pe.matmul(o, a[0], b[1], start=False, stop=False)
                return pe.matmul(o, a[1], b[0], start=False, stop=stop)

            def ready(t, k):
                pe.wait_ge(lo_split[k], t.split(k))

            def wcols(t, at, n, rows=P):
                return w_hi[0:rows, t.slot, at:at + n], w_lo[0:rows, t.slot, at:at + n]

            def x_chunk(t, c, at=0, n=512):
                return wcols(t, OFF[c // 2] + (c % 2) * 512 + at, n)

            def transpose_half(src, h, b, ready_sem, count, told=None):
                pe.wait_ge(ready_sem, count)
                for c in range(NC):
                    ins = pe.transpose(bank[b + c // 2][:, (c % 2) * P:(c % 2) * P + P],
                                       src[:, h, c * P:c * P + P], ident)
                    if told is not None and c == 0:
                        ins.then_inc(told, 1)
                    if c % 2:
                        ins.then_inc(bank_full[b + c // 2], 1)

            def project_t(t, first_bank, told=None, split=None):
                for m in range(NC):
                    b = first_bank + m // 2
                    for c in range(NC):
                        if m == 0 and c % 2 == 0:
                            ready(t, c // 2)
                            if split is not None:
                                pe.wait_ge(ev_lo, split + c // 2)
                        ins = product(bank[b][:, (m % 2) * T:(m % 2) * T + T], x_chunk(t, c, m * P, P),
                                      (xt_hi[:, c, :], xt_lo[:, c, :]), c == 0, c == NC - 1,
                                      told if m == c == 0 else None)
                        if m == NC - 1 and c == 1:
                            ins.then_inc(used[0], 1)
                    if m % 2:
                        ins.then_inc(bank_full[b], 1)

            def project_rows(t, a_hi, a_lo, first_bank, width=512, told=None, split=None, midway=(None, None)):
                for h in range(2):
                    for c in range(NC):
                        if split is not None and c % 2 == 0:
                            pe.wait_ge(ev_lo, split + 2 * h + c // 2)
                        if h == 0 and c % 2 == 0:
                            ready(t, c // 2)
                        w = wcols(t, OFF[c // 2] + (c % 2) * width, width)
                        ins = product(bank[first_bank + h][:, 0:width],
                                      (a_hi[:, c, half(h)], a_lo[:, c, half(h)]), w, c == 0, c == NC - 1,
                                      told if h == c == 0 else None)
                        if h == 1 and c == 1:
                            ins.then_inc(used[0], 1)
                        if c == 1 and midway[h] is not None:
                            midway[h]()
                    ins.then_inc(bank_full[first_bank + h], 1)

            pe.wait_ge(ident_loaded, 16)
            for h in range(2):
                transpose_half(xn, h, 4 * h, xn_ready, h + 1)
            project_t(Tile(0, T_WQ), 2, split=V_LN1 + 2)
            project_t(Tile(0, T_WK), 4, told=used[1])
            pe.wait_ge(ev_lo, V_Q + 1)

            def score_group(j, s):
                t = Tile(j, T_CT + s)
                for h in range(2):
                    b = 2 * (s % 2) + h
                    if not isinstance(j, int):
                        pe.wait_ge(s_copied, j * 4 + (2 * s + h - 3))
                    for c in range(NC):
                        if h == 0 and c % 2 == 0:
                            ready(t, c // 2)
                        ins = product(bank[b][:, :], (q_hi[:, c, half(h)], q_lo[:, c, half(h)]),
                                      x_chunk(t, c), c == 0, c == NC - 1,
                                      used[1] if h == c == 0 else None)
                        if h == 1 and c == 1:
                            ins.then_inc(used[0], 1)
                    ins.then_inc(bank_full[b], 1)

            score_group(0, 0)
            score_group(0, 1)
            with pe.Fori(1, NG // 2) as j:
                score_group(j, 0)
                score_group(j, 1)
            for h in range(2):
                pe.wait_ge(s_copied, 2 * (NG - 2) + h + 1)
                for c in range(NC):
                    ins = product(bank[h][:, 0:T], (q_hi[:, c, half(h)], q_lo[:, c, half(h)]),
                                  (k_hi[:, c, :], k_lo[:, c, :]), c == 0, c == NC - 1,
                                  used[1] if h == c == 0 else None)
                ins.then_inc(bank_full[h], 1)
            project_rows(Tile(0, T_WV), xt_hi, xt_lo, 4)

            def transpose_probs(ring, exps, blocks=4, told=None):
                for h in range(2):
                    pe.wait_ge(p_ready, exps + (h + 1))
                    for k in range(blocks):
                        ins = pe.transpose(bank[2 * ring + h][:, k * P:k * P + P],
                                           probs[:, ring, h, k * P:k * P + P], ident)
                        if told is not None and h == k == 0:
                            ins.then_inc(told, 1)
                    ins.then_inc(bank_full[2 * ring + h], 1)

            def times_values(ring, t, number, last=False, midway=None):
                for h in range(2):
                    pe.wait_ge(ev_lo, number + h)
                    for k in range(4):
                        if h == 0 and k % 2 == 0:
                            ready(t, k // 2)
                        ins = product(bank[6 + h][:, :], (pt_hi[:, ring, h, k * P:k * P + P],
                                                          pt_lo[:, ring, h, k * P:k * P + P]),
                                      x_chunk(t, k), False, last and k == 3)
                        if h == 1 and k == 1:
                            ins.then_inc(used[0], 1)
                            if midway is not None:
                                midway()
                    if last:
                        ins.then_inc(bank_full[6 + h], 1)
                if not last:
                    ins.then_inc(used[1], 1)

            transpose_probs(1, 0, blocks=2, told=used[1])
            transpose_probs(0, 2)
            for h in range(2):
                pe.wait_ge(ev_lo, V_PT + h)
                for k in range(2):
                    product(bank[6 + h][:, :], (pt_hi[:, 1, h, k * P:k * P + P], pt_lo[:, 1, h, k * P:k * P + P]),
                            (v_hi[:, k, :], v_lo[:, k, :]), k == 0, False)
            with pe.Fori(0, NG // 2 - 1) as j:
                transpose_probs(1, j * 4 + 4)
                times_values(0, Tile(j, T_CN), j * 4 + (V_PT + 2))
                transpose_probs(0, j * 4 + 6)
                times_values(1, Tile(j, T_CN + 1), j * 4 + (V_PT + 4))
            transpose_probs(1, 2 * NG)
            times_values(0, Tile(0, T_CN + 6), V_PT + 14)
            times_values(1, Tile(0, T_CN + 7), V_PT + 16, last=True,
                         midway=lambda: transpose_half(o_row, 0, 0, o_ready, 1))

            project_rows(Tile(0, T_WO), ot_hi, ot_lo, 4, told=used[1], split=V_OT,
                         midway=(lambda: transpose_half(o_row, 1, 2, o_ready, 2), None))

            def transpose_compressed(h):
                pe.wait_ge(rows_ready, h + 1)
                for c in range(2):
                    ins = pe.transpose(bank[4 + 2 * h][0:QR2, c * P:c * P + P],
                                       qc_row[:, h, c * QR2:c * QR2 + QR2], ident)
                ins.then_inc(bank_full[4 + 2 * h], 1)
                pe.transpose(bank[5 + 2 * h][:, 0:P], kvc_row[:, h, :], ident)
                for d in range(2):
                    ins = pe.transpose(bank[5 + 2 * h][:, (d + 1) * P:(d + 2) * P],
                                       kr_row[:, h, d * P:d * P + P], ident)
                ins.then_inc(bank_full[5 + 2 * h], 1)

            def qkv_half(h):
                t = Tile(0, T_QKV)
                for c in range(NC):
                    if c % 2 == 0:
                        pe.wait_ge(ev_lo, V_LN2 + 2 * h + c // 2)
                    if h == 0 and c % 2 == 0:
                        ready(t, c // 2)
                    ins = product(bank[2 + h][:, 0:384], (xt_hi[:, c, half(h)], xt_lo[:, c, half(h)]),
                                  wcols(t, OFF[c // 2] + (c % 2) * 384, 384), c == 0, c == NC - 1)
                    if h == 1 and c == 1:
                        ins.then_inc(used[0], 1)
                ins.then_inc(bank_full[2 + h], 1)

            transpose_half(xn, 0, 0, xn_ready, 3, told=used[1])
            qkv_half(0)
            transpose_half(xn, 1, 4, xn_ready, 4)
            qkv_half(1)
            transpose_compressed(0)

            def rope_queries(h, told=(None, None), midway=lambda: None):
                t = Tile(0, T_ROPE)
                for g in range(2):
                    if h == 0:
                        ready(t, g)
                    for c in range(2):
                        w = x_chunk(t, 2 * g + c)
                        ins = product(bank[2 * h + g][:, :], (qc_hi[0:QR2, c, half(h)], qc_lo[0:QR2, c, half(h)]),
                                      (w[0][0:QR2], w[1][0:QR2]), c == 0, c == 1, told[g] if c == 0 else None)
                    ins.then_inc(bank_full[2 * h + g], 1)
                    if g == 0:
                        midway()

            pe.wait_ge(ev_lo, V_C)
            rope_queries(0, told=(used[1], None), midway=lambda: transpose_compressed(1))
            pe.wait_ge(ev_lo, V_C + 3)
            rope_queries(1, told=(None, used[0]))
            pe.wait_ge(mask_zeroed, 1)
            pe.wait_ge(consts_rounded, 4)

            def project_pair(t, out_split=None, told=None, after_q=None):
                ready(t, 0)
                for hd in range(2):
                    for c in range(2):
                        ins = product(bank[4][:, hd * T:hd * T + T], wcols(t, c * 256 + hd * P, P, QR2),
                                      (qc_hi[0:QR2, c, :], qc_lo[0:QR2, c, :]), c == 0, c == 1,
                                      told if hd == c == 0 else None)
                ins.then_inc(bank_full[4], 1)
                if after_q is not None:
                    after_q()
                if out_split is not None:
                    pe.wait_ge(ev_lo, out_split)
                for hd in range(2):
                    ins = product(bank[5][:, hd * T:hd * T + T], wcols(t, 512 + hd * P, P),
                                  (kvc_hi, kvc_lo), True, True)
                ins.then_inc(bank_full[5], 1)
                for h in range(2):
                    ins = product(bank[6][:, h * T:h * T + T], (kvc_hi[:, half(h)], kvc_lo[:, half(h)]),
                                  wcols(t, 768, T), True, True)
                ins.then_inc(bank_full[6], 1)

            def rope_transpose(rope, told=None):
                pe.wait_ge(rope_ready, rope)
                for h in range(2):
                    ins = pe.transpose(bank[7][:, half(h)], q_rope[:, h, :], ident)
                    if told is not None and h == 0:
                        ins.then_inc(told, 1)
                ins.then_inc(bank_full[7], 1)

            def score_pair(told=None):
                for hd in range(2):
                    ins = pe.matmul(bank[2 + hd][:, 0:3 * P], ident_r[:, :], flat(mask_r[:, :, :]), start=True,
                                    stop=False)
                    if told is not None and hd == 0:
                        ins.then_inc(told, 1)
                    for h, at, n in ((1, 0, T), (0, T, P)):
                        o = bank[2 + hd][:, at:at + n]
                        product(o, (mq_hi[:, hd, half(h)], mq_lo[:, hd, half(h)]),
                                (mk_hi[:, hd, 0:n], mk_lo[:, hd, 0:n]), False, False)
                        ins = product(o, (qr_hi[:, half(h)], qr_lo[:, half(h)]),
                                      (kr_hi[:, hd, 0:n], kr_lo[:, hd, 0:n]), False, h == 0)
                    ins.then_inc(bank_full[2 + hd], 1)

            def transpose_pair(normed, told=None):
                for hd in range(2):
                    pe.wait_ge(m_norm, normed + 2 * (hd + 1))
                    for dst, src in ((0, T), (P, 0), (T, P)):
                        ins = pe.transpose(bank[2 + hd][:, dst:dst + P], pair_probs[:, hd, src:src + P], ident)
                        if told is not None and hd == dst == 0:
                            ins.then_inc(told, 1)
                    ins.then_inc(bank_full[2 + hd], 1)

            def values_pair(ring):
                for hd in range(2):
                    a = slice(hd * VDIM, hd * VDIM + VDIM)
                    product(bank[5][:, hd * T:hd * T + T], (mv_hi[:, ring, 0, a], mv_lo[:, ring, 0, a]),
                            (mpt_hi[:, hd, 0:T], mpt_lo[:, hd, 0:T]), True, False)
                    ins = product(bank[5][:, hd * T + P:hd * T + T], (mv_hi[:, ring, 1, a], mv_lo[:, ring, 1, a]),
                                  (mpt_hi[:, hd, T:T + P], mpt_lo[:, hd, T:T + P]), False, True)
                ins.then_inc(bank_full[5], 1)

            def out_pair(t, first=False, last=False, halves=(0, 1)):
                ready(t, 1)
                for h in halves:
                    for hd in range(2):
                        ins = product(bank[h][:, :], (mo_hi[:, hd, half(h)], mo_lo[:, hd, half(h)]),
                                      wcols(t, OFF[1] + hd * 512, 512), first and hd == 0, last and hd == 1)
                    if last:
                        ins.then_inc(bank_full[h], 1)
                if not last and 1 in halves:
                    ins.then_inc(used[1], 1)

            def pair_step(j, s, first_out=False):
                n = j * (2 * PER_PAIR) + s * PER_PAIR
                start = isinstance(j, int) and s == 0
                last_out = Tile(j, T_M + s - 1)
                if not start:
                    pe.wait_ge(ev_lo, n + (V_MLA - 3))
                score_pair(told=used[0] if start else None)
                project_pair(Tile(j, T_M + s + 1), n + (V_MLA - 1))
                if not start:
                    out_pair(last_out, first=first_out, halves=(0,))
                transpose_pair(j * 8 + 4 * s, told=used[0])
                rope_transpose(j * 2 + (s + 2))
                if not start:
                    out_pair(last_out, first=first_out, halves=(1,))
                pe.wait_ge(ev_lo, n + (V_MLA + (2 if start else 3)))
                values_pair(s % 2)

            project_pair(Tile(0, T_M), told=used[1], after_q=lambda: rope_transpose(1))
            pe.wait_ge(ev_lo, V_MLA - 2)
            pe.wait_ge(rope_part, 12)
            pair_step(0, 0)
            pair_step(0, 1, first_out=True)
            with pe.Fori(0, 2) as j:
                pair_step(j, 2)
                pair_step(j, 3)
            pair_step(0, 6)
            n = V_MLA + (PAIRS - 1) * PER_PAIR
            last = Tile(0, T_M + PAIRS - 1)
            ring = (PAIRS - 1) % 2

            def score_last(h):
                n = (h + 1) * P
                for hd in range(2):
                    o = bank[2 + h][:, hd * n:hd * n + n]
                    product(o, (mq_hi[:, hd, half(h)], mq_lo[:, hd, half(h)]),
                            (mk_hi[:, hd, 0:n], mk_lo[:, hd, 0:n]), True, False)
                    product(o, (qr_hi[:, half(h)], qr_lo[:, half(h)]),
                            (kr_hi[:, hd, 0:n], kr_lo[:, hd, 0:n]), False, False)
                    ins = pe.matmul(o[:, n - P:n], ident_r[:, :], mask_r[:, 1, :], start=False, stop=True)
                ins.then_inc(bank_full[2 + h], 1)

            def transpose_last(h):
                pe.wait_ge(m_norm, 4 * (PAIRS - 1) + 2 * (h + 1))
                for k in range(2 * (h + 1)):
                    ins = pe.transpose(bank[2 + h][:, k * P:k * P + P], last_probs[h][:, k * P:k * P + P], ident)
                ins.then_inc(bank_full[2 + h], 1)

            def values_last(h):
                for hd in range(2):
                    a = slice(hd * VDIM, hd * VDIM + VDIM)
                    for key in range(h + 1):
                        p = slice((hd * (h + 1) + key) * P, (hd * (h + 1) + key + 1) * P)
                        ins = product(bank[4 + h][:, hd * P:hd * P + P],
                                      (mv_hi[:, ring, key, a], mv_lo[:, ring, key, a]),
                                      (last_pt_hi[h][:, p], last_pt_lo[h][:, p]), key == 0, key == h)
                ins.then_inc(bank_full[4 + h], 1)

            pe.wait_ge(ev_lo, n - 3)
            score_last(0)
            score_last(1)
            pe.wait_ge(ev_lo, n - 1)
            out_pair(Tile(0, T_M + PAIRS - 2), halves=(0,))
            transpose_last(0)
            out_pair(Tile(0, T_M + PAIRS - 2), halves=(1,))
            pe.wait_ge(ev_lo, n)
            values_last(0)
            transpose_last(1)
            pe.wait_ge(ev_lo, n + 1)
            out_pair(last, last=True, halves=(0,))
            pe.wait_ge(ev_lo, n + 2)
            values_last(1)
            pe.wait_ge(ev_lo, n + 3)
            out_pair(last, last=True, halves=(1,))

            def expert_rows(s, h, b, told=None, split=None):
                t = Tile(0, T_E + s)
                for u in range(2):
                    for c in range(NC):
                        k = 0 if u == 0 or c == 0 else 2
                        if h == 0 and (u == c == 0 or u == c == 1):
                            ready(t, k)
                        if split is not None and u == 0 and c % 2 == 0:
                            pe.wait_ge(ev_lo, split + c // 2)
                        at = (u * NC + c) * I if k == 0 else OFF[2] + (c - 1) * I
                        ins = product(bank[b][:, u * I:u * I + I], (xt_hi[:, c, half(h)], xt_lo[:, c, half(h)]),
                                      wcols(t, at, I), c == 0, c == NC - 1, told if u == c == 0 else None)
                        if h == u == 1 and c == 0:
                            ins.then_inc(used[0], 1)
                ins.then_inc(bank_full[b], 1)

            def transpose_hidden(s):
                pe.wait_ge(row_hidden, s + 3)
                for h in range(2):
                    for m in range(2):
                        ins = pe.transpose(bank[s][:, m * T + h * P:m * T + h * P + P],
                                           h_row[:, s, h * I + m * P:h * I + m * P + P], ident)
                ins.then_inc(bank_full[s], 1)

            transpose_half(xn, 0, 2, xn_ready, 5, told=used[1])
            expert_rows(0, 0, 4, split=V_LN3)
            transpose_half(xn, 1, 0, xn_ready, 6)
            expert_rows(1, 0, 5)
            expert_rows(0, 1, 6, split=V_LN3 + 2)
            expert_rows(1, 1, 7, told=used[2])
            transpose_hidden(0)

            def gate_up(j, s, told=None):
                t = Tile(j, T_E + s)
                b = 2 * (s % 2)
                for u in range(2):
                    for m in range(2):
                        for c in range(NC):
                            k = 0 if u == 0 or c == 0 else 2
                            if m == 0 and (c == 0 and u == 0 or c == 1 and u == 1):
                                ready(t, k)
                            at = (u * NC + c) * I if k == 0 else OFF[2] + (c - 1) * I
                            ins = product(bank[b + u][:, m * T:m * T + T], wcols(t, at + m * P, P),
                                          (xt_hi[:, c, :], xt_lo[:, c, :]), c == 0, c == NC - 1,
                                          told if u == m == c == 0 else None)
                            if u == m == 1 and c == 0:
                                ins.then_inc(used[0], 1)
                    ins.then_inc(bank_full[b + u], 1)

            def down(j, s, told=None):
                t = Tile(j, T_E + s)
                pe.wait_ge(ev_lo, j * 2 + (V_H + s))
                ready(t, 1)
                for h in range(2):
                    b = 4 + 2 * (s % 2) + h
                    pe.wait_ge(res_done, j * 4 + (2 * s + h + 1))
                    for m in range(2):
                        a = slice(m * T + h * P, m * T + h * P + P)
                        ins = product(bank[b][:, :], (h_hi[:, s % 2, a], h_lo[:, s % 2, a]),
                                      wcols(t, OFF[1] + m * 512, 512), m == 0, m == 1,
                                      told if h == m == 0 else None)
                    ins.then_inc(bank_full[b], 1)

            pe.wait_ge(rw_split, 1)
            for c in range(NC):
                ins = product(bank[6][0:E, 0:T], (rw_hi[:, c, :], rw_lo[:, c, :]),
                              (xt_hi[:, c, :], xt_lo[:, c, :]), c == 0, c == NC - 1)
            ins.then_inc(bank_full[6], 1)
            transpose_hidden(1)
            down(0, 0, told=used[2])
            pe.wait_ge(ev_lo, V_H + 1)
            pe.wait_ge(sigmoid_ready, 1)
            for h in range(2):
                ins = pe.transpose(bank[7][:, h * E:h * E + E], score_t[:, half(h)], ident[0:E, 0:E])
            ins.then_inc(bank_full[7], 1)
            gate_up(0, 2, told=used[1])
            pe.wait_ge(score_taken, 1)
            down(0, 1, told=used[2])
            with pe.Fori(1, NE // 2 - 1) as j:
                gate_up(j, 1, told=used[1])
                down(j, 0, told=used[2])
                gate_up(j, 2, told=used[1])
                down(j, 1, told=used[2])
            gate_up(0, NE - 1, told=used[1])
            down(0, NE - 2, told=used[2])
            down(0, NE - 1)

        @block.scalar
        def _(act):
            split_hi(act, Tile(0, T_WQ), 0, X_SIZES, first=True)
            for h in range(2):
                tokens_hi(act, 4 * h, (F01 if h == 0 else F45)["ln1"], xt_hi, h)
            split_hi(act, Tile(0, T_WQ), 1, X_SIZES, first=True)
            for k in range(2):
                split_hi(act, Tile(0, T_WK), k, X_SIZES, first=True)
            for b in range(2):
                out_hi(act, 2 + b, F23["q"], flat(q_hi[:, 2 * b:2 * b + 2, :]), 512)
            for k in range(2):
                split_hi(act, Tile(0, T_CT), k, X_SIZES)
            for b in range(2):
                out_hi(act, 4 + b, F45["k"], flat(k_hi[:, 2 * b:2 * b + 2, :]), 512)
            act.wait_ge(ident_loaded, 16)
            act.copy(ident_r[:, :], smalls[:, C_ID:C_ID + P]).then_inc(consts_rounded, 1)
            act.wait_ge(small_loaded, 16)
            for k in range(1, 3):
                act.copy(mask_r[:, k, :], smalls[:, C_MASK:C_MASK + P]).then_inc(consts_rounded, 1)
            act.copy(flat(rw_hi[:, :, :]), smalls[:, C_RW:C_RW + NC * E]).then_inc(consts_rounded, 1)

            with act.Fori(0, NG // 2) as j:
                for s in range(2):
                    for k in range(2):
                        split_hi(act, Tile(j, T_CT + s + 1), k, X_SIZES)
                    for h in range(2):
                        b = 2 * s + h
                        act.wait_ge(bank_full[b], j + (F01["s_even"] if s == 0 else F23["s_odd"]))
                        act.copy(scores[:, h, bass.ds(j * 1024 + s * 512, 512)], bank[b][:, :]) \
                           .then_inc(s_copied, 1)
            for h in range(2):
                act.wait_ge(bank_full[h], F01["s_new"])
                act.copy(scores[:, h, CTX:KEYS], bank[h][:, 0:T]).then_inc(s_copied, 1)
            for k in range(2):
                split_hi(act, Tile(0, T_CN), k, X_SIZES)

            def exps(ring, at, n, sum_at):
                for h in range(2):
                    act.activation(probs[:, ring, h, 0:n], scores[:, h, at], ACT.Exp, bias=exp_bias[:, h:h + 1],
                                   scale=XSCALE, accum_out=sums[:, h, sum_at]).then_inc(p_ready, 1)

            def probs_hi(ring, full, n=512):
                for h in range(2):
                    out_hi(act, 2 * ring + h, full, pt_hi[:, ring, h, 0:n], n)

            act.wait_ge(bias_ready, 1)
            exps(1, slice(CTX, KEYS), T, slice(NG, NG + 1))
            exps(0, slice(0, 512), 512, slice(0, 1))
            for b in range(2):
                out_hi(act, 4 + b, F45["v"], v_hi[:, b, :], 512)
            probs_hi(1, F23["pt_new"], T)
            exps(1, slice(512, 1024), 512, slice(1, 2))
            probs_hi(0, F01["pt_even"])
            with act.Fori(0, NG // 2 - 1) as j:
                for s in range(2):
                    exps(s, bass.ds(j * 1024 + (s + 2) * 512, 512), 512, bass.ds(j * 2 + (s + 2), 1))
                    probs_hi(1 - s, j + (F23["pt_odd"] if s == 0 else F01["pt_even"] + 1))
                    for k in range(2):
                        split_hi(act, Tile(j, T_CN + s + 1), k, X_SIZES)
            probs_hi(1, F23["pt_odd"] + 3)
            for s in (NG - 1, NG):
                for k in range(2):
                    split_hi(act, Tile(0, T_CN + s), k, X_SIZES)

            tokens_hi(act, 0, F01["ot"], ot_hi, 0)
            for k in range(2):
                split_hi(act, Tile(0, T_QKV), k, Q_SIZES)
            tokens_hi(act, 2, F23["ot"], ot_hi, 1)
            split_hi(act, Tile(0, T_ROPE), 0, X_SIZES)
            tokens_hi(act, 0, F01["ln2"], xt_hi, 0)
            split_hi(act, Tile(0, T_ROPE), 1, X_SIZES)
            tokens_hi(act, 4, F45["ln2"], xt_hi, 1)
            for h in range(2):
                full = (F45 if h == 0 else F67)["c"]
                half_hi(act, 4 + 2 * h, full, qc_hi, h, 2, rows=slice(0, QR2))
                half_hi(act, 5 + 2 * h, full, ckr_hi, h, 3)
                if h == 0:
                    split_hi(act, Tile(0, T_M), 0, M_SIZES)
            split_hi(act, Tile(0, T_M), 1, M_SIZES)
            split_hi(act, Tile(0, T_M + 1), 0, M_SIZES)

            def pair_qk_hi(j, s):
                out_hi(act, 4, j * 2 + (F4["q"] + s), flat(mq_hi[:, :, :]), 512)
                out_hi(act, 5, F5["k0"] if isinstance(j, int) and s == 0 else j * 4 + (F5["k"] + 2 * s),
                       flat(mk_hi[:, :, :]), 512)

            def pair_v_hi(j, s):
                out_hi(act, 6, j * 2 + (F6["v"] + s), flat(mv_hi[:, s % 2, :, :]), 512)

            def pair_exps(j, s):
                act.wait_ge(m_bias_ready, j * 2 + (s + 1))
                for hd in range(2):
                    for late, at, n in ((0, 0, T), (1, T, P)):
                        k = 2 * hd + late
                        act.activation(pair_probs[:, hd, at:at + n], bank[2 + hd][:, at:at + n], ACT.Exp,
                                       bias=m_bias[:, k:k + 1], scale=MSCALE, accum_out=m_sum[:, k:k + 1]) \
                           .then_inc(m_exp, 1)

            def pair_probs_hi(j, s):
                for hd in range(2):
                    out_hi(act, 2 + hd, j * 4 + (F23["pt"] + 2 * s), mpt_hi[:, hd, :], 384)

            def rope_hi(j, s):
                out_hi(act, 7, j * 2 + (F7["rope_t"] + s), qr_hi, T)

            def pair_step(j, s, sizes=M_SIZES):
                split_hi(act, Tile(j, T_M + s + 2), 0, sizes)
                pair_exps(j, s)
                pair_qk_hi(j, s + 1)
                pair_probs_hi(j, s)
                rope_hi(j, s + 1)
                pair_v_hi(j, s + 1)
                out_hi(act, 5, j * 4 + (F5["o"] + 2 * s), flat(mo_hi[:, :, :]), 512)
                split_hi(act, Tile(j, T_M + s + 1), 1, M_SIZES)

            out_hi(act, 4, F4["q"], flat(mq_hi[:, :, :]), 512)
            rope_hi(0, 0)
            out_hi(act, 5, F5["k0"], flat(mk_hi[:, :, :]), 512)
            pair_v_hi(0, 0)
            pair_step(0, 0)
            with act.Fori(0, (PAIRS - 4) // 2) as j:
                pair_step(j, 1)
                pair_step(j, 2)
            pair_step(0, PAIRS - 3)
            pair_step(0, PAIRS - 2, E_SIZES)
            def last_exps(h):
                act.wait_ge(m_bias_ready, PAIRS + h)
                n = (h + 1) * P
                for hd in range(2):
                    k = 2 * h + hd
                    act.activation(last_probs[h][:, hd * n:hd * n + n], bank[2 + h][:, hd * n:hd * n + n], ACT.Exp,
                                   bias=m_bias[:, k:k + 1], scale=MSCALE, accum_out=m_sum[:, k:k + 1]) \
                       .then_inc(m_exp, 1)

            def last_probs_hi(h):
                out_hi(act, 2 + h, F23["pt"] + 2 * (PAIRS - 1), last_pt_hi[h], 256 * (h + 1))

            last_exps(0)
            last_exps(1)
            last_probs_hi(0)
            split_hi(act, Tile(0, T_E), 2, E_SIZES, first=True)
            half_hi(act, 4, F4["o_last"], mo_hi, 0, 2)
            last_probs_hi(1)
            split_hi(act, Tile(0, T_E + 1), 0, E_SIZES)
            split_hi(act, Tile(0, T_E + 1), 2, E_SIZES, first=True)
            half_hi(act, 5, F5["o_last"], mo_hi, 1, 2)
            split_hi(act, Tile(0, T_E), 1, E_SIZES)
            tokens_hi(act, 2, F23["ln3"], xt_hi, 0)
            tokens_hi(act, 0, F01["ln3"], xt_hi, 1)

            def rows_silu(s, h):
                b = 4 + 2 * h + s
                act.wait_ge(bank_full[b], (F67 if h else F5 if s else F4)["rows"])
                act.activation(gate_act[:, s, h * I:h * I + I], bank[b][:, 0:I], ACT.Silu).then_inc(row_silu, 1)

            rows_silu(0, 0)
            split_hi(act, Tile(0, T_E + 1), 1, E_SIZES)
            rows_silu(1, 0)
            rows_silu(0, 1)
            split_hi(act, Tile(0, T_E + 2), 0, E_SIZES)
            rows_silu(1, 1)
            for s in range(2):
                out_hi(act, s, F01["h_t"], h_hi[:, s, :], 512)
                if s == 0:
                    split_hi(act, Tile(0, T_E + 2), 2, E_SIZES)
            act.wait_ge(bank_full[6], F6["router"])
            act.activation(score_t, bank[6][0:E, 0:T], ACT.Sigmoid).then_inc(sigmoid_ready, 1)
            split_hi(act, Tile(0, T_E + 3), 0, E_SIZES)
            split_hi(act, Tile(0, T_E + 3), 2, E_SIZES)
            split_hi(act, Tile(0, T_E + 2), 1, E_SIZES)

            def expert_step(j, s, ahead=2):
                act.wait_ge(bank_full[2 * (s % 2)], j + ((F01 if s % 2 == 0 else F23)["moe"] + s // 2))
                act.activation(gate_act[:, s % 2, :], bank[2 * (s % 2)][:, :], ACT.Silu).then_inc(silu_ready, 1)
                if ahead >= 1:
                    split_hi(act, Tile(j, T_E + s + 1), 1, E_SIZES)
                if ahead >= 2:
                    split_hi(act, Tile(j, T_E + s + 2), 0, E_SIZES)
                act.wait_ge(h_ready, j * 2 + (s - 1))
                act.copy(h_hi[:, s % 2, :], h_row[:, s % 2, :]).then_inc(ev_hi, 1)
                if ahead >= 2:
                    split_hi(act, Tile(j, T_E + s + 2), 2, E_SIZES)

            with act.Fori(1, NE // 2 - 1) as j:
                expert_step(j, 0)
                expert_step(j, 1)
            expert_step(0, NE - 2, ahead=1)
            expert_step(0, NE - 1, ahead=0)

        @block.vector
        def _(dve):
            step = [0]

            def then(ins):
                step[0] += 1
                ins.then_inc(vec, 1)
                dve.wait_ge(vec, step[0])

            def norm_stats(h, midway=None):
                then(dve.bn_stats(stat[:, h, :], res[:, h, :]))
                if midway is not None:
                    midway()
                then(dve.bn_aggr(mean_var[:, h, :], stat[:, h, :]))
                dve.tensor_scalar(var_eps[:, h:h + 1], mean_var[:, h, 1:2], LN_EPS, None, ALU.add) \
                   .then_inc(var_ready, 1)

            def normalize(h, roots):
                dve.wait_ge(rstd_ready, roots)
                dve.tensor_scalar(xn[:, h, :], res[:, h, :], mean_var[:, h, 0:1], rstd[:, h:h + 1],
                                  ALU.subtract, ALU.mult).then_inc(xn_ready, 1)

            def add_to_residual(b, full, h, number):
                dve.wait_ge(bank_full[b + h], full)
                dve.tensor_tensor(res[:, h, :], bank[b + h][:, :], res[:, h, :], ALU.add) \
                   .then_inc(res_done, 1)
                dve.wait_ge(res_done, number)

            def split_pair_lo(number, b, hi, lo):
                for k in range(2):
                    out_lo(dve, b + k, number + k, flat(hi[:, 2 * k:2 * k + 2, :]),
                           flat(lo[:, 2 * k:2 * k + 2, :]), 512)

            for h in range(2):
                dve.wait_ge(x_loaded[h], 16)
                norm_stats(h)
            for h in range(2):
                normalize(h, h + 1)
            split_lo(dve, Tile(0, T_WQ), 0, X_SIZES)
            for h in range(2):
                tokens_lo(dve, 4 * h, V_LN1 + 2 * h, xt_hi, xt_lo, h)
            split_lo(dve, Tile(0, T_WQ), 1, X_SIZES)
            split_lo(dve, Tile(0, T_WK), 0, X_SIZES)
            split_pair_lo(V_Q, 2, q_hi, q_lo)
            split_lo(dve, Tile(0, T_CT), 0, X_SIZES)
            split_pair_lo(V_K, 4, k_hi, k_lo)
            dve.wait_ge(consts_rounded, 4)
            dve.tensor_tensor(flat(rw_lo[:, :, :]), smalls[:, C_RW:C_RW + NC * E],
                              flat(rw_hi[:, :, :]).bitcast(F32), ALU.subtract).then_inc(rw_split, 1)
            with dve.Fori(0, NG // 2) as j:
                for s in range(2):
                    split_lo(dve, Tile(j, T_CT + s + 1), 0, X_SIZES)
                    for h in range(2):
                        dve.wait_ge(s_copied, j * 4 + (2 * s + h + 1))
                        dve.tensor_reduce(row_max[:, h, bass.ds(j * 2 + s, 1)],
                                          scores[:, h, bass.ds(j * 1024 + s * 512, 512)], AX, ALU.max) \
                           .then_inc(s_max, 1)
            for h in range(2):
                dve.wait_ge(s_copied, 2 * NG + h + 1)
                dve.tensor_reduce(row_max[:, h, NG:NG + 1], scores[:, h, CTX:KEYS], AX, ALU.max) \
                   .then_inc(s_max, 1)
            dve.wait_ge(s_max, 2 * NG + 2)
            then(dve.tensor_reduce(neg_max[:, :], row_max[:, :, :], AX, ALU.max, negate=True))
            dve.tensor_scalar(exp_bias[:, :], neg_max[:, :], XSCALE, None, ALU.mult).then_inc(bias_ready, 1)
            split_lo(dve, Tile(0, T_CN), 0, X_SIZES)
            for b in range(2):
                out_lo(dve, 4 + b, V_V + b, v_hi[:, b, :], v_lo[:, b, :], 512)

            def probs_lo(ring, number, n=512):
                for h in range(2):
                    out_lo(dve, 2 * ring + h, number + h, pt_hi[:, ring, h, 0:n], pt_lo[:, ring, h, 0:n], n)

            probs_lo(1, V_PT, T)
            probs_lo(0, V_PT + 2)
            with dve.Fori(0, NG // 2 - 1) as j:
                for s in range(2):
                    probs_lo(1 - s, j * 4 + (V_PT + 4 + 2 * s))
                    split_lo(dve, Tile(j, T_CN + s + 1), 0, X_SIZES)
            probs_lo(1, V_PT + 16)
            for s in (NG - 1, NG):
                split_lo(dve, Tile(0, T_CN + s), 0, X_SIZES)
            dve.wait_ge(p_ready, 2 * (NG + 1))
            then(dve.tensor_reduce(row_sum[:, :], sums[:, :, :], AX, ALU.add))
            then(dve.reciprocal(row_inv[:, :], row_sum[:, :]))
            dve.memset(kr_row[:, :, :], 0.0).then_inc(kr_zeroed, 1)

            def normalize_output(h):
                dve.wait_ge(bank_full[6 + h], F67["pv"])
                dve.tensor_scalar(o_row[:, h, :], bank[6 + h][:, :], row_inv[:, h:h + 1], None, ALU.mult) \
                   .then_inc(o_ready, 1)

            def mean_squares(h, midway=None):
                dve.wait_ge(bank_full[2 + h], F23["qkv"])
                then(dve.tensor_copy(qkv_row[:, h, :], bank[2 + h][:, 0:Q_RANK + KV_RANK]))
                if midway is not None:
                    midway()
                for at, n, k in ((0, Q_RANK, 0), (Q_RANK, KV_RANK, 1)):
                    v = qkv_row[:, h, at:at + n]
                    ins = dve.tensor_tensor_reduce(squares[:, 0:n], v, v, 1.0 / n, RMS_EPS, ALU.mult, ALU.add,
                                                   var_eps[:, 2 + 2 * h + k:3 + 2 * h + k])
                    if k == 0:
                        then(ins)
                ins.then_inc(var_ready, 1)

            def rope_keys(h):
                raw_k = bank[2 + h][:, Q_RANK + KV_RANK:384]
                cos = smalls[:, C_COS + h * ROPE:C_COS + (h + 1) * ROPE]
                sin = smalls[:, C_SIN + h * ROPE:C_SIN + (h + 1) * ROPE]
                dve.tensor_tensor(kr_cos, raw_k, cos, ALU.mult).then_inc(kr_part, 1)
                dve.tensor_tensor(kr_sin[:, 0:R2], raw_k[:, R2:ROPE], sin[:, 0:R2], ALU.mult).then_inc(kr_part, 1)
                dve.tensor_tensor(kr_sin[:, R2:ROPE], raw_k[:, 0:R2], sin[:, R2:ROPE], ALU.mult) \
                   .then_inc(kr_part, 1)
                dve.wait_ge(kr_part, 3 * h + 3)
                for at in (0, 3 * ROPE):
                    dve.tensor_tensor(kr_row[:, h, at:at + ROPE], kr_cos, kr_sin, ALU.add).then_inc(kr_done, 1)

            def compressed_rows(h, roots):
                dve.wait_ge(rstd_ready, roots)
                for out_row, at, n, gain, k in ((qc_row, 0, Q_RANK, C_GQ, 0), (kvc_row, Q_RANK, KV_RANK, C_GKV, 1)):
                    ins = dve.scalar_tensor_tensor(
                        out=out_row[:, h, :], in0=qkv_row[:, h, at:at + n],
                        scalar=rstd[:, 2 + 2 * h + k:3 + 2 * h + k], in1=smalls[:, gain:gain + n],
                        op0=ALU.mult, op1=ALU.mult)
                    if k == 0:
                        then(ins)
                dve.wait_ge(kr_done, 2 * h + 2)
                ins.then_inc(rows_ready, 1)

            def compressed_q_lo(h):
                half_lo(dve, 4 + 2 * h, V_C + 2 * h, qc_hi, qc_lo, h, 2, rows=slice(0, QR2))

            def compressed_kv_lo(h):
                half_lo(dve, 5 + 2 * h, V_C + 2 * h + 1, ckr_hi, ckr_lo, h, 3)

            def rope_products(h, g):
                b = 2 * h + g
                dve.wait_ge(bank_full[b], (F01 if b < 2 else F23)["rope"])
                q, to_cos, to_sin = (v.rearrange("p (g n) -> p g n", n=ROPE)
                                     for v in (bank[b][:, :], q_cos[:, h, g * 512:g * 512 + 512],
                                               q_sin[:, h, g * 512:g * 512 + 512]))
                cos, sin = (smalls[:, at + h * ROPE:at + (h + 1) * ROPE].unsqueeze(1).broadcast_to([P, 8, ROPE])
                            for at in (C_COS, C_SIN))
                dve.tensor_tensor(to_cos, q, cos, ALU.mult).then_inc(rope_part, 1)
                dve.tensor_tensor(to_sin[:, :, 0:R2], q[:, :, R2:ROPE], sin[:, :, 0:R2], ALU.mult) \
                   .then_inc(rope_part, 1)
                dve.tensor_tensor(to_sin[:, :, R2:ROPE], q[:, :, 0:R2], sin[:, :, R2:ROPE], ALU.mult) \
                   .then_inc(rope_part, 1)

            R2 = ROPE // 2
            normalize_output(0)
            tokens_lo(dve, 0, V_OT, ot_hi, ot_lo, 0)
            normalize_output(1)
            split_lo(dve, Tile(0, T_QKV), 0, Q_SIZES)
            tokens_lo(dve, 2, V_OT + 2, ot_hi, ot_lo, 1)
            add_to_residual(4, F45["wo"], 0, 1)
            norm_stats(0)
            normalize(0, 3)
            add_to_residual(4, F45["wo"], 1, 2)
            norm_stats(1, midway=lambda: tokens_lo(dve, 0, V_LN2, xt_hi, xt_lo, 0))
            normalize(1, 4)
            mean_squares(0, midway=lambda: tokens_lo(dve, 4, V_LN2 + 2, xt_hi, xt_lo, 1))
            dve.wait_ge(kr_zeroed, 1)
            rope_keys(0)
            compressed_rows(0, 5)
            mean_squares(1)
            compressed_q_lo(0)
            rope_keys(1)
            compressed_rows(1, 6)
            compressed_kv_lo(0)
            compressed_q_lo(1)
            compressed_kv_lo(1)
            rope_products(0, 0)
            rope_products(0, 1)
            rope_products(1, 0)
            rope_products(1, 1)

            def pair_bias(j, s):
                for hd in range(2):
                    dve.wait_ge(bank_full[2 + hd], j * 4 + (F23["scores"] + 2 * s))
                    for k, at, n in ((2 * hd, 0, T), (2 * hd + 1, T, P)):
                        dve.tensor_reduce(m_neg[:, k:k + 1], bank[2 + hd][:, at:at + n], AX, ALU.max,
                                          negate=True).then_inc(m_neg_ready, 1)
                dve.wait_ge(m_neg_ready, j * 8 + (4 * s + 4))
                dve.tensor_scalar(m_bias[:, :], m_neg[:, :], MSCALE, None, ALU.mult).then_inc(m_bias_ready, 1)

            def pair_normalize(j, s):
                dve.wait_ge(m_exp, j * 8 + (4 * s + 4))
                dve.reciprocal(m_inv[:, :], m_sum[:, :]).then_inc(m_inv_ready, 1)
                dve.wait_ge(m_inv_ready, j * 2 + (s + 1))
                for hd in range(2):
                    for k, at, n in ((2 * hd, 0, T), (2 * hd + 1, T, P)):
                        v = pair_probs[:, hd, at:at + n]
                        dve.tensor_scalar(v, v, m_inv[:, k:k + 1], None, ALU.mult).then_inc(m_norm, 1)

            def pair_qk_lo(n):
                out_lo(dve, 4, n, flat(mq_hi[:, :, :]), flat(mq_lo[:, :, :]), 512)
                out_lo(dve, 5, n + 1, flat(mk_hi[:, :, :]), flat(mk_lo[:, :, :]), 512)

            def pair_rope_v_lo(n, s):
                out_lo(dve, 7, n, qr_hi, qr_lo, T)
                out_lo(dve, 6, n + 1, flat(mv_hi[:, s % 2, :, :]), flat(mv_lo[:, s % 2, :, :]), 512)

            def pair_probs_lo(n):
                for hd in range(2):
                    out_lo(dve, 2 + hd, n + hd, mpt_hi[:, hd, :], mpt_lo[:, hd, :], 384)

            def pair_step(j, s):
                n = j * (2 * PER_PAIR) + (V_MLA + s * PER_PAIR)
                pair_bias(j, s)
                pair_normalize(j, s)
                if isinstance(j, int) and s == 0:
                    out_lo(dve, 5, n + 1, flat(mk_hi[:, :, :]), flat(mk_lo[:, :, :]), 512)
                    pair_probs_lo(n + 2)
                    out_lo(dve, 4, n, flat(mq_hi[:, :, :]), flat(mq_lo[:, :, :]), 512)
                else:
                    pair_qk_lo(n)
                    pair_probs_lo(n + 2)
                pair_rope_v_lo(n + 4, s + 1)
                out_lo(dve, 5, n + 6, flat(mo_hi[:, :, :]), flat(mo_lo[:, :, :]), 512)

            out_lo(dve, 4, V_M0, flat(mq_hi[:, :, :]), flat(mq_lo[:, :, :]), 512)
            out_lo(dve, 7, V_M0 + 1, qr_hi, qr_lo, T)
            out_lo(dve, 5, V_M0 + 2, flat(mk_hi[:, :, :]), flat(mk_lo[:, :, :]), 512)
            out_lo(dve, 6, V_M0 + 3, flat(mv_hi[:, 0, :, :]), flat(mv_lo[:, 0, :, :]), 512)
            pair_step(0, 0)
            with dve.Fori(0, (PAIRS - 2) // 2) as j:
                pair_step(j, 1)
                pair_step(j, 2)

            def last_bias(h):
                dve.wait_ge(bank_full[2 + h], F23["scores"] + 2 * (PAIRS - 1))
                n = (h + 1) * P
                for hd in range(2):
                    dve.tensor_reduce(m_neg[:, 2 * h + hd:2 * h + hd + 1], bank[2 + h][:, hd * n:hd * n + n], AX,
                                      ALU.max, negate=True).then_inc(m_neg_ready, 1)
                dve.wait_ge(m_neg_ready, 4 * (PAIRS - 1) + 2 * (h + 1))
                k = slice(2 * h, 2 * h + 2)
                dve.tensor_scalar(m_bias[:, k], m_neg[:, k], MSCALE, None, ALU.mult).then_inc(m_bias_ready, 1)

            def last_normalize(h):
                dve.wait_ge(m_exp, 4 * (PAIRS - 1) + 2 * (h + 1))
                k = slice(2 * h, 2 * h + 2)
                dve.reciprocal(m_inv[:, k], m_sum[:, k]).then_inc(m_inv_ready, 1)
                dve.wait_ge(m_inv_ready, PAIRS + h)
                n = (h + 1) * P
                for hd in range(2):
                    v = last_probs[h][:, hd * n:hd * n + n]
                    dve.tensor_scalar(v, v, m_inv[:, 2 * h + hd:2 * h + hd + 1], None, ALU.mult) \
                       .then_inc(m_norm, 1)

            def last_probs_lo(h):
                out_lo(dve, 2 + h, n + 2 * h, last_pt_hi[h], last_pt_lo[h], 256 * (h + 1))

            n = V_MLA + (PAIRS - 1) * PER_PAIR
            last_bias(0)
            last_bias(1)
            last_normalize(0)
            last_normalize(1)
            last_probs_lo(0)
            split_lo(dve, Tile(0, T_E), 2, E_SIZES)
            half_lo(dve, 4, n + 1, mo_hi, mo_lo, 0, 2)
            last_probs_lo(1)
            add_to_residual(0, F01["y"], 0, 3)
            norm_stats(0)
            half_lo(dve, 5, n + 3, mo_hi, mo_lo, 1, 2)
            normalize(0, 7)
            split_lo(dve, Tile(0, T_E + 1), 2, E_SIZES)
            add_to_residual(0, F01["y"], 1, 4)
            tokens_lo(dve, 2, V_LN3, xt_hi, xt_lo, 0)
            norm_stats(1)
            normalize(1, 8)
            split_lo(dve, Tile(0, T_E), 1, E_SIZES, handed_over=True)
            tokens_lo(dve, 0, V_LN3 + 2, xt_hi, xt_lo, 1)

            def rows_hidden(s, h):
                dve.wait_ge(row_silu, 2 * h + s + 1)
                b = 4 + 2 * h + s
                dve.tensor_tensor(h_row[:, s, h * I:h * I + I], bank[b][:, I:2 * I], gate_act[:, s, h * I:h * I + I],
                                  ALU.mult).then_inc(row_hidden, 1)

            then(dve.memset(weights[:, :, 0:SHARED], 1.0))
            rows_hidden(0, 0)
            rows_hidden(1, 0)
            split_lo(dve, Tile(0, T_E + 1), 1, E_SIZES)
            rows_hidden(0, 1)
            rows_hidden(1, 1)
            out_lo(dve, 0, V_H, h_hi[:, 0, :], h_lo[:, 0, :], 512)
            split_lo(dve, Tile(0, T_E + 2), 2, E_SIZES)
            out_lo(dve, 1, V_H + 1, h_hi[:, 1, :], h_lo[:, 1, :], 512)

            score = route(0, 64)
            choice, big, small_, g_top, g_low, g_two = (route(64 + 64 * k, 64) for k in range(6))
            beats, ties = route(448, 128), route(576, 128)
            rank, chosen_g = route(704, 16), route(720, 16)
            masked, replaced = route(736, 64), route(800, 64)
            top8, picked = route(864, 16), route(880, 64)
            total, scaled = route(944, 2), route(946, 2)

            def pairs_of(v):
                g = v.rearrange("p (g n) -> p g n", n=PER)
                return g[:, :, 0:2], g[:, :, 2:4]

            def by2(v):
                return v[:, 0:32].rearrange("p (g n) -> p g n", n=2)

            dve.wait_ge(bank_full[7], F7["score"])
            dve.tensor_copy(score, bank[7][:, 0:2 * E]).then_inc(score_taken, 1)
            dve.wait_ge(score_taken, 1)
            then(dve.tensor_tensor(choice, score, smalls[:, C_BIAS:C_BIAS + 64], ALU.add))
            a, b = pairs_of(choice)
            then(dve.tensor_tensor(by2(big), a, b, ALU.max))
            then(dve.tensor_tensor(by2(small_), a, b, ALU.min))
            big2, small2 = by2(big), by2(small_)
            then(dve.tensor_tensor(g_top[:, 0:16], big2[:, :, 0], big2[:, :, 1], ALU.max))
            then(dve.tensor_tensor(g_low[:, 0:16], big2[:, :, 0], big2[:, :, 1], ALU.min))
            then(dve.tensor_tensor(g_two[:, 0:16], small2[:, :, 0], small2[:, :, 1], ALU.max))
            then(dve.tensor_tensor(g_two[:, 16:32], g_low[:, 0:16], g_two[:, 0:16], ALU.max))
            then(dve.tensor_tensor(g_two[:, 32:48], g_top[:, 0:16], g_two[:, 16:32], ALU.add))
            by_half = g_two[:, 32:48].rearrange("p (h g) -> p h g", h=2)
            cube = [P, 2, GROUPS, GROUPS]
            other = by_half.unsqueeze(2).broadcast_to(cube)
            own = by_half.unsqueeze(3).broadcast_to(cube)

            def cubed(v):
                return v.rearrange("p (h i k) -> p h i k", h=2, i=GROUPS)

            then(dve.tensor_tensor(cubed(beats), other, own, ALU.is_gt))
            then(dve.tensor_tensor(cubed(ties), other, own, ALU.is_equal))
            then(dve.tensor_tensor(ties, ties, smalls[:, C_TIE:C_TIE + 128], ALU.mult))
            then(dve.tensor_tensor(beats, beats, ties, ALU.add))
            then(dve.tensor_reduce(rank, beats.rearrange("p (g k) -> p g k", k=GROUPS), AX, ALU.add))
            then(dve.tensor_scalar(chosen_g, rank, float(TOP_GROUPS), None, ALU.is_lt))
            then(dve.tensor_tensor(masked.rearrange("p (g n) -> p g n", n=PER),
                                   choice.rearrange("p (g n) -> p g n", n=PER),
                                   chosen_g.unsqueeze(2).broadcast_to([P, 2 * GROUPS, PER]), ALU.mult))
            then(dve.tensor_scalar(masked, masked, 0.0, None, ALU.add))
            for h in range(2):
                m = masked[:, h * E:h * E + E]
                then(dve.max(top8[:, h * TOP:h * TOP + TOP], m))
                then(dve.match_replace(replaced[:, h * E:h * E + E], top8[:, h * TOP:h * TOP + TOP], m, TAKEN))
            then(dve.tensor_tensor(picked, replaced, masked, ALU.not_equal))
            then(dve.tensor_tensor(picked, picked, score, ALU.mult))
            then(dve.tensor_reduce(total, picked.rearrange("p (h n) -> p h n", h=2), AX, ALU.add))
            then(dve.reciprocal(scaled, total))
            for h in range(2):
                then(dve.tensor_scalar(weights[:, h, SHARED:NE], picked[:, h * E:h * E + E], scaled[:, h:h + 1],
                                       ROUTED_SCALE, ALU.mult, ALU.mult))

            def expert_hidden(j, s):
                dve.wait_ge(silu_ready, j * 2 + (s - 1))
                up = 2 * (s % 2) + 1
                dve.wait_ge(bank_full[up], j + ((F01 if s % 2 == 0 else F23)["moe"] + s // 2))
                dve.tensor_tensor(h_row[:, s % 2, :], bank[up][:, :], gate_act[:, s % 2, :], ALU.mult) \
                   .then_inc(h_ready, 1)
                dve.wait_ge(ev_hi, j * 2 + (V_H + s))
                dve.tensor_tensor(h_lo[:, s % 2, :], h_row[:, s % 2, :], h_hi[:, s % 2, :].bitcast(F32),
                                  ALU.subtract).then_inc(ev_lo, 1)

            def expert_add(j, s):
                for h in range(2):
                    b = 4 + 2 * (s % 2) + h
                    first = {4: F4, 5: F5, 6: F6, 7: F7}[b]["moe"]
                    dve.wait_ge(bank_full[b], j + (first + s // 2))
                    dve.wait_ge(res_done, j * 4 + (3 + 2 * s + h))
                    w = weights[:, h, bass.ds(j * 2 + s, 1)]
                    dve.scalar_tensor_tensor(out=res[:, h, :], in0=bank[b][:, :], scalar=w, in1=res[:, h, :],
                                             op0=ALU.mult, op1=ALU.add).then_inc(res_done, 1)

            expert_add(0, 0)
            split_lo(dve, Tile(0, T_E + 3), 2, E_SIZES)
            expert_add(0, 1)
            dve.wait_ge(lo_split[1], T_E + 3)
            with dve.Fori(1, NE // 2 - 1) as j:
                for s in range(2):
                    expert_hidden(j, s)
                    split_lo(dve, Tile(j, T_E + s + 1), 1, E_SIZES)
                    split_lo(dve, Tile(j, T_E + s + 2), 2, E_SIZES)
                    expert_add(j, s)
            expert_hidden(0, NE - 2)
            split_lo(dve, Tile(0, T_E + NE - 1), 1, E_SIZES)
            expert_hidden(0, NE - 1)
            expert_add(0, NE - 2)
            expert_add(0, NE - 1)

        @block.gpsimd
        def _(pool):
            def root(n, at, cols):
                pool.wait_ge(var_ready, n)
                pool.tensor_tensor(rstd[:, at:at + cols], var_eps[:, at:at + cols], power[:, at:at + cols],
                                   ALU.pow).then_inc(rstd_ready, 1)

            pool.memset(power[:, :], -0.5).then_inc(power_set, 1)
            pool.memset(mask_r.bitcast(F32)[:, 0, :], 0.0).then_inc(mask_zeroed, 1)
            pool.wait_ge(power_set, 1)
            for h in range(2):
                root(h + 1, h, 1)
            split_lo(pool, Tile(0, T_WK), 1, X_SIZES, handed_over=True)
            split_lo(pool, Tile(0, T_CT), 1, X_SIZES)
            with pool.Fori(0, NG // 2) as j:
                for s in range(2):
                    split_lo(pool, Tile(j, T_CT + s + 1), 1, X_SIZES)
            split_lo(pool, Tile(0, T_CN), 1, X_SIZES)
            with pool.Fori(0, NG // 2) as j:
                for s in range(2):
                    split_lo(pool, Tile(j, T_CN + s + 1), 1, X_SIZES)
            split_lo(pool, Tile(0, T_QKV), 1, Q_SIZES)
            def rope_sum(j, s):
                if not (isinstance(j, int) and s == 0):
                    pool.wait_ge(bank_full[7], j * 2 + (F7["rope_t"] - 1 + s))
                at = bass.ds(j * 2 * P + s * P, P)
                pool.tensor_tensor(q_rope, q_cos[:, :, at], q_sin[:, :, at], ALU.add).then_inc(rope_ready, 1)

            root(3, 0, 1)
            root(4, 1, 1)
            split_lo(pool, Tile(0, T_ROPE), 0, X_SIZES, handed_over=True)
            root(5, 2, 2)
            split_lo(pool, Tile(0, T_ROPE), 1, X_SIZES)
            root(6, 4, 2)
            split_lo(pool, Tile(0, T_M), 0, M_SIZES)
            pool.wait_ge(rope_part, 9)
            rope_sum(0, 0)
            split_lo(pool, Tile(0, T_M + 1), 0, M_SIZES)
            pool.wait_ge(rope_part, 12)
            rope_sum(0, 1)
            split_lo(pool, Tile(0, T_M), 1, M_SIZES)

            def pair_step(j, s, sizes=M_SIZES):
                split_lo(pool, Tile(j, T_M + s + 2), 0, sizes)
                split_lo(pool, Tile(j, T_M + s + 1), 1, M_SIZES)

            pair_step(0, 0)
            rope_sum(0, 2)
            with pool.Fori(0, (PAIRS - 4) // 2) as j:
                for s in range(1, 3):
                    pair_step(j, s)
                    rope_sum(j, s + 2)
            pair_step(0, PAIRS - 3)
            rope_sum(0, PAIRS - 1)
            pair_step(0, PAIRS - 2, E_SIZES)
            root(7, 0, 1)
            split_lo(pool, Tile(0, T_E + 1), 0, E_SIZES)
            root(8, 1, 1)
            for s in range(2, 4):
                split_lo(pool, Tile(0, T_E + s), 0, E_SIZES)
            split_lo(pool, Tile(0, T_E + 2), 1, E_SIZES, handed_over=True)
            with pool.Fori(1, NE // 2 - 1) as j:
                for s in range(2):
                    split_lo(pool, Tile(j, T_E + s + 2), 0, E_SIZES)


def _rope_tables():
    half = np.arange(0, ROPE, 2, dtype=np.float32) / np.float32(ROPE)
    inv = (np.float32(1.0) / np.power(np.float32(10000.0), half)).astype(np.float32)
    ang = np.arange(T, dtype=np.float32)[:, None] * inv[None, :]
    ang = np.concatenate([ang, ang], axis=-1).astype(np.float32)
    sign = np.where(np.arange(ROPE) < ROPE // 2, np.float32(-1), np.float32(1))
    return np.cos(ang), np.sin(ang) * sign


def _chunked(w):
    return np.ascontiguousarray(w.reshape(NC, P, -1).transpose(1, 0, 2).reshape(P, -1))


def kernel(**inputs):
    import concourse.bacc as _bacc
    from concourse.bass_utils import run_bass_kernel_spmd as _run

    a = {k: np.asarray(v) for k, v in inputs.items()}
    rows = a["x"][0].reshape(2, P, D).transpose(1, 0, 2)

    small = np.zeros((P, C_END), np.float32)
    small[:, C_ID:C_ID + P] = np.eye(P, dtype=np.float32)
    small[:, C_MASK:C_MASK + P] = np.triu(np.full((P, P), MASKED, np.float32), 1)
    cos, sin = _rope_tables()
    for at, table in ((C_COS, cos), (C_SIN, sin)):
        small[:, at:at + 2 * ROPE] = table.reshape(2, P, ROPE).transpose(1, 0, 2).reshape(P, 2 * ROPE)
    small[:, C_RW:C_RW + NC * E] = _chunked(a["L0_ffn_router_w"])
    small[:, C_BIAS:C_BIAS + 64] = np.tile(a["L0_ffn_router_bias"], 2)[None, :]
    small[:, C_GQ:C_GQ + Q_RANK] = a["L0_attn_g_qa"][None, :]
    small[:, C_GKV:C_GKV + KV_RANK] = a["L0_attn_g_kva"][None, :]
    tie = np.tril(np.ones((GROUPS, GROUPS), np.float32), -1)
    small[:, C_TIE:C_END] = np.tile(tie.reshape(-1), 2)[None, :]

    context = a["ctx_2048"][0]
    ctx_t = np.stack([_chunked(context[g * 512:(g + 1) * 512].T) for g in range(NG)])
    ctx_n = np.stack([_chunked(context[g * 512:(g + 1) * 512]) for g in range(NG)])
    w_qkv = _chunked(np.concatenate([a["L0_attn_Wqa"], a["L0_attn_Wkva"]], axis=1))

    wqb = a["L0_attn_Wqb"].reshape(2, QR2, PAIRS, 2, NOPE + ROPE)
    wkvb = a["L0_attn_Wkvb"].reshape(KV_RANK, PAIRS, 2, NOPE + VDIM)
    wout = a["L0_attn_Wo"].reshape(PAIRS, 2, VDIM, D)
    w_mla = np.zeros((PAIRS, P, sum(M_SIZES)), np.float32)
    for i in range(PAIRS):
        for c in range(2):
            w = wqb[c, :, i]
            w_mla[i, 0:QR2, c * 256:c * 256 + 256] = w[:, :, 0:NOPE].reshape(QR2, 256)
        w_mla[i, :, 512:768] = wkvb[:, i, :, 0:NOPE].reshape(P, 256)
        w_mla[i, :, 768:1024] = wkvb[:, i, :, NOPE:].reshape(P, 256)
        w_mla[i, :, 1024:2048] = wout[i].transpose(1, 0, 2).reshape(P, 1024)
    w_rope = np.zeros((P, 2, 2, 512), np.float32)
    w_rope[0:QR2] = wqb[:, :, :, :, NOPE:].reshape(2, QR2, 2, 512).transpose(1, 2, 0, 3)

    def halves(w, axis):
        return np.stack(np.split(w, 2, axis=axis))

    gate = np.concatenate([halves(a["L0_ffn_sw_gate"], 1), a["L0_ffn_w_gate"]])
    up = np.concatenate([halves(a["L0_ffn_sw_up"], 1), a["L0_ffn_w_up"]])
    down = np.concatenate([halves(a["L0_ffn_sw_down"], 0), a["L0_ffn_w_down"]])
    gate, up = (w.reshape(NE, NC, P, I).transpose(0, 2, 1, 3).reshape(NE, P, NC * I) for w in (gate, up))
    down = down.reshape(NE, 2, P, D).transpose(0, 2, 1, 3).reshape(NE, P, 2 * D)
    w_exp = np.concatenate([gate, up[:, :, 0:I], down, up[:, :, I:]], axis=2)

    arrays = {
        "x": rows, "small": small,
        "wq": _chunked(a["L0_xattn_wq"].T), "wk": _chunked(a["L0_xattn_wk"].T),
        "wv": _chunked(a["L0_xattn_wv"].T), "wo": _chunked(a["L0_xattn_wo"].T),
        "ctx_t": ctx_t, "ctx_n": ctx_n, "w_qkv": w_qkv, "w_rope": w_rope.reshape(P, 2048), "w_mla": w_mla, "w_exp": w_exp,
    }
    arrays = {f"{k}_dram": np.ascontiguousarray(v) for k, v in arrays.items()}
    nc = _bacc.Bacc("TRN2", target_bir_lowering=False, num_devices=1)
    args = [nc.dram_tensor(k, v.shape, F32, kind="ExternalInput").ap() for k, v in arrays.items()]
    args.append(nc.dram_tensor("out_dram", (P, 2, D), F32, kind="ExternalOutput").ap())
    perceiver_layer(nc, *args)
    r = _run(nc, [arrays], core_ids=[0])
    return r.results[0]["out_dram"].transpose(1, 0, 2).reshape(1, T, D)
```
